# Optimizing a Trainium2 kernel written in Bass

```python
import numpy as np
import jax
import jax.numpy as jnp

def _softmax(x, axis=-1):
    return jax.nn.softmax(x, axis=axis)

def _gelu(x):
    return jax.nn.gelu(x, approximate=True)

def _silu(x):
    return jax.nn.silu(x)

def _sigmoid(x):
    return jax.nn.sigmoid(x)

def _layernorm(x, axis=-1, eps=1e-05):
    m = jnp.mean(x, axis=axis, keepdims=True)
    v = jnp.var(x, axis=axis, keepdims=True)
    return (x - m) / jnp.sqrt(v + eps)

def _scatter_add(tgt, idx, src, axis=0):
    return tgt.at[idx].add(src)

def _segment_sum(src, seg, n):
    return jax.ops.segment_sum(src, seg, n)
kernel_name = 'mk_decoder_preln_d2_seqx_r8_34298c'

def setup_inputs(seed: int=0):
    np.random.seed(seed)
    _w = jnp.asarray

    def _rec_inputs():
        import jax
        import jax.numpy as jnp
        _rk = jax.random.key(seed)
        x = -0.0003929 + 0.9999 * jax.random.normal(jax.random.fold_in(_rk, 1), (32, 64, 512), jnp.float32)
        _lenS = 64 - jax.random.randint(jax.random.fold_in(_rk, 7), (32,), 0, max(1, 64 // 4) + 1, jnp.int32)
        _lenS2 = 64 - jax.random.randint(jax.random.fold_in(_rk, 8), (32,), 0, max(1, 64 // 4) + 1, jnp.int32)
        _ctx_1024P = jax.random.normal(jax.random.fold_in(_rk, 11), (32, 16, 128), jnp.float32)
        _ctx_1024c = jax.random.dirichlet(jax.random.fold_in(_rk, 511), 0.3 * jnp.ones((16,), jnp.float32), (32, 64))
        _ctx_1024t = jnp.einsum('bsk,bkd->bsd', _ctx_1024c, _ctx_1024P)
        _ctx_1024t = _ctx_1024t * jax.lax.rsqrt(jnp.mean(jnp.square(_ctx_1024t)) + 1e-12) * 0.953939
        ctx_1024 = -1.39393e-06 + 0.999914 * (_ctx_1024t + 0.3 * jax.random.normal(jax.random.fold_in(_rk, 611), (32, 64, 128), jnp.float32))
        _validS = jnp.arange(64)[None, :] < _lenS[:, None]
        _validS2 = jnp.arange(64)[None, :] < _lenS2[:, None]
        _causal = jnp.tril(jnp.ones((64, 64), dtype=bool))
        mask_SxS2_ff0 = jnp.where(jnp.ones((64, 64), dtype=bool), 0.0, -1000000000.0).astype(jnp.float32)
        return (x, ctx_1024, mask_SxS2_ff0)
    x, ctx_1024, mask_SxS2_ff0 = _rec_inputs()

    def _L0_attn_setup():
        import jax, jax.numpy as jnp
        import numpy as np
        D_MODEL = 512
        NUM_HEADS = 32
        HEAD_DIM = D_MODEL // NUM_HEADS
        Q_LAT = 12
        KV_LAT = 4
        B, S = (2, 256)
        key = jax.random.key(seed)
        ks = jax.random.split(key, 6)
        sc = lambda fan_in: 1.0 / np.sqrt(fan_in)
        return {'x': jax.random.normal(ks[0], (B, S, D_MODEL), jnp.float32), 'Wq_d': jax.random.normal(ks[1], (D_MODEL, Q_LAT), jnp.float32) * sc(D_MODEL), 'bq_d': jnp.zeros((Q_LAT,), jnp.float32), 'W_qk': jax.random.normal(ks[2], (Q_LAT, NUM_HEADS * KV_LAT), jnp.float32) * sc(Q_LAT), 'b_qk': jnp.zeros((NUM_HEADS * KV_LAT,), jnp.float32), 'Wkv_d': jax.random.normal(ks[3], (D_MODEL, KV_LAT), jnp.float32) * sc(D_MODEL), 'bkv_d': jnp.zeros((KV_LAT,), jnp.float32), 'Wv_u': jax.random.normal(ks[4], (KV_LAT, NUM_HEADS * HEAD_DIM), jnp.float32) * sc(KV_LAT), 'bv_u': jnp.zeros((NUM_HEADS * HEAD_DIM,), jnp.float32), 'Wo': jax.random.normal(ks[5], (NUM_HEADS * HEAD_DIM, D_MODEL), jnp.float32) * sc(NUM_HEADS * HEAD_DIM), 'bo': jnp.zeros((D_MODEL,), jnp.float32)}
    _L0_attn_all = _L0_attn_setup()
    _L0_attn_in = {k: v for k, v in _L0_attn_all.items() if k in ('Wq_d', 'bq_d', 'W_qk', 'b_qk', 'Wkv_d', 'bkv_d', 'Wv_u', 'bv_u', 'Wo', 'bo')}
    del _L0_attn_all

    def _L0_xattn_setup():
        import math
        import jax, jax.numpy as jnp
        import numpy as np
        N_HEADS = 32
        N_KV_HEADS = 8
        N_REP = N_HEADS // N_KV_HEADS
        HEAD_DIM = 512 // N_HEADS
        key = jax.random.key(seed)
        kq, kk, kv = jax.random.split(key, 3)
        B, S, T = (2, 256, 256)
        q = jax.random.normal(kq, (B, S, N_HEADS * HEAD_DIM), dtype=jnp.float32)
        k = jax.random.normal(kk, (B, T, N_KV_HEADS * HEAD_DIM), dtype=jnp.float32)
        v = jax.random.normal(kv, (B, T, N_KV_HEADS * HEAD_DIM), dtype=jnp.float32)
        mask = jnp.zeros((S, T), dtype=jnp.float32)
        return {'q': q, 'k': k, 'v': v, 'start_pos': 0, 'mask': mask}
    _L0_xattn_all = _L0_xattn_setup()
    _L0_xattn_in = {k: v for k, v in _L0_xattn_all.items() if k in ()}
    del _L0_xattn_all

    def _L0_ffn_setup():
        import jax, jax.numpy as jnp
        import numpy as np
        NUM_EXPERTS = 4
        HIDDEN = 512
        RANK = 8
        ALPHA = 8.0
        SCALE = ALPHA / RANK
        key = jax.random.key(seed)
        ks = jax.random.split(key, 6)
        B, T, H, E, R = (4, 512, HIDDEN, NUM_EXPERTS, RANK)
        x = jax.random.normal(ks[0], (B, T, H), dtype=jnp.float32)
        W_up = jax.random.normal(ks[1], (H, H), dtype=jnp.float32) / np.sqrt(H)
        gate_w = jax.random.normal(ks[2], (E, H), dtype=jnp.float32) / np.sqrt(H)
        expert_bias = jnp.zeros((E,), dtype=jnp.float32)
        lora_A = jax.random.normal(ks[3], (E, R, H), dtype=jnp.float32) / np.sqrt(H)
        lora_B = jax.random.normal(ks[4], (E, H, R), dtype=jnp.float32) * 0.01
        return {'x': x, 'W_up': W_up, 'gate_w': gate_w, 'expert_bias': expert_bias, 'lora_A': lora_A, 'lora_B': lora_B}
    _L0_ffn_all = _L0_ffn_setup()
    _L0_ffn_in = {k: v for k, v in _L0_ffn_all.items() if k in ('W_up', 'gate_w', 'expert_bias', 'lora_A', 'lora_B')}
    del _L0_ffn_all

    def _L1_attn_setup():
        import jax, jax.numpy as jnp
        import numpy as np
        B, T, H, S, F, G = (2, 256, 512, 128, 1248, 6)
        GRAD_ORDER_MIN = 4
        THD = 2.5
        key = jax.random.key(seed)
        ks = jax.random.split(key, 9)
        sc = 0.02
        hidden_states = jax.random.normal(ks[0], (B, T, H), jnp.float32)
        up_w = jax.random.normal(ks[1], (S, H), jnp.float32) * sc
        gate_w = jax.random.normal(ks[2], (S, H), jnp.float32) / np.sqrt(H)
        local_point = jax.random.normal(ks[3], (S,), jnp.float32)
        local_approx_output = jax.random.normal(ks[4], (H, S), jnp.float32) * sc
        fuse_weight = jax.random.normal(ks[5], (H, S, G), jnp.float32) * sc
        discount_factor = jnp.asarray(np.cumsum(np.log(np.arange(1, G + 1, dtype=np.float64))), jnp.float32)
        ffn_gate_w = jax.random.normal(ks[6], (F, H), jnp.float32) * sc
        ffn_up_w = jax.random.normal(ks[7], (F, H), jnp.float32) * sc
        ffn_down_w = jax.random.normal(ks[8], (H, F), jnp.float32) * sc
        return {'hidden_states': hidden_states, 'up_w': up_w, 'gate_w': gate_w, 'local_point': local_point, 'local_approx_output': local_approx_output, 'fuse_weight': fuse_weight, 'discount_factor': discount_factor, 'ffn_gate_w': ffn_gate_w, 'ffn_up_w': ffn_up_w, 'ffn_down_w': ffn_down_w}
    _L1_attn_all = _L1_attn_setup()
    _L1_attn_in = {k: v for k, v in _L1_attn_all.items() if k in ('up_w', 'gate_w', 'local_point', 'local_approx_output', 'fuse_weight', 'discount_factor', 'ffn_gate_w', 'ffn_up_w', 'ffn_down_w')}
    del _L1_attn_all

    def _L1_xattn_setup():
        import jax, jax.numpy as jnp
        import numpy as np
        import math
        DIM_V = 64
        key = jax.random.key(seed)
        k1, k2, k3, k4, k5, k6 = jax.random.split(key, 6)
        B, C, N, M = (8, DIM_V, 512, 128)
        pcd_up = jax.random.normal(k1, (B, C, N), dtype=jnp.float32)
        pcd_down = jax.random.normal(k2, (B, C, M), dtype=jnp.float32)
        s = 1.0 / math.sqrt(C)
        Wq = jax.random.normal(k3, (C, C), dtype=jnp.float32) * s
        Wk = jax.random.normal(k4, (C, C), dtype=jnp.float32) * s
        Wv = jax.random.normal(k5, (C, C), dtype=jnp.float32) * s
        Wskip = jax.random.normal(k6, (C, C), dtype=jnp.float32) * s
        return {'pcd_up': pcd_up, 'pcd_down': pcd_down, 'Wq': Wq, 'Wk': Wk, 'Wv': Wv, 'Wskip': Wskip}
    _L1_xattn_all = _L1_xattn_setup()
    _L1_xattn_in = {k: v for k, v in _L1_xattn_all.items() if k in ('Wq', 'Wk', 'Wv', 'Wskip')}
    del _L1_xattn_all

    def _L1_ffn_setup():
        import jax, jax.numpy as jnp
        import numpy as np
        HID, INT, LAT, NE, K = (512, 1024, 256, 8, 2)
        LN_EPS = 1e-05

        def _layernorm(x, gamma, beta):
            mu = jnp.mean(x, axis=-1, keepdims=True)
            var = jnp.var(x, axis=-1, keepdims=True)
            return (x - mu) * jax.lax.rsqrt(var + LN_EPS) * gamma + beta
        key = jax.random.key(seed)
        ks = jax.random.split(key, 8)
        s = lambda d: 1.0 / np.sqrt(d)
        return {'hidden_states': jax.random.normal(ks[0], (4, 256, HID), jnp.float32), 'gate_w': jax.random.normal(ks[1], (HID, NE), jnp.float32) * s(HID), 'up_w': jax.random.normal(ks[2], (HID, INT), jnp.float32) * s(HID), 'down_w': jax.random.normal(ks[3], (INT, HID), jnp.float32) * s(INT), 'fc1_w': jax.random.normal(ks[4], (HID, LAT), jnp.float32) * s(HID), 'fc2_w': jax.random.normal(ks[5], (LAT, HID), jnp.float32) * s(LAT), 'expert_w': jax.random.normal(ks[6], (LAT, LAT), jnp.float32), 'ln_gamma': jnp.ones((HID,), jnp.float32), 'ln_beta': jnp.zeros((HID,), jnp.float32)}
    _L1_ffn_all = _L1_ffn_setup()
    _L1_ffn_in = {k: v for k, v in _L1_ffn_all.items() if k in ('gate_w', 'up_w', 'down_w', 'fc1_w', 'fc2_w', 'expert_w', 'ln_gamma', 'ln_beta')}
    del _L1_ffn_all
    return {'x': x, 'ctx_1024': ctx_1024, 'mask_SxS2_ff0': mask_SxS2_ff0, 'L0_attn_Wq_d': _L0_attn_in['Wq_d'], 'L0_attn_bq_d': _L0_attn_in['bq_d'], 'L0_attn_W_qk': _L0_attn_in['W_qk'], 'L0_attn_b_qk': _L0_attn_in['b_qk'], 'L0_attn_Wkv_d': _L0_attn_in['Wkv_d'], 'L0_attn_bkv_d': _L0_attn_in['bkv_d'], 'L0_attn_Wv_u': _L0_attn_in['Wv_u'], 'L0_attn_bv_u': _L0_attn_in['bv_u'], 'L0_attn_Wo': _L0_attn_in['Wo'], 'L0_attn_bo': _L0_attn_in['bo'], 'L0_ffn_W_up': _L0_ffn_in['W_up'], 'L0_ffn_gate_w': _L0_ffn_in['gate_w'], 'L0_ffn_expert_bias': _L0_ffn_in['expert_bias'], 'L0_ffn_lora_A': _L0_ffn_in['lora_A'], 'L0_ffn_lora_B': _L0_ffn_in['lora_B'], 'L1_attn_up_w': _L1_attn_in['up_w'], 'L1_attn_gate_w': _L1_attn_in['gate_w'], 'L1_attn_local_point': _L1_attn_in['local_point'], 'L1_attn_local_approx_output': _L1_attn_in['local_approx_output'], 'L1_attn_fuse_weight': _L1_attn_in['fuse_weight'], 'L1_attn_discount_factor': _L1_attn_in['discount_factor'], 'L1_attn_ffn_gate_w': _L1_attn_in['ffn_gate_w'], 'L1_attn_ffn_up_w': _L1_attn_in['ffn_up_w'], 'L1_attn_ffn_down_w': _L1_attn_in['ffn_down_w'], 'L1_xattn_Wq': _L1_xattn_in['Wq'], 'L1_xattn_Wk': _L1_xattn_in['Wk'], 'L1_xattn_Wv': _L1_xattn_in['Wv'], 'L1_xattn_Wskip': _L1_xattn_in['Wskip'], 'L1_ffn_gate_w': _L1_ffn_in['gate_w'], 'L1_ffn_up_w': _L1_ffn_in['up_w'], 'L1_ffn_down_w': _L1_ffn_in['down_w'], 'L1_ffn_fc1_w': _L1_ffn_in['fc1_w'], 'L1_ffn_fc2_w': _L1_ffn_in['fc2_w'], 'L1_ffn_expert_w': _L1_ffn_in['expert_w'], 'L1_ffn_ln_gamma': _L1_ffn_in['ln_gamma'], 'L1_ffn_ln_beta': _L1_ffn_in['ln_beta']}

def reference(x, ctx_1024, mask_SxS2_ff0, L0_attn_Wq_d, L0_attn_bq_d, L0_attn_W_qk, L0_attn_b_qk, L0_attn_Wkv_d, L0_attn_bkv_d, L0_attn_Wv_u, L0_attn_bv_u, L0_attn_Wo, L0_attn_bo, L0_ffn_W_up, L0_ffn_gate_w, L0_ffn_expert_bias, L0_ffn_lora_A, L0_ffn_lora_B, L1_attn_up_w, L1_attn_gate_w, L1_attn_local_point, L1_attn_local_approx_output, L1_attn_fuse_weight, L1_attn_discount_factor, L1_attn_ffn_gate_w, L1_attn_ffn_up_w, L1_attn_ffn_down_w, L1_xattn_Wq, L1_xattn_Wk, L1_xattn_Wv, L1_xattn_Wskip, L1_ffn_gate_w, L1_ffn_up_w, L1_ffn_down_w, L1_ffn_fc1_w, L1_ffn_fc2_w, L1_ffn_expert_w, L1_ffn_ln_gamma, L1_ffn_ln_beta):
    import jax
    import jax.numpy as jnp

    def _L0_attn_ref(x, Wq_d, bq_d, W_qk, b_qk, Wkv_d, bkv_d, Wv_u, bv_u, Wo, bo):
        import jax, jax.numpy as jnp
        import numpy as np
        D_MODEL = 512
        NUM_HEADS = 32
        HEAD_DIM = D_MODEL // NUM_HEADS
        Q_LAT = 12
        KV_LAT = 4
        B, S = (2, 256)
        b, s, _ = x.shape
        C_q = x @ Wq_d + bq_d
        C_kv = x @ Wkv_d + bkv_d
        q = (C_q @ W_qk + b_qk).reshape(b, s, NUM_HEADS, KV_LAT)
        scores = jnp.einsum('bqhd,bkd->bhqk', q, C_kv) / jnp.sqrt(jnp.asarray(KV_LAT, x.dtype))
        attn = jax.nn.softmax(scores, axis=-1)
        V = (C_kv @ Wv_u + bv_u).reshape(b, s, NUM_HEADS, HEAD_DIM)
        out = jnp.einsum('bhqk,bkhd->bqhd', attn, V).reshape(b, s, NUM_HEADS * HEAD_DIM)
        return out @ Wo + bo

    def _L0_xattn_ref(q, k, v, start_pos, mask):
        import math
        import jax, jax.numpy as jnp
        import numpy as np
        N_HEADS = 32
        N_KV_HEADS = 8
        N_REP = N_HEADS // N_KV_HEADS
        HEAD_DIM = 512 // N_HEADS
        b, s, _ = q.shape
        t = k.shape[1]
        xq = q.reshape(b, s, N_KV_HEADS, N_REP, HEAD_DIM)
        xk = k.reshape(b, t, N_KV_HEADS, HEAD_DIM)
        xv = v.reshape(b, t, N_KV_HEADS, HEAD_DIM)
        scores = jnp.einsum('bsgrd,btgd->bgrst', xq, xk) / math.sqrt(HEAD_DIM)
        scores = scores + mask
        probs = jax.nn.softmax(scores.astype(jnp.float32), axis=-1).astype(q.dtype)
        out = jnp.einsum('bgrst,btgd->bsgrd', probs, xv)
        return out.reshape(b, s, N_HEADS * HEAD_DIM)

    def _L0_ffn_ref(x, W_up, gate_w, expert_bias, lora_A, lora_B):
        import jax, jax.numpy as jnp
        import numpy as np
        NUM_EXPERTS = 4
        HIDDEN = 512
        RANK = 8
        ALPHA = 8.0
        SCALE = ALPHA / RANK
        B, T, H = x.shape
        E = gate_w.shape[0]
        x_flat = x.reshape(-1, H)
        logits = x_flat @ gate_w.T + expert_bias
        top1 = jnp.argmax(logits, axis=-1)
        one_hot = jax.nn.one_hot(top1, E, dtype=x_flat.dtype)
        base_out = jnp.einsum('bth,oh->bto', x, W_up)
        z = jnp.einsum('nh,erh->ner', x_flat, lora_A)
        d = jnp.einsum('ner,ehr->neh', z, lora_B) * SCALE
        delta = jnp.einsum('neh,ne->nh', d, one_hot)
        return base_out + delta.reshape(B, T, H)

    def _L1_attn_ref(hidden_states, up_w, gate_w, local_point, local_approx_output, fuse_weight, discount_factor, ffn_gate_w, ffn_up_w, ffn_down_w):
        import jax, jax.numpy as jnp
        import numpy as np
        B, T, H, S, F, G = (2, 256, 512, 128, 1248, 6)
        GRAD_ORDER_MIN = 4
        THD = 2.5
        approx_up = hidden_states @ up_w.T
        gate_pre = hidden_states @ gate_w.T
        delta = gate_pre - local_point
        neg_factor = jnp.where(delta > 0, 1.0, -1.0).astype(hidden_states.dtype)
        delta_abs = jnp.abs(delta)
        log_delta = jnp.log(delta_abs)
        keep = (delta_abs <= THD).astype(hidden_states.dtype)
        approx_out = approx_up @ local_approx_output.T
        for idx in range(G):
            m = idx + 1
            dterm = jnp.exp(log_delta * m - discount_factor[idx])
            if m % 2 == 1:
                dterm = dterm * neg_factor
            tmp = dterm * approx_up
            if m > GRAD_ORDER_MIN:
                tmp = tmp * keep
            approx_out = approx_out + tmp @ fuse_weight[:, :, idx].T
        ffn_out = jax.nn.silu(hidden_states @ ffn_gate_w.T) * (hidden_states @ ffn_up_w.T) @ ffn_down_w.T
        return approx_out + ffn_out

    def _L1_xattn_ref(pcd_up, pcd_down, Wq, Wk, Wv, Wskip):
        import jax, jax.numpy as jnp
        import numpy as np
        import math
        DIM_V = 64
        q = jnp.einsum('oc,bcn->bon', Wq, pcd_up)
        k = jnp.einsum('oc,bcm->bom', Wk, pcd_down)
        v = jnp.einsum('oc,bcm->bom', Wv, pcd_down)
        C = q.shape[1]
        scale = jnp.sqrt(jnp.asarray(C, dtype=q.dtype))
        energy = jnp.einsum('bcn,bcm->bnm', q, k) / scale
        attention = jax.nn.softmax(energy, axis=-1)
        x = jnp.einsum('bnm,bcm->bcn', attention, v)
        skip = jnp.einsum('oc,bcn->bon', Wskip, pcd_up)
        return skip + x

    def _L1_ffn_ref(hidden_states, gate_w, up_w, down_w, fc1_w, fc2_w, expert_w, ln_gamma, ln_beta):
        import jax, jax.numpy as jnp
        import numpy as np
        HID, INT, LAT, NE, K = (512, 1024, 256, 8, 2)
        LN_EPS = 1e-05

        def _layernorm(x, gamma, beta):
            mu = jnp.mean(x, axis=-1, keepdims=True)
            var = jnp.var(x, axis=-1, keepdims=True)
            return (x - mu) * jax.lax.rsqrt(var + LN_EPS) * gamma + beta
        logits = jnp.einsum('bsh,he->bse', hidden_states, gate_w)
        routing_weights, selected_experts = jax.lax.top_k(logits, K)
        h = jax.nn.relu(jnp.einsum('bsh,hi->bsi', hidden_states, up_w)) ** 2
        shared_out = jnp.einsum('bsi,ih->bsh', h, down_w)
        x_latent = jnp.einsum('bsh,hl->bsl', hidden_states, fc1_w)
        expert_out = jnp.einsum('bsl,lm->bsm', x_latent, expert_w)
        moe_out = expert_out * jnp.sum(routing_weights, axis=-1, keepdims=True)
        routed_out = jnp.einsum('bsl,lh->bsh', moe_out, fc2_w)
        return _layernorm(shared_out + routed_out, ln_gamma, ln_beta)
    x = x + _L0_attn_ref(_layernorm(x, axis=-1), L0_attn_Wq_d, L0_attn_bq_d, L0_attn_W_qk, L0_attn_b_qk, L0_attn_Wkv_d, L0_attn_bkv_d, L0_attn_Wv_u, L0_attn_bv_u, L0_attn_Wo, L0_attn_bo)
    x = x + _L0_xattn_ref(_layernorm(x, axis=-1), ctx_1024, ctx_1024, 0, mask_SxS2_ff0)
    x = x + _L0_ffn_ref(_layernorm(x, axis=-1), L0_ffn_W_up, L0_ffn_gate_w, L0_ffn_expert_bias, L0_ffn_lora_A, L0_ffn_lora_B)
    x = x + _L1_attn_ref(_layernorm(x, axis=-1), L1_attn_up_w, L1_attn_gate_w, L1_attn_local_point, L1_attn_local_approx_output, L1_attn_fuse_weight, L1_attn_discount_factor, L1_attn_ffn_gate_w, L1_attn_ffn_up_w, L1_attn_ffn_down_w)
    x = x + _L1_xattn_ref(_layernorm(x, axis=-1), ctx_1024, L1_xattn_Wq, L1_xattn_Wk, L1_xattn_Wv, L1_xattn_Wskip)
    x = x + _L1_ffn_ref(_layernorm(x, axis=-1), L1_ffn_gate_w, L1_ffn_up_w, L1_ffn_down_w, L1_ffn_fc1_w, L1_ffn_fc2_w, L1_ffn_expert_w, L1_ffn_ln_gamma, L1_ffn_ln_beta)
    return x

_drawn_inputs = setup_inputs


def setup_inputs(seed=0):
    import zlib

    import numpy as np

    out = dict(_drawn_inputs(seed))
    spreads = {'mask_SxS2_ff0': (0.0, 0.612),
     'L0_attn_bq_d': (0.0, 0.1),
     'L0_attn_b_qk': (0.0, 0.1),
     'L0_attn_bkv_d': (0.0, 0.1),
     'L0_attn_bv_u': (0.0, 0.1),
     'L0_attn_bo': (0.0, 0.1),
     'L0_ffn_expert_bias': (0.0, 0.8),
     'L1_ffn_ln_gamma': (1.0, 0.2),
     'L1_ffn_ln_beta': (0.0, 0.1)}
    factors = {'L0_ffn_gate_w': 3.798, 'L0_ffn_lora_A': 2.924, 'L0_ffn_lora_B': 3.24}
    for name, (base, spread) in spreads.items():
        noise = np.random.default_rng([zlib.crc32(name.encode()), seed]).standard_normal(out[name].shape)
        drawn = base * np.exp(spread * noise) if base else spread * noise
        out[name] = jnp.asarray(drawn.astype(out[name].dtype))
    for name, factor in factors.items():
        out[name] = (out[name] * factor).astype(out[name].dtype)
    return out
```

```python
from contextlib import ExitStack

import concourse.bass as bass
from concourse import mybir

F32 = mybir.dt.float32
F16 = mybir.dt.float16
BF16 = mybir.dt.bfloat16
ALU = mybir.AluOpType
ACT = mybir.ActivationFunctionType
AX = mybir.AxisListType

NSEQ, S, D = 32, 64, 512
TOK = NSEQ * S
NT = TOK // 128
KB = D // 128
NC = 4
TC = NT // NC
CH = 128 * TC
EPS = 1e-5
H = 32
DL = 4
QL = 12
DH = D // H
G8 = 8
XS = 2.0 ** 8
WS = 2.0 ** 8
HS = 2.0 ** 2
FS = 2.0 ** 4
AS = 2.0 ** 6
EX4, R8 = 4, 8
CG = EX4 + EX4 * R8
CW = KB * (D + CG)
SD, G6 = 128, 6
FD = 1248
FB = [(i, min(128, FD - i)) for i in range(0, FD, 128)]
UPD = 2 * SD + 2 * FD
DND = G6 + 1 + len(FB)
DW = KB * UPD + DND * D
INT, LAT, NE = 1024, 256, 8
FU, FL = INT // 128, LAT // 128
FC = INT + LAT + NE
FW = KB * FC + FU * D
NP_D, NP_C, NP_F = 16, 4, 8
PD, PC, PF = DW // NP_D, CW // NP_C, FW // NP_F
assert PD * NP_D == DW and PC * NP_C == CW and PF * NP_F == FW


class Held:
    pass


def row(v):
    return v.rearrange("(a n) -> a n", a=1)


def wait_apart(eng, sem, value, marks):
    eng.wait_ge(sem, value)
    eng.sem_inc(marks, 1)


def norm_tile(nc, held, xn, t):
    return nc.vector.tensor_scalar(xn, held.X[:, t, :], held.mv[:, t, 0:1], held.rstd[:, t, 0:1],
                                   ALU.subtract, ALU.mult)


def transpose_tile(nc, held, ps, xn):
    for k in range(KB):
        last = nc.tensor.transpose(ps[:, 128 * k:128 * k + 128], xn[:, 128 * k:128 * k + 128], held.ident[:])
    return last


def mm3(nc, ps, st, mv, start, stop):
    nc.tensor.matmul(ps, st[0], mv[0], start=start, stop=False)
    nc.tensor.matmul(ps, st[0], mv[1], start=False, stop=False)
    return nc.tensor.matmul(ps, st[1], mv[0], start=False, stop=stop)


def rstd_all(nc, pool, held, ready):
    nc.gpsimd.tensor_scalar(held.ve[:], held.mv[:, :, 1], EPS, None, ALU.add).then_inc(ready, 1)
    pool.wait_ge(ready, 1)
    nc.gpsimd.tensor_tensor(held.rstd[:, :, 0], held.ve[:], held.mhalf[:], ALU.pow).then_inc(ready, 1)


def split_piece(nc, pool, raw, hi, lo, loaded, loaded_at, done, done_at, marks):
    wait_apart(pool, loaded, loaded_at, marks)
    nc.gpsimd.tensor_scalar(raw, raw, WS, None, ALU.mult).then_inc(done, 1)
    wait_apart(pool, done, done_at + 1, marks)
    nc.gpsimd.tensor_copy(hi, raw).then_inc(done, 1)
    wait_apart(pool, done, done_at + 2, marks)
    nc.gpsimd.tensor_tensor(lo, raw, hi, ALU.subtract).then_inc(done, 1)


def setup_stage(nc, held, a):
    with ExitStack() as es:
        def sb(name, shape, dt=F32):
            return es.enter_context(nc.sbuf_tensor(name, shape, dt))

        def sem(name):
            return held.sems.enter_context(nc.semaphore(name))

        def pb(name, shape):
            return es.enter_context(nc.psum_tensor(name, shape, F32))

        sel_wv = sb("sel_wv", [128, 4, H])
        sel_a = sb("sel_a", [96, 8, 3])
        sel_b = sb("sel_b", [128, 2, 4])
        sel_o = sb("sel_o", [128, 128, 3])
        wv_t = sb("wv_t", [128, 4, DL])
        wv_bd = sb("wv_bd", [128, 4, H, DL])
        wo = sb("wo", [128, 4, D])
        bv_col = sb("bv_col", [128, 4])
        bv_rep = sb("bv_rep", [128, 4, 128])
        bo = sb("bo", [1, D])
        wkv = sb("wkv", [128, KB, DL + QL])
        mask4 = sb("mask4", [128, S])
        mask_rest = sb("mask_rest", [128, S])
        disc = sb("disc", [128, G6])
        growth = sb("growth_log", [128, G6])
        p_wvo = pb("p_wvo", [128, D])
        p_bvo = pb("p_bvo", [128, D])
        x_in, par_in, pat, cast, wv_ready, growth_ready, growth_exp, fold_ready = (
            sem("su_" + n) for n in ("x_in", "par_in", "pattern", "cast", "wv_ready", "growth_ready",
                                     "growth_exp", "fold_ready"))
        loads = [
            (wv_t[:], a["Wv_uT"].rearrange("(o p) d -> p o d", p=128)),
            (wo[:], a["Wo"].rearrange("(o p) n -> p o n", p=128)),
            (bv_col[:], a["bv_uT"]),
            (bo[:], row(a["bo"])),
            (wkv[:], a["Wkvq"].rearrange("(k p) n -> p k n", p=128)),
            (disc[:], row(a["discount"]).broadcast_to([128, G6])),
            (held.nlp[:], a["local_point"].rearrange("(p a) -> p a", a=1)),
            (held.gam[:], row(a["gamma"]).broadcast_to([128, D])),
            (held.bet[:], row(a["beta"]).broadcast_to([128, D])),
            (held.ebias[:], row(a["expert_bias"]).broadcast_to([128, EX4])),
            (held.lora_b[:], a["lora_B"]),
            (held.kq_bias[0:96, :], a["bkv_rep"].rearrange("(p a) -> p a", a=1)),
            (held.kq_bias[96:96 + QL, :], a["bq_d"].rearrange("(p a) -> p a", a=1)),
        ]
        loads += [(mask4[64 * j:64 * j + 64, :], a["mask"]) for j in range(2)]
        for part in range(3):
            r = slice(32 * part, 32 * part + 32)
            loads += [(held.wqk[96:96 + QL, :, r], a["W_qk"].rearrange("q (g n) -> q g n", g=4)),
                      (held.qk_bias[r, :], a["b_qkT"])]
        on_sp, on_act = loads[0::2], loads[1::2]
        par_all = 16 * len(loads)
        with nc.Block() as block:
            @block.sync
            def _(sp):
                for dst, src in on_sp:
                    sp.dma_start(dst, src).then_inc(par_in, 16)
                for q in range(NC):
                    sp.dma_start(held.X[:, TC * q:TC * q + TC, :],
                                 a["x"][CH * q:CH * q + CH, :].rearrange("(t p) n -> p t n", p=128)).then_inc(x_in, 16)
                sp.wait_ge(par_in, par_all)
                sp.wait_ge(x_in, 16 * NC)

            @block.gpsimd
            def _(pool):
                built = 0

                def put(ins):
                    nonlocal built
                    built += 1
                    ins.then_inc(pat, 1)

                def band(t, base, pattern, width):
                    put(nc.gpsimd.affine_select(out=t, in_=t, compare_op=ALU.is_ge, fill=0.0, base=base,
                                                pattern=pattern, channel_multiplier=1))
                    pool.wait_ge(pat, built)
                    put(nc.gpsimd.affine_select(out=t, in_=t, compare_op=ALU.is_ge, fill=0.0,
                                                base=width - 1 - base, pattern=[[-st, n] for st, n in pattern],
                                                channel_multiplier=-1))
                for t in (held.ident, sel_wv, sel_a, sel_b, sel_o, held.ones):
                    put(nc.gpsimd.memset(t[:], 1.0))
                put(nc.gpsimd.memset(held.mhalf[:], -0.5))
                pool.wait_ge(pat, built)
                band(held.ident[:], 0, [[-1, 128]], 1)
                band(sel_wv[:], 0, [[128, 4], [-DH, H]], DH)
                band(sel_a[:], 0, [[-DL, 8], [-32, 3]], DL)
                band(sel_b[:], 0, [[-DH, 2], [-32, 4]], DH)
                band(sel_o[:], -64, [[-1, 128], [64, 3]], 1)
                assert built == 17

            @block.vector
            def _(v):
                made = 0

                def step(ins):
                    nonlocal made
                    made += 1
                    ins.then_inc(cast, 1)
                v.wait_ge(pat, 17)
                step(nc.vector.tensor_reduce(held.mask_a[:], sel_a[:], AX.X, ALU.add))
                step(nc.vector.tensor_reduce(held.mask_b[:], sel_b[:], AX.X, ALU.add))
                v.wait_ge(cast, made)
                step(nc.vector.tensor_scalar(held.mask_bs[:], held.mask_b[:], AS, None, ALU.mult))
                step(nc.vector.tensor_reduce(held.onehot[:], sel_o[:], AX.X, ALU.max))
                for e in range(EX4):
                    step(nc.vector.memset(held.rank[:, e:e + 1], float(EX4 - e)))
                v.wait_ge(par_in, par_all)
                for o in range(4):
                    nc.vector.tensor_tensor(
                        wv_bd[:, o, :, :], wv_t[:, o:o + 1, :].broadcast_to([128, H, DL]),
                        sel_wv[:, o, :].rearrange("p (h a) -> p h a", a=1).broadcast_to([128, H, DL]),
                        ALU.mult).then_inc(wv_ready, 1)
                    nc.vector.tensor_scalar(bv_rep[:, o, :], held.ones[:], bv_col[:, o:o + 1], None,
                                            ALU.mult).then_inc(wv_ready, 1)
                nc.vector.tensor_copy(growth[:, 0:1], disc[:, 0:1]).then_inc(growth_ready, 1)
                nc.vector.tensor_tensor(growth[:, 1:G6], disc[:, 1:G6], disc[:, 0:G6 - 1],
                                        ALU.subtract).then_inc(growth_ready, 1)
                step(nc.vector.tensor_scalar(held.nlp[:], held.nlp[:], -1.0, None, ALU.mult))
                step(nc.vector.tensor_copy(
                    held.wkq[:, :, 0:96].rearrange("p k (r d) -> p k r d", d=DL),
                    wkv[:, :, 0:DL].rearrange("p k (a d) -> p k a d", a=1).broadcast_to([128, KB, 24, DL])))
                step(nc.vector.tensor_copy(held.wkq[:, :, 96:96 + QL], wkv[:, :, DL:DL + QL]))
                step(nc.vector.tensor_scalar(held.qk_bias_s[:], held.qk_bias[:], AS, None, ALU.mult))
                step(nc.vector.tensor_scalar(mask4[:], mask4[:], DH ** 0.5 * XS * AS, None, ALU.mult))
                v.wait_ge(cast, made)
                step(nc.vector.tensor_copy(held.mk01[:], mask4[:]))
                v.wait_ge(cast, made)
                step(nc.vector.tensor_tensor(mask_rest[:], mask4[:], held.mk01[:], ALU.subtract))
                v.wait_ge(cast, made)
                step(nc.vector.tensor_copy(held.mk01[64:128, :], mask_rest[64:128, :]))
                step(nc.vector.tensor_copy(held.mk2[:], mask_rest[0:64, :]))
                v.wait_ge(cast, made)
                step(nc.vector.tensor_tensor(held.mk2[:], mask_rest[0:64, :], held.mk2[:], ALU.subtract))
                for t in range(NT):
                    v.wait_ge(x_in, 16 * NC)
                    step(nc.vector.bn_stats(held.st[:, t % TC, :], held.X[:, t, :]))
                    v.wait_ge(cast, made)
                    step(nc.vector.bn_aggr(held.mv[:, t, :], held.st[:, t % TC, :]))
                v.wait_ge(fold_ready, 1)
                step(nc.vector.tensor_copy(held.wvo[:], p_wvo[:]))
                v.wait_ge(fold_ready, 2)
                step(nc.vector.tensor_copy(held.bvo[:], p_bvo[0:1, :]))
                v.wait_ge(cast, made)

            @block.tensor
            def _(pe):
                pe.wait_ge(par_in, par_all)
                pe.wait_ge(wv_ready, 8)
                for o in range(4):
                    last = nc.tensor.matmul(p_wvo[:], wv_bd[:, o, :, :].rearrange("p h d -> p (h d)"), wo[:, o, :],
                                            start=o == 0, stop=o == 3)
                last.then_inc(fold_ready, 1)
                for o in range(4):
                    nc.tensor.matmul(p_bvo[:], bv_rep[:, o, :], wo[:, o, :], start=o == 0, stop=False)
                pe.wait_ge(pat, 17)
                nc.tensor.matmul(p_bvo[:], held.ones[0:1, :], bo[:], start=False, stop=True).then_inc(fold_ready, 1)

            @block.scalar
            def _(act):
                for dst, src in on_act:
                    act.dma_start(dst, src).then_inc(par_in, 16)
                act.wait_ge(growth_ready, 2)
                nc.scalar.activation(held.growth[:], growth[:], ACT.Exp, scale=-1.0).then_inc(growth_exp, 1)
                act.wait_ge(growth_exp, 1)


def high(act, nc, c, i, t_ready, hi_ready, xt, ps):
    act.wait_ge(t_ready, TC * c + i + 3)
    nc.scalar.activation(xt[0][:, :, 128 * i:128 * i + 128], ps[:, i, :].rearrange("p (k n) -> p k n", k=KB),
                         ACT.Copy, scale=XS).then_inc(hi_ready, 1)


def low(v, nc, c, i, hi_ready, xt_ready, xt, ps):
    tile = slice(128 * i, 128 * i + 128)
    v.wait_ge(hi_ready, TC * c + i + 1)
    nc.vector.scalar_tensor_tensor(xt[1][:, :, tile], ps[:, i, :].rearrange("p (k n) -> p k n", k=KB), XS,
                                   xt[0][:, :, tile], ALU.mult, ALU.subtract).then_inc(xt_ready, 1)


def silu(act, nc, c, j, n, up_ready, sg_ready, sg, p_up, val_ready):
    act.wait_ge(up_ready, (1 + len(FB)) * c + j + 1)
    if j > 2:
        act.wait_ge(val_ready, (DND - 1) * c + G6 + j - 1)
    nc.scalar.activation(sg[0:n, (j + G6) % 2, :], p_up[0:n, 2 * (j % 2), :], ACT.Silu,
                         scale=1.0 / (XS * WS)).then_inc(sg_ready, 1)


def update_tile(v, nc, held, c, i, ready, x_sum, scale, read, marks):
    t = TC * c + i
    v.wait_ge(ready, t + 1)
    nc.vector.scalar_tensor_tensor(held.X[:, t, :], x_sum, 1.0 / scale, held.X[:, t, :],
                                   ALU.mult, ALU.add).then_inc(read, 1)
    stats_tile(v, nc, held, c, i, read, t + 2, marks)


def stats_tile(v, nc, held, c, i, read, read_at, marks):
    apart, stats = marks
    k = (2 * TC + 1) * c + 2 * i
    wait_apart(v, read, read_at, apart)
    nc.vector.bn_stats(held.st[:, i, :], held.X[:, TC * c + i, :]).then_inc(stats, 1)
    wait_apart(v, stats, k + 1, apart)
    nc.vector.bn_aggr(held.mvc[:, i, :], held.st[:, i, :]).then_inc(stats, 1)
    if i == TC - 1:
        v.wait_ge(stats, k + 2)
        nc.vector.tensor_scalar(held.mv[:, bass.ds(TC * c, TC), :], held.mvc[:], 1.0, None, ALU.mult).then_inc(stats, 1)


def load_weights(nc, held, name, dram, hi, lo, pieces, width):
    with ExitStack() as es:
        raw = es.enter_context(nc.sbuf_tensor(name + "_raw", [128, 2, width], F32))
        loaded = [held.sems.enter_context(nc.semaphore(f"{name}_loaded_{j}")) for j in range(2)]
        split = held.sems.enter_context(nc.semaphore(name + "_split"))
        with nc.Block() as block:
            @block.sync
            def _(sp):
                with sp.Fori(0, pieces // 2) as q:
                    for j in range(2):
                        sp.wait_ge(split, 6 * q + 3 * j + 3)
                        sp.dma_start(raw[:, j, :], dram[:, bass.ds((2 * q + j) * width, width)]).then_inc(loaded[j], 16)

            @block.gpsimd
            def _(pool):
                pool.sem_inc(split, 6)
                with pool.Fori(0, pieces // 2) as q:
                    for j in range(2):
                        part = bass.ds((2 * q + j) * width, width)
                        split_piece(nc, pool, raw[:, j, :], hi[:, part], lo[:, part], loaded[j],
                                    16 * q + 16, split, 6 * q + 3 * j + 6, held.apart)
                pool.wait_ge(split, 3 * pieces + 6)


NU = 2 * TC
UH = H // 2


def soft_unit(nc, v, sems, bufs, u, slot):
    s_ready, top_ready, t_ready, sub_ready = sems
    p_s, top, prob = bufs
    scores = p_s[:, 2 * slot:2 * slot + 2, :].rearrange("p b (h k) -> p (b h) k", k=S)
    v.wait_ge(s_ready, u + 1)
    nc.vector.tensor_reduce(top[:, slot, :], scores, AX.X, ALU.max).then_inc(top_ready, 1)
    v.wait_ge(top_ready, u + 1)
    v.wait_ge(t_ready, u + 1)
    nc.vector.tensor_tensor(prob[:, slot, :, :], scores,
                            top[:, slot, :].rearrange("p (h a) -> p h a", a=1).broadcast_to([128, UH, S]),
                            ALU.subtract).then_inc(sub_ready, 1)


def exp_unit(nc, act, sub_ready, exp_ready, prob, u, slot, scale):
    act.wait_ge(sub_ready, u + 3)
    nc.scalar.activation(prob[:, slot, :, :], prob[:, slot, :, :], ACT.Exp, scale=scale).then_inc(exp_ready, 1)


def transpose_unit(nc, pe, held, sems, p_t, prob, u, slot):
    exp_ready, pt0_ready, pt1_ready, t_ready = sems
    pe.wait_ge(exp_ready, u + 1)
    pe.wait_ge(pt0_ready, u + 1)
    pe.wait_ge(pt1_ready, u + 1)
    for j in range(UH // 2):
        last = nc.tensor.transpose(p_t[:, j // 4, 128 * (j % 4):128 * (j % 4) + 128],
                                   prob[:, slot, 2 * j:2 * j + 2, :].rearrange("p h k -> p (h k)"), held.ident[:])
    last.then_inc(t_ready, 1)


def stage_a(nc, held, a):
    with ExitStack() as es:
        def sb(name, shape, dt=F32):
            return es.enter_context(nc.sbuf_tensor("a_" + name, shape, dt))

        def sem(name):
            return held.sems.enter_context(nc.semaphore("a_" + name))

        def pb(name, shape):
            return es.enter_context(nc.psum_tensor("a_" + name, shape, F32))

        PR = 96
        PREP = 21
        VC = 2 * (DL + 1)
        xn = sb("xn", [128, 2, D])
        xt = sb("xt", [128, KB, CH])
        kf = sb("kf", [128, CH])
        keys = sb("keys", [PR, CH], F16)
        bd = sb("bd", [PR, 8, CH], F16)
        qf = sb("qf", [PR, CH])
        qs = sb("qs", [PR, 4, CH], F16)
        vb = sb("vb", [128, 2 * TC, 2, DL + 1])
        top = sb("top", [128, 2, UH])
        prob = sb("prob", [128, 2, UH, S])
        pt = sb("pt", [128, 2, UH // 2, 128])
        rec = sb("rec", [128, 2, UH])
        z = sb("z", [128, TC, H, DL])
        zt = sb("zt", [128, CH])
        p_s = pb("p_s", [128, 4, D])
        p_t = pb("p_t", [128, 2, D])
        p_v = pb("p_v", [128, 2, D])
        p_x = p_v[:, 1, :]
        rs_ready, vb_clear, xn_ready, tr_ready, xt_ready, lat_ready, cq_ready, prep, vt_ready, q_ready, q_high, \
            s_ready, top_ready, sub_ready, exp_ready, t_ready, pt0_ready, pt1_ready, v_ready, rec_ready, z_part, \
            z_ready, zt_ready, zt_sb, o_ready, x_read, stats = (sem(n) for n in (
                "rs_ready", "vb_clear", "xn_ready", "tr_ready", "xt_ready", "lat_ready", "cq_ready", "prep",
                "vt_ready", "q_ready", "q_high", "s_ready", "top_ready", "sub_ready", "exp_ready", "t_ready",
                "pt0_ready", "pt1_ready", "v_ready", "rec_ready", "z_part", "z_ready", "zt_ready", "zt_sb",
                "o_ready", "x_read", "stats"))
        VU = UH // 2 * 2 * VC

        with nc.Block() as block:
            @block.gpsimd
            def _(pool):
                nc.gpsimd.memset(vb[:], 0.0).then_inc(vb_clear, 1)
                pool.wait_ge(vb_clear, 1)
                for h in range(2):
                    nc.gpsimd.memset(vb[64 * h:64 * h + 64, :, h, DL:DL + 1], AS).then_inc(vb_clear, 1)
                pool.wait_ge(vb_clear, 3)
                rstd_all(nc, pool, held, rs_ready)

            @block.vector
            def _(v):
                v.wait_ge(rs_ready, 2)
                v.wait_ge(vb_clear, 3)
                v.sem_inc(sub_ready, 2)
                v.sem_inc(pt1_ready, 1)
                v.sem_inc(z_ready, 2)
                v.sem_inc(x_read, 1)
                with v.Fori(0, NC) as c:
                    for i in range(TC):
                        v.wait_ge(tr_ready, TC * c + i + 1)
                        norm_tile(nc, held, xn[:, i % 2, :], TC * c + i).then_inc(xn_ready, 1)
                    v.wait_ge(lat_ready, c + 1)
                    nc.vector.tensor_scalar(kf[0:PR, :], p_x[0:PR, :], held.kq_bias[0:PR, 0:1], AS,
                                            ALU.add, ALU.mult).then_inc(prep, 1)
                    v.wait_ge(prep, PREP * c + 1)
                    nc.vector.tensor_copy(keys[:], kf[0:PR, :]).then_inc(prep, 1)
                    v.wait_ge(prep, PREP * c + 2)
                    nc.vector.tensor_tensor(keys[32:64, :], kf[32:64, :], keys[32:64, :], ALU.subtract).then_inc(prep, 1)
                    v.wait_ge(prep, PREP * c + 3)
                    for h in range(8):
                        nc.vector.tensor_scalar(bd[:, h, :], keys[:], held.mask_a[:, h:h + 1], None,
                                                ALU.mult).then_inc(prep, 1)
                    v.wait_ge(vt_ready, c + 1)
                    for h in range(2):
                        r = slice(64 * h, 64 * h + 64)
                        nc.vector.tensor_copy(vb[r, :, h, 0:DL],
                                              p_v[r, 0, 0:8 * DL].rearrange("p (b d) -> p b d", d=DL)
                                              ).then_inc(prep, 1)
                    for g in range(4):
                        r = slice(64, 96)
                        v.wait_ge(q_high, 4 * c + g + 1)
                        v.wait_ge(prep, PREP * c + 13 + 2 * g)
                        nc.vector.tensor_scalar(qf[r, :], p_s[r, g, :], held.qk_bias[r, g:g + 1], AS,
                                                ALU.add, ALU.mult).then_inc(prep, 1)
                        v.wait_ge(prep, PREP * c + 14 + 2 * g)
                        nc.vector.tensor_tensor(qs[r, g, :], qf[r, :], qs[r, g, :], ALU.subtract).then_inc(prep, 1)

                    def values(j):
                        u = NU * c + j
                        v.wait_ge(t_ready, u + 3)
                        v.wait_ge(v_ready, u + 1)
                        nc.vector.tensor_copy(pt[:, j % 2, 4:8, :].rearrange("p b n -> p (b n)"),
                                              p_t[:, 1, :]).then_inc(pt1_ready, 1)

                    def norm_z(j):
                        u, slot, i = NU * c + j, j % 2, j // 2
                        sums = p_v[:, slot, 0:VU].rearrange("p (b s h n) -> p b s h n", s=2, h=2,
                                                                             n=DL + 1)
                        v.wait_ge(v_ready, u + 3)
                        for s in range(2):
                            r = slice(64 * s, 64 * s + 64)
                            nc.vector.reciprocal(rec[r, slot, :].rearrange("p (b h) -> p b h", h=2),
                                                 sums[r, :, s, :, DL]).then_inc(rec_ready, 1)
                        v.wait_ge(rec_ready, 2 * u + 2)
                        for s in range(2):
                            r = slice(64 * s, 64 * s + 64)
                            last = nc.vector.tensor_tensor(
                                z[r, i, UH * slot:UH * slot + UH, :].rearrange("p (b h) n -> p b h n", h=2),
                                sums[r, :, s, :, 0:DL],
                                rec[r, slot, :].rearrange("p (b h a) -> p b h a", h=2, a=1)
                                .broadcast_to([64, UH // 2, 2, DL]), ALU.mult)
                            last.then_inc(z_ready if s else z_part, 1)
                    for j in range(NU):
                        soft_unit(nc, v, (s_ready, top_ready, t_ready, sub_ready), (p_s, top, prob),
                                  NU * c + j, j % 2)
                        if j >= 1:
                            values(j - 1)
                        if j >= 2:
                            norm_z(j - 2)
                    values(NU - 1)
                    norm_z(NU - 2)
                    norm_z(NU - 1)
                    for i in range(TC):
                        update_tile(v, nc, held, c, i, o_ready, p_s[:, i, :], 1.0, x_read, (held.apart, stats))
                v.wait_ge(stats, NC * (2 * TC + 1))

            @block.scalar
            def _(act):
                act.sem_inc(pt0_ready, 1)
                with act.Fori(0, NC) as c:
                    for i in range(TC):
                        act.wait_ge(tr_ready, TC * c + i + 3)
                        nc.scalar.activation(xt[:, :, 128 * i:128 * i + 128],
                                             p_s[:, i, :].rearrange("p (k n) -> p k n", k=KB),
                                             ACT.Copy).then_inc(xt_ready, 1)
                    act.wait_ge(lat_ready, c + 1)
                    nc.scalar.activation(kf[96:96 + QL, :], p_x[96:96 + QL, :], ACT.Identity,
                                         bias=held.kq_bias[96:96 + QL, 0:1]).then_inc(cq_ready, 1)
                    for g in range(4):
                        act.wait_ge(q_ready, 4 * c + g + 1)
                        nc.scalar.activation(qs[:, g, :], p_s[0:PR, g, :], ACT.Identity,
                                             bias=held.qk_bias_s[:, g:g + 1], scale=AS).then_inc(q_high, 1)

                    def values(j):
                        u = NU * c + j
                        act.wait_ge(t_ready, u + 3)
                        act.wait_ge(v_ready, u + 1)
                        nc.scalar.activation(pt[:, j % 2, 0:4, :].rearrange("p b n -> p (b n)"), p_t[:, 0, :],
                                             ACT.Copy).then_inc(pt0_ready, 1)
                    for j in range(NU):
                        if j:
                            values(j - 1)
                        exp_unit(nc, act, sub_ready, exp_ready, prob, NU * c + j, j % 2, DL ** -0.5 / (AS * AS))
                    values(NU - 1)
                    act.wait_ge(zt_ready, c + 1)
                    nc.scalar.activation(zt[:], p_x, ACT.Copy).then_inc(zt_sb, 1)

            @block.tensor
            def _(pe):
                pe.sem_inc(tr_ready, 2)
                pe.sem_inc(t_ready, 2)
                pe.sem_inc(v_ready, 2)
                with pe.Fori(0, NC) as c:
                    pe.wait_ge(x_read, TC * c + 1)
                    for i in range(TC):
                        pe.wait_ge(xn_ready, TC * c + i + 1)
                        transpose_tile(nc, held, p_s[:, i, :], xn[:, i % 2, :]).then_inc(tr_ready, 1)
                    pe.wait_ge(xt_ready, TC * c + TC)
                    for k in range(KB):
                        last = nc.tensor.matmul(p_x[0:96 + QL, :], held.wkq[:, k, :], xt[:, k, :],
                                                start=k == 0, stop=k == KB - 1)
                    last.then_inc(lat_ready, 1)
                    pe.wait_ge(cq_ready, c + 1)
                    for g in range(4):
                        nc.tensor.matmul(p_s[0:PR, g, :], held.wqk[96:96 + QL, g, :], kf[96:96 + QL, :],
                                         start=True, stop=True).then_inc(q_ready, 1)
                    pe.wait_ge(prep, PREP * c + 1)
                    for b in range(2 * TC):
                        for h in range(2):
                            last = nc.tensor.matmul(p_v[64 * h:64 * h + 64, 0, DL * b:DL * b + DL],
                                                    kf[0:DL, 64 * b:64 * b + 64], held.ident[0:DL, 0:DL],
                                                    start=True, stop=True)
                    last.then_inc(vt_ready, 1)
                    pe.wait_ge(prep, PREP * c + PREP)

                    def scores(j):
                        u, slot, i = NU * c + j, j % 2, j // 2
                        pe.wait_ge(sub_ready, u + 1)
                        for gi in range(2):
                            for s in range(2):
                                seq = slice(128 * i + 64 * s, 128 * i + 64 * s + 64)
                                last = nc.tensor.matmul(p_s[64 * s:64 * s + 64, 2 * slot + gi, :],
                                                        qs[:, 2 * slot + gi, seq], bd[:, :, seq],
                                                        start=True, stop=True)
                        last.then_inc(s_ready, 1)

                    def attend(j):
                        u, slot, i = NU * c + j, j % 2, j // 2
                        pe.wait_ge(pt0_ready, u + 2)
                        pe.wait_ge(pt1_ready, u + 2)
                        pe.wait_ge(z_ready, u + 1)
                        for b in range(UH // 2):
                            last = nc.tensor.matmul(p_v[:, slot, 2 * VC * b:2 * VC * b + 2 * VC], pt[:, slot, b, :],
                                                    vb[:, 2 * i:2 * i + 2, :, :].rearrange("p s h n -> p (s h n)"),
                                                    start=True, stop=True)
                        last.then_inc(v_ready, 1)
                    scores(0)
                    scores(1)
                    for j in range(NU):
                        transpose_unit(nc, pe, held, (exp_ready, pt0_ready, pt1_ready, t_ready), p_t, prob,
                                       NU * c + j, j % 2)
                        if j + 2 < NU:
                            scores(j + 2)
                        attend(j)
                    pe.wait_ge(z_ready, NU * c + NU + 2)
                    for i in range(TC):
                        last = nc.tensor.transpose(p_x[:, 128 * i:128 * i + 128],
                                                   z[:, i, :, :].rearrange("p h d -> p (h d)"), held.ident[:])
                    last.then_inc(zt_ready, 1)
                    pe.wait_ge(zt_sb, c + 1)
                    for i in range(TC):
                        nc.tensor.matmul(p_s[:, i, :], zt[:, 128 * i:128 * i + 128], held.wvo[:], start=True,
                                         stop=False)
                        nc.tensor.matmul(p_s[:, i, :], held.ones[0:1, :], held.bvo[:], start=False,
                                         stop=True).then_inc(o_ready, 1)


def stage_b(nc, held, a):
    with ExitStack() as es:
        def sb(name, shape, dt=F32):
            return es.enter_context(nc.sbuf_tensor("b_" + name, shape, dt))

        def sem(name):
            return held.sems.enter_context(nc.semaphore("b_" + name))

        def pb(name, shape):
            return es.enter_context(nc.psum_tensor("b_" + name, shape, F32))

        VC = 2 * 2 * (DH + 1)
        xn = sb("xn", [128, 2, D])
        xt = [sb("xt_high", [128, KB, CH], F16), sb("xt_low", [128, KB, CH], F16)]
        kt = sb("kt", [128, KB, CH])
        bd = [sb("bd_high", [128, 2, KB, CH], F16), sb("bd_low", [128, 2, KB, CH], F16)]
        cd = sb("cd", [128, 2 * TC, 128])
        vb = sb("vb", [128, 2, G8, 2, 2, DH + 1])
        top = sb("top", [128, 2, UH])
        prob = sb("prob", [128, 2, UH, S])
        pt = sb("pt", [128, 2, UH // 2, 128])
        rec = sb("rec", [128, 2, UH])
        o = sb("o", [128, 2, KB, 4, 2, DH])
        p_s = pb("p_s", [128, 4, D])
        p_t = pb("p_t", [128, 2, D])
        p_v = pb("p_v", [128, 2, D])
        rs_ready, vb_clear, kt_in, cd_in, vb_ready, xn_ready, tr_ready, hi_ready, xt_ready, bd_high, bd_ready, \
            s_ready, top_ready, sub_ready, exp_ready, t_ready, pt0_ready, pt1_ready, v_ready, rec_ready, o_part, \
            z_ready, x_ready, vb_read, stats = (sem(n) for n in (
                "rs_ready", "vb_clear", "kt_in", "cd_in", "vb_ready", "xn_ready", "tr_ready", "hi_ready",
                "xt_ready", "bd_high", "bd_ready", "s_ready", "top_ready", "sub_ready", "exp_ready", "t_ready",
                "pt0_ready", "pt1_ready", "v_ready", "rec_ready", "o_part", "z_ready", "x_ready", "vb_read",
                "stats"))
        ctx_b = a["ctx"].rearrange("(b k) n -> k b n", k=S)

        with nc.Block() as block:
            @block.sync
            def _(sp):
                sp.sem_inc(kt_in, 16)
                with sp.Fori(0, NC) as c:
                    sp.wait_ge(bd_ready, 2 * c + 1)
                    for k in range(KB):
                        for g in range(2):
                            for r in range(4):
                                at = 64 * g + 16 * r
                                sp.dma_start(kt[at:at + DH, k, :],
                                             a["ctx_t"][DH * (2 * k + g):DH * (2 * k + g) + DH, bass.ds(CH * c, CH)]
                                             ).then_inc(kt_in, 16)
                    sp.wait_ge(vb_ready, 2 * TC * c + 1)
                    for h in range(2):
                        sp.dma_start(cd[64 * h:64 * h + 64, :, :],
                                     ctx_b[:, bass.ds(2 * TC * c, 2 * TC), :]).then_inc(cd_in, 16)

            @block.gpsimd
            def _(pool):
                nc.gpsimd.memset(vb[:], 0.0).then_inc(vb_clear, 1)
                pool.wait_ge(vb_clear, 1)
                for h in range(2):
                    for b in range(2):
                        nc.gpsimd.memset(vb[64 * h:64 * h + 64, b, :, :, h, DH:DH + 1], 1.0).then_inc(vb_clear, 1)
                pool.wait_ge(vb_clear, 5)
                rstd_all(nc, pool, held, rs_ready)
                pool.sem_inc(vb_ready, 1)
                with pool.Fori(0, NC) as c:
                    for i in range(TC):
                        if i == 0:
                            wait_apart(pool, cd_in, 32 * c + 32, held.apart)
                        wait_apart(pool, vb_read, TC * c + i + 1, held.apart)
                        for h in range(2):
                            r = slice(64 * h, 64 * h + 64)
                            for s in range(2):
                                last = nc.gpsimd.tensor_copy(
                                    vb[r, i % 2, :, s, h, 0:DH],
                                    cd[r, 2 * i + s, :].rearrange("p (g d) -> p g d", g=G8))
                            last.then_inc(vb_ready, 1)

            @block.vector
            def _(v):
                v.wait_ge(rs_ready, 2)
                v.sem_inc(sub_ready, 2)
                v.sem_inc(pt1_ready, 1)
                v.sem_inc(z_ready, 1)
                v.sem_inc(bd_ready, 1)
                with v.Fori(0, NC) as c:
                    for i in range(TC):
                        v.wait_ge(tr_ready, TC * c + i + 1)
                        norm_tile(nc, held, xn[:, i % 2, :], TC * c + i).then_inc(xn_ready, 1)
                        if i:
                            low(v, nc, c, i - 1, hi_ready, xt_ready, xt, p_s)
                    low(v, nc, c, TC - 1, hi_ready, xt_ready, xt, p_s)
                    for h in range(2):
                        v.wait_ge(bd_high, 2 * c + h + 1)
                        nc.vector.scalar_tensor_tensor(bd[1][:, h, :, :], kt[:], held.mask_bs[:, h:h + 1],
                                                       bd[0][:, h, :, :], ALU.mult, ALU.subtract).then_inc(bd_ready, 1)

                    def values(j):
                        u = NU * c + j
                        v.wait_ge(t_ready, u + 3)
                        v.wait_ge(v_ready, u + 1)
                        nc.vector.tensor_copy(pt[:, j % 2, 4:8, :].rearrange("p b n -> p (b n)"),
                                              p_t[:, 1, :]).then_inc(pt1_ready, 1)

                    def norm_o(j):
                        u, slot, i = NU * c + j, j % 2, j // 2
                        v.wait_ge(v_ready, u + 3)
                        for s in range(2):
                            r = slice(64 * s, 64 * s + 64)
                            for q in range(2):
                                sums = p_v[r, q, 0:KB * VC].rearrange("p (k s h n) -> p k s h n", s=2, h=2, n=DH + 1)
                                nc.vector.reciprocal(rec[r, slot, 8 * q:8 * q + 8].rearrange("p (k h) -> p k h", h=2),
                                                     sums[:, :, s, :, DH]).then_inc(rec_ready, 1)
                        v.wait_ge(rec_ready, 4 * u + 4)
                        for s in range(2):
                            r = slice(64 * s, 64 * s + 64)
                            for q in range(2):
                                sums = p_v[r, q, 0:KB * VC].rearrange("p (k s h n) -> p k s h n", s=2, h=2, n=DH + 1)
                                last = nc.vector.tensor_tensor(
                                    o[r, i % 2, :, 2 * slot + q, :, :], sums[:, :, s, :, 0:DH],
                                    rec[r, slot, 8 * q:8 * q + 8].rearrange("p (k h a) -> p k h a", h=2, a=1)
                                    .broadcast_to([64, KB, 2, DH]), ALU.mult)
                                last.then_inc(z_ready if s and q else o_part, 1)

                    def update(i):
                        t = TC * c + i
                        v.wait_ge(z_ready, 2 * t + 3)
                        nc.vector.tensor_tensor(held.X[:, t, :], held.X[:, t, :],
                                                o[:, i % 2, :, :, :, :].rearrange("p k q h d -> p (k q h d)"),
                                                ALU.add).then_inc(x_ready, 1)
                        stats_tile(v, nc, held, c, i, x_ready, t + 1, (held.apart, stats))
                    for j in range(NU):
                        soft_unit(nc, v, (s_ready, top_ready, t_ready, sub_ready), (p_s, top, prob),
                                  NU * c + j, j % 2)
                        if j >= 1:
                            values(j - 1)
                        if j >= 2:
                            norm_o(j - 2)
                            if j % 2:
                                update((j - 2) // 2)
                    values(NU - 1)
                    norm_o(NU - 2)
                    norm_o(NU - 1)
                    update(TC - 1)
                v.wait_ge(stats, NC * (2 * TC + 1))

            @block.scalar
            def _(act):
                act.sem_inc(pt0_ready, 1)
                with act.Fori(0, NC) as c:
                    for i in range(TC):
                        high(act, nc, c, i, tr_ready, hi_ready, xt, p_s)
                    act.wait_ge(kt_in, 16 * 32 * c + 16 * 33)
                    for h in range(2):
                        nc.scalar.activation(bd[0][:, h, :, :], kt[:], ACT.Copy,
                                             scale=held.mask_bs[:, h:h + 1]).then_inc(bd_high, 1)

                    def values(j):
                        u = NU * c + j
                        act.wait_ge(t_ready, u + 3)
                        act.wait_ge(v_ready, u + 1)
                        nc.scalar.activation(pt[:, j % 2, 0:4, :].rearrange("p b n -> p (b n)"), p_t[:, 0, :],
                                             ACT.Copy).then_inc(pt0_ready, 1)
                    for j in range(NU):
                        if j:
                            values(j - 1)
                        exp_unit(nc, act, sub_ready, exp_ready, prob, NU * c + j, j % 2, DH ** -0.5 / (XS * AS))
                    values(NU - 1)

            @block.tensor
            def _(pe):
                pe.sem_inc(tr_ready, 2)
                pe.sem_inc(t_ready, 2)
                pe.sem_inc(v_ready, 2)
                pe.sem_inc(vb_read, 2)
                with pe.Fori(0, NC) as c:
                    pe.wait_ge(sub_ready, NU * c + 2)
                    for i in range(TC):
                        pe.wait_ge(xn_ready, TC * c + i + 1)
                        transpose_tile(nc, held, p_s[:, i, :], xn[:, i % 2, :]).then_inc(tr_ready, 1)
                    pe.wait_ge(xt_ready, TC * c + TC)
                    pe.wait_ge(bd_ready, 2 * c + 3)

                    def scores(j):
                        u, slot, i = NU * c + j, j % 2, j // 2
                        pe.wait_ge(sub_ready, u + 1)
                        for r in (2 * slot, 2 * slot + 1):
                            nc.tensor.matmul(p_s[:, r, :], held.onehot[:],
                                             held.mk01[:].rearrange("p (a k) -> p a k", a=1).broadcast_to([128, 8, S]),
                                             start=True, stop=False)
                            nc.tensor.matmul(p_s[:, r, :], held.onehot[0:64, :],
                                             held.mk2[:].rearrange("p (a k) -> p a k", a=1).broadcast_to([64, 8, S]),
                                             start=False, stop=False)
                            pair = slice(32 * r, 32 * r + 32)
                            for k in range(KB):
                                for s in range(2):
                                    seq = slice(128 * i + 64 * s, 128 * i + 64 * s + 64)
                                    last = mm3(nc, p_s[64 * s:64 * s + 64, r, 128 * k:128 * k + 128],
                                               [x[pair, k, seq] for x in xt], [x[pair, :, k, seq] for x in bd],
                                               False, k == KB - 1)
                        last.then_inc(s_ready, 1)

                    def attend(j):
                        u, slot, i = NU * c + j, j % 2, j // 2
                        pe.wait_ge(pt0_ready, u + 2)
                        pe.wait_ge(pt1_ready, u + 2)
                        pe.wait_ge(z_ready, u + 1)
                        if slot == 0:
                            pe.wait_ge(vb_ready, 2 * (TC * c + i) + 3)
                        for b in range(UH // 2):
                            q, k = b // KB, b % KB
                            last = nc.tensor.matmul(p_v[:, q, VC * k:VC * k + VC], pt[:, slot, b, :],
                                                    vb[:, i % 2, 2 * k + slot, :, :, :]
                                                    .rearrange("p s h n -> p (s h n)"), start=True, stop=True)
                        last.then_inc(v_ready, 1)
                        if slot == 1:
                            pe.wait_ge(v_ready, u + 3)
                            pe.sem_inc(vb_read, 1)
                    scores(0)
                    scores(1)
                    for j in range(NU):
                        transpose_unit(nc, pe, held, (exp_ready, pt0_ready, pt1_ready, t_ready), p_t, prob,
                                       NU * c + j, j % 2)
                        if j + 2 < NU:
                            scores(j + 2)
                        attend(j)


def stage_c(nc, held, a):
    with ExitStack() as es:
        def sb(name, shape, dt=F32):
            return es.enter_context(nc.sbuf_tensor(name, shape, dt))

        def sem(name):
            return held.sems.enter_context(nc.semaphore("c_" + name))

        def pb(name, shape):
            return es.enter_context(nc.psum_tensor(name, shape, F32))

        xn = sb("c_xn", [128, 2, D])
        xt = [sb("c_xt_high", [128, 2, KB, 128], F16), sb("c_xt_low", [128, 2, KB, 128], F16)]
        logit = sb("c_logit", [128, EX4])
        top = sb("c_top", [128, 2])
        pick = sb("c_pick", [128, EX4])
        zp = sb("c_zp", [128, 2, EX4, R8])
        zt = sb("c_zt", [EX4 * R8, 2, 128])
        p_t = pb("c_p_t", [128, 2, D])
        p_out = pb("c_p_out", [128, 2, D])
        p_aux = pb("c_p_aux", [128, 2, D])
        p_zt = pb("c_p_zt", [128, D])
        rs_ready, xn_ready, t_ready, hi_ready, xt_ready, aux_ready, gated, zp_ready, zt_ready, zt_sb, \
            out_ready, updated, stats = (sem(n) for n in (
                "rs_ready", "xn_ready", "t_ready", "hi_ready", "xt_ready", "aux_ready", "gated", "zp_ready",
                "zt_ready", "zt_sb", "out_ready", "updated", "stats"))
        whl = [w[:, 0:KB * D].rearrange("p (k n) -> p k n", k=KB) for w in (held.wc_hi, held.wc_lo)]
        ghl = [w[:, KB * D:CW].rearrange("p (k n) -> p k n", k=KB) for w in (held.wc_hi, held.wc_lo)]

        with nc.Block() as block:
            @block.gpsimd
            def _(pool):
                rstd_all(nc, pool, held, rs_ready)

            @block.vector
            def _(v):
                v.wait_ge(rs_ready, 2)
                v.sem_inc(xt_ready, 2)
                v.sem_inc(updated, 2)
                v.sem_inc(zp_ready, 2)
                with v.Fori(0, NC) as c:
                    def norm(i):
                        v.wait_ge(t_ready, TC * c + i + 1)
                        norm_tile(nc, held, xn[:, i % 2, :], TC * c + i).then_inc(xn_ready, 1)

                    def low(i):
                        v.wait_ge(hi_ready, TC * c + i + 1)
                        nc.vector.scalar_tensor_tensor(
                            xt[1][:, i % 2, :, :].rearrange("p k n -> p (k n)"), p_t[:, i % 2, :], XS,
                            xt[0][:, i % 2, :, :].rearrange("p k n -> p (k n)"),
                            ALU.mult, ALU.subtract).then_inc(xt_ready, 1)

                    def gate(i):
                        k = 7 * (TC * c + i)
                        v.wait_ge(aux_ready, TC * c + i + 1)
                        nc.vector.scalar_tensor_tensor(logit[:], p_aux[:, i % 2, 0:EX4], 1.0 / (XS * WS),
                                                       held.ebias[:], ALU.mult, ALU.add).then_inc(gated, 1)
                        v.wait_ge(gated, k + 1)
                        nc.vector.tensor_reduce(top[:, 0:1], logit[:], AX.X, ALU.max).then_inc(gated, 1)
                        v.wait_ge(gated, k + 2)
                        nc.vector.tensor_scalar(pick[:], logit[:], top[:, 0:1], None,
                                                ALU.is_equal).then_inc(gated, 1)
                        v.wait_ge(gated, k + 3)
                        nc.vector.tensor_tensor(pick[:], pick[:], held.rank[:], ALU.mult).then_inc(gated, 1)
                        v.wait_ge(gated, k + 4)
                        nc.vector.tensor_reduce(top[:, 1:2], pick[:], AX.X, ALU.max).then_inc(gated, 1)
                        v.wait_ge(gated, k + 5)
                        nc.vector.tensor_scalar(pick[:], pick[:], top[:, 1:2], None,
                                                ALU.is_equal).then_inc(gated, 1)
                        v.wait_ge(gated, k + 6)
                        nc.vector.tensor_copy(zp[:, i % 2, :, :],
                                              p_aux[:, i % 2, EX4:CG].rearrange("p (e r) -> p e r", e=EX4)
                                              ).then_inc(gated, 1)
                        v.wait_ge(gated, k + 7)
                        nc.vector.tensor_tensor(
                            zp[:, i % 2, :, :], zp[:, i % 2, :, :],
                            pick[:].rearrange("p (e b) -> p e b", b=1).broadcast_to([128, EX4, R8]),
                            ALU.mult).then_inc(zp_ready, 1)

                    def update(i):
                        t = TC * c + i
                        v.wait_ge(out_ready, t + 1)
                        nc.vector.scalar_tensor_tensor(held.X[:, t, :], p_out[:, i % 2, :], 1.0 / (XS * WS),
                                                       held.X[:, t, :], ALU.mult, ALU.add).then_inc(updated, 1)
                        stats_tile(v, nc, held, c, i, updated, t + 3, (held.apart, stats))
                    norm(0)
                    for i in range(TC):
                        if i + 1 < TC:
                            norm(i + 1)
                        low(i)
                        gate(i)
                        if i:
                            update(i - 1)
                    update(TC - 1)
                v.wait_ge(stats, NC * (2 * TC + 1))

            @block.scalar
            def _(act):
                with act.Fori(0, NC) as c:
                    def high(i):
                        act.wait_ge(t_ready, TC * c + i + 3)
                        nc.scalar.activation(xt[0][:, i % 2, :, :].rearrange("p k n -> p (k n)"), p_t[:, i % 2, :],
                                             ACT.Copy, scale=XS).then_inc(hi_ready, 1)

                    def zcopy(i):
                        act.wait_ge(zt_ready, TC * c + i + 1)
                        nc.scalar.activation(zt[:, i % 2, :], p_zt[0:EX4 * R8, 0:128], ACT.Copy).then_inc(zt_sb, 1)
                    for i in range(TC):
                        act.wait_ge(updated, TC * c + i + 1)
                        high(i)
                        if i:
                            zcopy(i - 1)
                    zcopy(TC - 1)

            @block.tensor
            def _(pe):
                pe.sem_inc(t_ready, 2)
                with pe.Fori(0, NC) as c:
                    def trans(i):
                        pe.wait_ge(xn_ready, TC * c + i + 1)
                        pe.wait_ge(xt_ready, TC * c + i + 1)
                        transpose_tile(nc, held, p_t[:, i % 2, :], xn[:, i % 2, :]).then_inc(t_ready, 1)

                    def products(i):
                        st = [x[:, i % 2, :, :] for x in xt]
                        pe.wait_ge(xt_ready, TC * c + i + 3)
                        pe.wait_ge(zp_ready, TC * c + i + 1)
                        for k in range(KB):
                            last = mm3(nc, p_aux[:, i % 2, 0:CG], [x[:, k, :] for x in st],
                                       [w[:, k, :] for w in ghl], k == 0, k == KB - 1)
                        last.then_inc(aux_ready, 1)
                        pe.wait_ge(updated, TC * c + i + 1)
                        for k in range(KB):
                            mm3(nc, p_out[:, i % 2, :], [x[:, k, :] for x in st],
                                [w[:, k, :] for w in whl], k == 0, False)

                    def delta(i):
                        pe.wait_ge(zp_ready, TC * c + i + 3)
                        nc.tensor.transpose(p_zt[0:EX4 * R8, 0:128],
                                            zp[:, i % 2, :, :].rearrange("p e r -> p (e r)"),
                                            held.ident[:]).then_inc(zt_ready, 1)
                        pe.wait_ge(zt_sb, TC * c + i + 1)
                        nc.tensor.matmul(p_out[:, i % 2, :], zt[:, i % 2, :], held.lora_b[:], start=False,
                                         stop=True).then_inc(out_ready, 1)
                    trans(0)
                    for i in range(TC):
                        if i + 1 < TC:
                            trans(i + 1)
                        products(i)
                        if i:
                            delta(i - 1)
                    delta(TC - 1)


def stage_d(nc, held, a):
    with ExitStack() as es:
        def sb(name, shape, dt=F32):
            return es.enter_context(nc.sbuf_tensor(name, shape, dt))

        def sem(name):
            return held.sems.enter_context(nc.semaphore("d_" + name))

        NH = 3
        NF = len(FB)
        xn = sb("d_xn", [128, 2, D])
        xt = [sb("d_xt_high", [128, KB, CH], F16), sb("d_xt_low", [128, KB, CH], F16)]
        hid = [sb("d_h_high", [128, NH, CH], F16), sb("d_h_low", [128, NH, CH], F16)]
        term = sb("d_term", [128, 2, CH])
        kept = sb("d_kept", [128, CH])
        delta = sb("d_delta", [128, CH])
        keep = sb("d_keep", [128, CH])
        sg = sb("d_sg", [128, 2, CH])
        hf = sb("d_hf", [128, 2, CH])
        p_up = es.enter_context(nc.psum_tensor("d_p_up", [128, 4, D], F32))
        p_y = es.enter_context(nc.psum_tensor("d_p_y", [128, TC, D], F32))
        rs_ready, xn_ready, t_ready, hi_ready, xt_ready, up_ready, terms_in, sg_ready, keep_ready, val_ready, \
            hh_ready, h_ready, down_done, y_ready, y_read, stats = (sem(n) for n in (
                "rs_ready", "xn_ready", "t_ready", "hi_ready", "xt_ready", "up_ready", "terms_in", "sg_ready",
                "keep_ready", "val_ready", "hh_ready", "h_ready", "down_done", "y_ready", "y_read", "stats"))
        NU = 1 + NF
        NV = DND - 1
        up_w = [w[:, 0:KB * UPD].rearrange("p (k n) -> p k n", k=KB) for w in (held.wd_hi, held.wd_lo)]
        dn_w = [w[:, KB * UPD:DW].rearrange("p (b n) -> p b n", b=DND) for w in (held.wd_hi, held.wd_lo)]
        rows = [128] * (G6 + 1) + [n for _, n in FB]

        with nc.Block() as block:
            @block.gpsimd
            def _(pool):
                rstd_all(nc, pool, held, rs_ready)

            @block.vector
            def _(v):
                v.wait_ge(rs_ready, 2)
                v.sem_inc(val_ready, 1)
                v.sem_inc(y_read, 1)
                with v.Fori(0, NC) as c:
                    for i in range(TC):
                        v.wait_ge(t_ready, TC * c + i + 1)
                        norm_tile(nc, held, xn[:, i % 2, :], TC * c + i).then_inc(xn_ready, 1)
                        if i:
                            low(v, nc, c, i - 1, hi_ready, xt_ready, xt, p_up)
                    low(v, nc, c, TC - 1, hi_ready, xt_ready, xt, p_up)
                    v.wait_ge(terms_in, 2 * c + 2)
                    nc.vector.tensor_scalar(keep[:], delta[:], 2.5, None, ALU.is_le).then_inc(keep_ready, 1)
                    v.wait_ge(keep_ready, 3 * c + 1)
                    nc.vector.scalar_tensor_tensor(keep[:], delta[:], -2.5, keep[:], ALU.is_ge,
                                                   ALU.mult).then_inc(keep_ready, 1)
                    for d in range(DND):
                        n = rows[d]
                        if d == 0:
                            value = term[:, 0, :]
                        elif d <= G6:
                            before = term[:, (d - 1) % 2, :]
                            if d > 1:
                                v.wait_ge(val_ready, NV * c + d)
                            if d == 5:
                                v.wait_ge(keep_ready, 3 * c + 2)
                                nc.vector.tensor_tensor(kept[:], before, keep[:], ALU.mult).then_inc(keep_ready, 1)
                                v.wait_ge(keep_ready, 3 * c + 3)
                                before = kept[:]
                            value = term[:, d % 2, :]
                            nc.vector.scalar_tensor_tensor(value, before, held.growth[:, d - 1:d], delta[:],
                                                           ALU.mult, ALU.mult).then_inc(val_ready, 1)
                        else:
                            j = d - G6
                            value = hf[0:n, d % 2, :]
                            v.wait_ge(sg_ready, NF * c + j)
                            nc.vector.scalar_tensor_tensor(value, p_up[0:n, 2 * (j % 2) + 1, :], HS / (XS * WS),
                                                           sg[0:n, d % 2, :], ALU.mult, ALU.mult).then_inc(val_ready, 1)
                        v.wait_ge(hh_ready, DND * c + d + 1)
                        nc.vector.tensor_tensor(hid[1][0:n, d % NH, :], value, hid[0][0:n, d % NH, :],
                                                ALU.subtract).then_inc(h_ready, 1)
                    for i in range(TC):
                        update_tile(v, nc, held, c, i, y_ready, p_y[:, i, :], HS * WS, y_read, (held.apart, stats))
                v.wait_ge(stats, NC * (2 * TC + 1))

            @block.scalar
            def _(act):
                with act.Fori(0, NC) as c:
                    act.wait_ge(down_done, DND * c + NH)
                    for i in range(TC):
                        high(act, nc, c, i, t_ready, hi_ready, xt, p_up)
                    act.wait_ge(up_ready, NU * c + 1)
                    nc.scalar.activation(term[:, 0, :], p_up[:, 0, :], ACT.Copy,
                                         scale=HS / (XS * WS)).then_inc(terms_in, 1)
                    nc.scalar.activation(delta[:], p_up[:, 1, :], ACT.Identity, bias=held.nlp[:, 0:1],
                                         scale=1.0 / (XS * WS)).then_inc(terms_in, 1)
                    for d in range(DND):
                        n = rows[d]
                        j = d - G6
                        if j == 0:
                            silu(act, nc, c, 1, FB[0][1], up_ready, sg_ready, sg, p_up, val_ready)
                        if j >= 1 and j < NF:
                            silu(act, nc, c, j + 1, FB[j][1], up_ready, sg_ready, sg, p_up, val_ready)
                        if d == 0:
                            act.wait_ge(terms_in, 2 * c + 1)
                            value = term[:, 0, :]
                        else:
                            act.wait_ge(val_ready, NV * c + d + 1)
                            value = term[:, d % 2, :] if d <= G6 else hf[0:n, d % 2, :]
                        act.wait_ge(down_done, DND * c + (NH if d < NH else d + 1))
                        nc.scalar.activation(hid[0][0:n, d % NH, :], value, ACT.Copy).then_inc(hh_ready, 1)

            @block.tensor
            def _(pe):
                pe.sem_inc(t_ready, 2)
                pe.sem_inc(down_done, NH)
                with pe.Fori(0, NC) as c:
                    pe.wait_ge(val_ready, NV * c + 1)
                    for i in range(TC):
                        pe.wait_ge(xn_ready, TC * c + i + 1)
                        transpose_tile(nc, held, p_up[:, i, :], xn[:, i % 2, :]).then_inc(t_ready, 1)
                    pe.wait_ge(xt_ready, TC * c + TC)

                    def up(j):
                        slot = 2 * (j % 2)
                        if j == 2:
                            pe.wait_ge(terms_in, 2 * c + 2)
                        if j > 2:
                            pe.wait_ge(val_ready, NV * c + G6 + j - 1)
                        at, n = (0, SD) if j == 0 else (2 * SD + FB[j - 1][0], FB[j - 1][1])
                        step = SD if j == 0 else FD
                        for half in range(2):
                            cols = slice(at + half * step, at + half * step + n)
                            for k in range(KB):
                                last = mm3(nc, p_up[0:n, slot + half, :], [w[:, k, cols] for w in up_w],
                                           [x[:, k, :] for x in xt], k == 0, k == KB - 1)
                        last.then_inc(up_ready, 1)

                    def down(d):
                        n = rows[d]
                        pe.wait_ge(h_ready, DND * c + d + 1)
                        if d == 0:
                            pe.wait_ge(y_read, TC * c + 1)
                        for i in range(TC):
                            last = mm3(nc, p_y[:, i, :], [h[0:n, d % NH, 128 * i:128 * i + 128] for h in hid],
                                       [w[0:n, d, :] for w in dn_w], d == 0, d == DND - 1)
                            if d == DND - 1:
                                last.then_inc(y_ready, 1)
                        if d < DND - 1:
                            last.then_inc(down_done, 1)
                    up(0)
                    up(1)
                    up(2)
                    for d in range(G6 + 1):
                        down(d)
                    for j in range(3, NU):
                        up(j)
                        down(G6 + j - 2)
                    down(DND - 2)
                    down(DND - 1)
                    pe.wait_ge(y_ready, TC * c + TC)
                    pe.sem_inc(down_done, 1)


def stage_e(nc, held, a):
    M = 128
    with ExitStack() as es:
        def sb(name, shape, dt=F32):
            return es.enter_context(nc.sbuf_tensor("e_" + name, shape, dt))

        def sem(name):
            return held.sems.enter_context(nc.semaphore("e_" + name))

        def pb(name, shape):
            return es.enter_context(nc.psum_tensor("e_" + name, shape, F32))

        NJ = 2 * KB
        wq = sb("wq", [S, S])
        wk = sb("wk", [S, S])
        wv = sb("wv", [128, 128])
        wskip = sb("wskip", [128, 128])
        wkq = sb("wkq", [128, 128])
        ctx = sb("ctx", [128, TC, M])
        xn = sb("xn", [128, 2, D])
        keys = sb("keys", [128, 2, 2, M])
        vt = sb("vt", [M, 2, 2, S])
        prob = sb("prob", [128, 2, NJ, M])
        top = sb("top", [128, 2, NJ])
        den = sb("den", [128, 2, NJ])
        pt = sb("pt", [M, 2, 2, D])
        p_s = pb("p_s", [128, 2, 2 * D])
        p_t = pb("p_t", [128, 2, D])
        p_o = pb("p_o", [128, D])
        p_m = pb("p_m", [128, D])
        w_in, clear, wkq_ready, wkq_in, rs_ready, ctx_in, ctx_read, xn_ready, m_ready, keys_ready, s_ready, \
            top_ready, sub_ready, exp_ready, den_ready, prob_ready, t_ready, pt0_ready, pt1_ready, o_ready, \
            o_read, stats = (sem(n) for n in (
                "w_in", "clear", "wkq_ready", "wkq_in", "rs_ready", "ctx_in", "ctx_read", "xn_ready", "m_ready",
                "keys_ready", "s_ready", "top_ready", "sub_ready", "exp_ready", "den_ready", "prob_ready",
                "t_ready", "pt0_ready", "pt1_ready", "o_ready", "o_read", "stats"))
        ctx_d = a["ctx"].rearrange("(t p) n -> p t n", p=128)

        with nc.Block() as block:
            @block.sync
            def _(sp):
                sp.dma_start(wq[:], a["Wq"]).then_inc(w_in, 16)
                sp.dma_start(wk[:], a["Wk"]).then_inc(w_in, 16)
                sp.wait_ge(clear, 2)
                for s in range(2):
                    half = slice(64 * s, 64 * s + 64)
                    sp.dma_start(wskip[half, half], a["WskipT"]).then_inc(w_in, 16)
                    sp.dma_start(wv[half, half], a["WvT"]).then_inc(w_in, 16)
                with sp.Fori(0, NC) as c:
                    sp.wait_ge(ctx_read, c + 1)
                    sp.dma_start(ctx[:], ctx_d[:, bass.ds(TC * c, TC), :]).then_inc(ctx_in, 16)

            @block.gpsimd
            def _(pool):
                nc.gpsimd.memset(wskip[:], 0.0).then_inc(clear, 1)
                nc.gpsimd.memset(wv[:], 0.0).then_inc(clear, 1)
                rstd_all(nc, pool, held, rs_ready)
                with pool.Fori(0, NC) as c:
                    for i in range(TC):
                        b, t = i % 2, TC * c + i
                        pool.wait_ge(den_ready, 2 * t + 2)
                        nc.gpsimd.tensor_tensor(
                            prob[:, b, :, :], prob[:, b, :, :],
                            den[:, b, :].rearrange("p (j a) -> p j a", a=1).broadcast_to([128, NJ, M]),
                            ALU.mult).then_inc(prob_ready, 1)

            @block.vector
            def _(v):
                nc.vector.memset(wkq[:], 0.0).then_inc(wkq_in, 1)
                nc.vector.memset(keys[:], 0.0).then_inc(wkq_in, 1)
                v.wait_ge(wkq_in, 2)
                v.wait_ge(wkq_ready, 1)
                for s in range(2):
                    half = slice(64 * s, 64 * s + 64)
                    nc.vector.tensor_copy(wkq[half, half], p_m[half, half]).then_inc(wkq_in, 1)
                v.wait_ge(rs_ready, 2)
                v.sem_inc(sub_ready, 2)
                v.sem_inc(pt1_ready, 1)
                v.sem_inc(o_read, 1)
                with v.Fori(0, NC) as c:
                    def norm(i):
                        t = TC * c + i
                        v.wait_ge(o_ready, t + 1)
                        norm_tile(nc, held, xn[:, i % 2, :], t).then_inc(xn_ready, 1)

                    def soft(i):
                        b, t = i % 2, TC * c + i
                        scores = p_s[:, b, :].rearrange("p (j m) -> p j m", j=NJ)
                        v.wait_ge(s_ready, t + 1)
                        nc.vector.tensor_reduce(top[:, b, :], scores, AX.X, ALU.max).then_inc(top_ready, 1)
                        v.wait_ge(top_ready, t + 1)
                        v.wait_ge(t_ready, t + 1)
                        nc.vector.tensor_tensor(
                            prob[:, b, :, :], scores,
                            top[:, b, :].rearrange("p (j a) -> p j a", a=1).broadcast_to([128, NJ, M]),
                            ALU.subtract).then_inc(sub_ready, 1)

                    def total(i):
                        b, t = i % 2, TC * c + i
                        v.wait_ge(exp_ready, t + 1)
                        nc.vector.tensor_reduce(den[:, b, :], prob[:, b, :, :], AX.X, ALU.add).then_inc(den_ready, 1)
                        v.wait_ge(den_ready, 2 * t + 1)
                        nc.vector.reciprocal(den[:, b, :], den[:, b, :]).then_inc(den_ready, 1)

                    def values(i):
                        t = TC * c + i
                        v.wait_ge(t_ready, t + 3)
                        v.wait_ge(o_ready, t + 1)
                        nc.vector.tensor_copy(pt[:, i % 2, 1, :], p_t[:, 1, :]).then_inc(pt1_ready, 1)

                    def update(i):
                        t = TC * c + i
                        v.wait_ge(o_ready, t + 3)
                        nc.vector.tensor_tensor(held.X[:, t, :], p_o[:], held.X[:, t, :], ALU.add).then_inc(o_read, 1)
                        stats_tile(v, nc, held, c, i, o_read, t + 2, (held.apart, stats))
                    norm(0)
                    soft(0)
                    for i in range(TC):
                        if i + 1 < TC:
                            if i:
                                update(i - 1)
                            norm(i + 1)
                            total(i)
                            soft(i + 1)
                        else:
                            update(i - 1)
                            total(i)
                        values(i)
                    update(TC - 1)
                v.wait_ge(stats, NC * (2 * TC + 1))

            @block.scalar
            def _(act):
                act.wait_ge(wkq_in, 4)
                act.sem_inc(keys_ready, 4)
                act.sem_inc(pt0_ready, 1)
                with act.Fori(0, NC) as c:
                    def keys_in(i):
                        b, t = i % 2, TC * c + i
                        act.wait_ge(m_ready, t + 1)
                        act.wait_ge(o_ready, t + 1)
                        for s in range(2):
                            half = slice(64 * s, 64 * s + 64)
                            nc.scalar.activation(keys[half, b, s, :], p_m[half, 0:M], ACT.Copy)
                        nc.scalar.activation(vt[:, b, :, :], p_m[:, M:2 * M].rearrange("p (s n) -> p s n", s=2),
                                             ACT.Copy).then_inc(keys_ready, 1)

                    def expo(i):
                        b, t = i % 2, TC * c + i
                        act.wait_ge(sub_ready, t + 3)
                        nc.scalar.activation(prob[:, b, :, :], prob[:, b, :, :], ACT.Exp,
                                             scale=S ** -0.5).then_inc(exp_ready, 1)

                    def values(i):
                        t = TC * c + i
                        act.wait_ge(t_ready, t + 3)
                        act.wait_ge(o_ready, t + 1)
                        nc.scalar.activation(pt[:, i % 2, 0, :], p_t[:, 0, :], ACT.Copy).then_inc(pt0_ready, 1)
                    keys_in(0)
                    expo(0)
                    for i in range(TC):
                        if i + 1 < TC:
                            keys_in(i + 1)
                            expo(i + 1)
                        values(i)

            @block.tensor
            def _(pe):
                pe.wait_ge(w_in, 96)
                for s in range(2):
                    half = slice(64 * s, 64 * s + 64)
                    last = nc.tensor.matmul(p_m[half, half], wk[:], wq[:], start=True, stop=True)
                last.then_inc(wkq_ready, 1)
                pe.wait_ge(wkq_in, 4)
                pe.sem_inc(o_ready, 2)
                pe.sem_inc(t_ready, 2)
                pe.sem_inc(ctx_read, 1)
                pe.wait_ge(keys_ready, 4)
                with pe.Fori(0, NC) as c:
                    def make_keys(i):
                        t = TC * c + i
                        if i == 0:
                            pe.wait_ge(ctx_in, 16 * c + 16)
                        pe.wait_ge(keys_ready, t + 4)
                        nc.tensor.matmul(p_m[:, 0:M], wkq[:], ctx[:, i, :], start=True, stop=True)
                        nc.tensor.matmul(p_m[:, M:2 * M], ctx[:, i, :], wv[:], start=True,
                                         stop=True).then_inc(m_ready, 1)
                        if i == TC - 1:
                            pe.wait_ge(m_ready, t + 1)
                            pe.sem_inc(ctx_read, 1)

                    def scores(i):
                        b, t = i % 2, TC * c + i
                        pe.wait_ge(xn_ready, t + 1)
                        pe.wait_ge(keys_ready, t + 5)
                        pe.wait_ge(sub_ready, t + 1)
                        for k in range(KB):
                            last = nc.tensor.matmul(p_s[:, b, 256 * k:256 * k + 256], xn[:, b, 128 * k:128 * k + 128],
                                                    keys[:, b, :, :].rearrange("p s m -> p (s m)"),
                                                    start=True, stop=True)
                        last.then_inc(s_ready, 1)

                    def transposes(i):
                        b, t = i % 2, TC * c + i
                        pe.wait_ge(prob_ready, t + 1)
                        pe.wait_ge(pt1_ready, t + 1)
                        pe.wait_ge(pt0_ready, t + 1)
                        for s in range(2):
                            for k in range(KB):
                                last = nc.tensor.transpose(p_t[:, s, 128 * k:128 * k + 128], prob[:, b, 2 * k + s, :],
                                                           held.ident[:])
                        last.then_inc(t_ready, 1)

                    def output(i):
                        b, t = i % 2, TC * c + i
                        pe.wait_ge(o_read, t + 1)
                        nc.tensor.matmul(p_o[:], wskip[:], xn[:, b, :], start=True, stop=False)
                        pe.wait_ge(pt0_ready, t + 2)
                        pe.wait_ge(pt1_ready, t + 2)
                        for s in range(2):
                            half = slice(64 * s, 64 * s + 64)
                            last = nc.tensor.matmul(p_o[half, :], vt[:, b, s, :], pt[:, b, s, :], start=False,
                                                    stop=True)
                        last.then_inc(o_ready, 1)
                    make_keys(0)
                    scores(0)
                    for i in range(TC):
                        if i + 1 < TC:
                            make_keys(i + 1)
                            scores(i + 1)
                        transposes(i)
                        output(i)


def stage_f(nc, held, a, out):
    with ExitStack() as es:
        def sb(name, shape, dt=F32):
            return es.enter_context(nc.sbuf_tensor("f_" + name, shape, dt))

        def sem(name):
            return held.sems.enter_context(nc.semaphore("f_" + name))

        NH = 3
        xn = sb("xn", [128, 2, D])
        xt = [sb("xt_high", [128, KB, CH], F16), sb("xt_low", [128, KB, CH], F16)]
        lat = [sb("lat_high", [128, FL, CH], F16), sb("lat_low", [128, FL, CH], F16)]
        hid = [sb("h_high", [128, NH, CH], F16), sb("h_low", [128, NH, CH], F16)]
        w2 = [sb("w2_high", [128, FL, D], F16), sb("w2_low", [128, FL, D], F16)]
        expert_t = sb("expert_t", [128, FL, LAT])
        fc2 = sb("fc2", [128, FL, D])
        relu = sb("relu", [128, 2, CH])
        sq = sb("sq", [128, 2, CH])
        routed = sb("routed", [128, TC, D])
        top8 = sb("top8", [128, TC, NE])
        route = sb("route", [128, TC])
        y = sb("y", [128, 2, D])
        yst = sb("yst", [128, 2, 6])
        ymv = sb("ymv", [128, 2, 2])
        yrs = sb("yrs", [128, 2, 2])
        p_up = es.enter_context(nc.psum_tensor("f_p_up", [128, 4, D], F32))
        p_y = es.enter_context(nc.psum_tensor("f_p_y", [128, TC, D], F32))
        rs_ready, w2_in, w2_ready, w2_split, xn_ready, t_ready, hi_ready, xt_ready, logit_ready, route_ready, \
            lat_ready, lat_hi, lat_lo, r_ready, r_read, up_ready, relu_ready, sq_ready, hh_ready, h_ready, \
            down_done, y_ready, y_read, y_steps, yrs_ready, final_steps, final = (sem(n) for n in (
                "rs_ready", "w2_in", "w2_ready", "w2_split", "xn_ready", "t_ready", "hi_ready", "xt_ready",
                "logit_ready", "route_ready", "lat_ready", "lat_hi", "lat_lo", "r_ready", "r_read", "up_ready",
                "relu_ready", "sq_ready", "hh_ready", "h_ready", "down_done", "y_ready", "y_read", "y_steps",
                "yrs_ready", "final_steps", "final"))
        stored = [sem(f"stored_{b}") for b in range(2)]
        up_w = [w[:, 0:KB * FC].rearrange("p (k n) -> p k n", k=KB) for w in (held.wf_hi, held.wf_lo)]
        dn_w = [w[:, KB * FC:FW].rearrange("p (b n) -> p b n", b=FU) for w in (held.wf_hi, held.wf_lo)]
        out_t = out.rearrange("(t p) n -> p t n", p=128)

        with nc.Block() as block:
            @block.sync
            def _(sp):
                sp.dma_start(expert_t[:], a["expertT"].rearrange("(k p) n -> p k n", p=128)).then_inc(w2_in, 16)
                sp.dma_start(fc2[:], a["fc2"].rearrange("(k p) n -> p k n", p=128)).then_inc(w2_in, 16)
                with sp.Fori(0, NC) as c:
                    for i in range(TC):
                        sp.wait_ge(final, TC * c + i + 1)
                        sp.dma_start(out_t[:, TC * c + i, :], y[:, i % 2, :]).then_inc(stored[i % 2], 16)
                for b in range(2):
                    sp.wait_ge(stored[b], 16 * (NT // 2) + 16)

            @block.gpsimd
            def _(pool):
                rstd_all(nc, pool, held, rs_ready)
                for b in range(2):
                    pool.sem_inc(stored[b], 16)
                with pool.Fori(0, NC) as c:
                    for i in range(TC):
                        b, t = i % 2, TC * c + i
                        wait_apart(pool, y_steps, 2 * t + 2, held.apart)
                        nc.gpsimd.tensor_scalar(yrs[:, b, 0:1], ymv[:, b, 1:2], EPS, None,
                                                ALU.add).then_inc(yrs_ready, 1)
                        pool.wait_ge(yrs_ready, 2 * t + 1)
                        nc.gpsimd.tensor_tensor(yrs[:, b, 1:2], yrs[:, b, 0:1], held.mhalf[:, 0:1],
                                                ALU.pow).then_inc(yrs_ready, 1)

            @block.vector
            def _(v):
                for k in range(FL):
                    v.wait_ge(w2_ready, k + 1)
                    nc.vector.tensor_scalar(w2[0][:, k, :], p_y[:, k, :], WS, None, ALU.mult).then_inc(w2_split, 1)
                    v.wait_ge(w2_split, 2 * k + 1)
                    nc.vector.scalar_tensor_tensor(w2[1][:, k, :], p_y[:, k, :], WS, w2[0][:, k, :],
                                                   ALU.mult, ALU.subtract).then_inc(w2_split, 1)
                v.wait_ge(rs_ready, 2)
                v.sem_inc(sq_ready, 1)
                v.sem_inc(y_read, 1)
                with v.Fori(0, NC) as c:
                    def finish(i):
                        b, t = i % 2, TC * c + i
                        v.wait_ge(y_ready, t + 1)
                        v.wait_ge(r_read, t + 1)
                        v.wait_ge(stored[b], 16 * (TC // 2 * c + i // 2) + 16)
                        nc.vector.scalar_tensor_tensor(y[:, b, :], p_y[:, i, :], 1.0 / (FS * WS), routed[:, i, :],
                                                       ALU.mult, ALU.add).then_inc(y_read, 1)
                        v.wait_ge(y_read, t + 2)
                        nc.vector.bn_stats(yst[:, b, :], y[:, b, :]).then_inc(y_steps, 1)
                        wait_apart(v, y_steps, 2 * t + 1, held.apart)
                        nc.vector.bn_aggr(ymv[:, b, :], yst[:, b, :]).then_inc(y_steps, 1)

                    def norm_out(i):
                        b, t = i % 2, TC * c + i
                        v.wait_ge(yrs_ready, 2 * t + 2)
                        nc.vector.tensor_scalar(y[:, b, :], y[:, b, :], ymv[:, b, 0:1], yrs[:, b, 1:2],
                                                ALU.subtract, ALU.mult).then_inc(final_steps, 1)
                        v.wait_ge(final_steps, 3 * t + 1)
                        nc.vector.tensor_tensor(y[:, b, :], y[:, b, :], held.gam[:], ALU.mult).then_inc(final_steps, 1)
                        v.wait_ge(final_steps, 3 * t + 2)
                        nc.vector.tensor_tensor(y[:, b, :], y[:, b, :], held.bet[:], ALU.add).then_inc(final_steps, 1)
                        v.wait_ge(final_steps, 3 * t + 3)
                        nc.vector.tensor_tensor(y[:, b, :], y[:, b, :], held.X[:, t, :], ALU.add).then_inc(final, 1)
                    for i in range(TC):
                        v.wait_ge(t_ready, TC * c + i + 1)
                        norm_tile(nc, held, xn[:, i % 2, :], TC * c + i).then_inc(xn_ready, 1)
                        if i:
                            low(v, nc, c, i - 1, hi_ready, xt_ready, xt, p_up)
                    low(v, nc, c, TC - 1, hi_ready, xt_ready, xt, p_up)
                    wait_apart(v, logit_ready, c + 1, held.apart)
                    for i in range(TC):
                        nc.vector.max(top8[:, i, :], p_up[:, 0, NE * i:NE * i + NE]).then_inc(route_ready, 1)
                    v.wait_ge(route_ready, (TC + 2) * c + TC)
                    nc.vector.tensor_tensor(route[:], top8[:, :, 0], top8[:, :, 1], ALU.add).then_inc(route_ready, 1)
                    v.wait_ge(route_ready, (TC + 2) * c + TC + 1)
                    nc.vector.tensor_scalar(route[:], route[:], 1.0 / (XS * WS * AS * WS), None,
                                            ALU.mult).then_inc(route_ready, 1)
                    for l in range(FL):
                        v.wait_ge(lat_hi, FL * c + l + 1)
                        nc.vector.scalar_tensor_tensor(lat[1][:, l, :], p_up[:, 1 + l, :], AS / (XS * WS),
                                                       lat[0][:, l, :], ALU.mult, ALU.subtract).then_inc(lat_lo, 1)
                    for f in range(FU):
                        v.wait_ge(relu_ready, FU * c + f + 1)
                        nc.vector.tensor_tensor(sq[:, f % 2, :], relu[:, f % 2, :], relu[:, f % 2, :],
                                                ALU.mult).then_inc(sq_ready, 1)
                        v.wait_ge(hh_ready, FU * c + f + 1)
                        nc.vector.tensor_tensor(hid[1][:, f % NH, :], sq[:, f % 2, :], hid[0][:, f % NH, :],
                                                ALU.subtract).then_inc(h_ready, 1)
                    finish(0)
                    for i in range(TC):
                        if i + 1 < TC:
                            finish(i + 1)
                        norm_out(i)

            @block.scalar
            def _(act):
                with act.Fori(0, NC) as c:
                    act.wait_ge(down_done, FU * c + NH)
                    for i in range(TC):
                        high(act, nc, c, i, t_ready, hi_ready, xt, p_up)
                    for l in range(FL):
                        act.wait_ge(lat_ready, FL * c + l + 1)
                        nc.scalar.activation(lat[0][:, l, :], p_up[:, 1 + l, :], ACT.Copy,
                                             scale=AS / (XS * WS)).then_inc(lat_hi, 1)
                    act.wait_ge(route_ready, (TC + 2) * (c + 1))
                    for i in range(TC):
                        act.wait_ge(r_ready, TC * c + i + 1)
                        nc.scalar.activation(routed[:, i, :], p_y[:, i, :], ACT.Copy,
                                             scale=route[:, i:i + 1]).then_inc(r_read, 1)
                    for f in range(FU + 1):
                        if f < FU:
                            act.wait_ge(up_ready, FU * c + f + 1)
                            if f >= 2:
                                act.wait_ge(sq_ready, FU * c + f)
                            nc.scalar.activation(relu[:, f % 2, :], p_up[:, f % 4, :], ACT.Relu,
                                                 scale=FS ** 0.5 / (XS * WS)).then_inc(relu_ready, 1)
                        if f:
                            g = f - 1
                            act.wait_ge(sq_ready, FU * c + g + 2)
                            act.wait_ge(down_done, FU * c + (NH if g < NH else g + 1))
                            nc.scalar.activation(hid[0][:, g % NH, :], sq[:, g % 2, :], ACT.Copy).then_inc(hh_ready, 1)

            @block.tensor
            def _(pe):
                pe.wait_ge(w2_in, 32)
                for l in range(FL):
                    for k in range(FL):
                        last = nc.tensor.matmul(p_y[:, l, :], expert_t[:, k, 128 * l:128 * l + 128], fc2[:, k, :],
                                                start=k == 0, stop=k == FL - 1)
                    last.then_inc(w2_ready, 1)
                pe.wait_ge(w2_split, 2 * FL)
                pe.sem_inc(t_ready, 2)
                pe.sem_inc(down_done, NH)
                with pe.Fori(0, NC) as c:
                    pe.wait_ge(sq_ready, FU * c + 1)
                    for i in range(TC):
                        pe.wait_ge(xn_ready, TC * c + i + 1)
                        transpose_tile(nc, held, p_up[:, i, :], xn[:, i % 2, :]).then_inc(t_ready, 1)
                    pe.wait_ge(xt_ready, TC * c + TC)
                    for i in range(TC):
                        for k in range(KB):
                            last = mm3(nc, p_up[:, 0, NE * i:NE * i + NE],
                                       [x[:, k, 128 * i:128 * i + 128] for x in xt],
                                       [w[:, k, INT + LAT:FC] for w in up_w], k == 0, k == KB - 1)
                    last.then_inc(logit_ready, 1)
                    for l in range(FL):
                        for k in range(KB):
                            last = mm3(nc, p_up[:, 1 + l, :], [w[:, k, INT + 128 * l:INT + 128 * l + 128] for w in up_w],
                                       [x[:, k, :] for x in xt], k == 0, k == KB - 1)
                        last.then_inc(lat_ready, 1)

                    def up(f):
                        if f == 0:
                            pe.wait_ge(route_ready, (TC + 2) * c + TC)
                        elif f <= 2:
                            pe.wait_ge(lat_lo, FL * c + f)
                        elif f >= 4:
                            pe.wait_ge(sq_ready, FU * c + f - 2)
                        for k in range(KB):
                            last = mm3(nc, p_up[:, f % 4, :], [w[:, k, 128 * f:128 * f + 128] for w in up_w],
                                       [x[:, k, :] for x in xt], k == 0, k == KB - 1)
                        last.then_inc(up_ready, 1)

                    def down(f):
                        pe.wait_ge(h_ready, FU * c + f + 1)
                        if f == 0:
                            pe.wait_ge(r_read, TC * c + TC)
                        for i in range(TC):
                            last = mm3(nc, p_y[:, i, :], [h[:, f % NH, 128 * i:128 * i + 128] for h in hid],
                                       [w[:, f, :] for w in dn_w], f == 0, f == FU - 1)
                            if f == FU - 1:
                                last.then_inc(y_ready, 1)
                        if f < FU - 1:
                            last.then_inc(down_done, 1)
                    up(0)
                    pe.wait_ge(lat_lo, FL * c + FL)
                    pe.wait_ge(y_read, TC * c + 1)
                    for i in range(TC):
                        for l in range(FL):
                            last = mm3(nc, p_y[:, i, :], [x[:, l, 128 * i:128 * i + 128] for x in lat],
                                       [w[:, l, :] for w in w2], l == 0, l == FL - 1)
                        last.then_inc(r_ready, 1)
                    up(1)
                    for f in range(2, FU):
                        up(f)
                        down(f - 2)
                    down(FU - 2)
                    down(FU - 1)
                    pe.wait_ge(y_ready, TC * c + TC)
                    pe.sem_inc(down_done, 1)


STAGES = "ABCDEF"


def build(nc, a, out):
    held = Held()
    with ExitStack() as es:
        def sb(name, shape, dt=F32):
            return es.enter_context(nc.sbuf_tensor(name, shape, dt))

        held.sems = es
        held.apart = es.enter_context(nc.semaphore("apart"))
        held.X = sb("X", [128, NT, D])
        held.mv = sb("mv", [128, NT, 2])
        held.st = sb("st", [128, TC, 6])
        held.mvc = sb("mvc", [128, TC, 2])
        held.ve = sb("ve", [128, NT])
        held.rstd = sb("rstd", [128, NT, 1])
        held.mhalf = sb("mhalf", [128, NT])
        held.ident = sb("ident", [128, 128])
        held.ones = sb("ones", [128, 128])
        held.onehot = sb("onehot", [128, 128], BF16)
        held.mask_a = sb("mask_a", [96, 8])
        held.mask_b = sb("mask_b", [128, 2])
        held.mask_bs = sb("mask_bs", [128, 2])
        held.mk01 = sb("mk01", [128, S], BF16)
        held.mk2 = sb("mk2", [S, S], BF16)
        held.nlp = sb("nlp", [128, 1])
        held.growth = sb("growth", [128, G6])
        held.gam = sb("gam", [128, D])
        held.bet = sb("bet", [128, D])
        held.ebias = sb("ebias", [128, EX4])
        held.rank = sb("rank", [128, EX4])
        held.lora_b = sb("lora_b", [EX4 * R8, D])
        held.wd_hi = sb("wd_hi", [128, DW], F16)
        held.wd_lo = sb("wd_lo", [128, DW], F16)
        with ExitStack() as early:
            def se(name, shape, dt=F32):
                return early.enter_context(nc.sbuf_tensor(name, shape, dt))
            held.wc_hi = se("wc_hi", [128, CW], F16)
            held.wc_lo = se("wc_lo", [128, CW], F16)
            held.kq_bias = se("kq_bias", [128, 1])
            held.wkq = se("wkq", [128, KB, 96 + QL])
            held.wqk = se("wqk", [128, 4, 96])
            held.qk_bias = se("qk_bias", [96, 4])
            held.qk_bias_s = se("qk_bias_s", [96, 4])
            held.wvo = se("wvo", [128, D])
            held.bvo = se("bvo", [1, D])
            setup_stage(nc, held, a)
            if "A" in STAGES:
                stage_a(nc, held, a)
            if "B" in STAGES:
                stage_b(nc, held, a)
            load_weights(nc, held, "wc", a["w_c"], held.wc_hi, held.wc_lo, NP_C, PC)
            load_weights(nc, held, "wd", a["w_d"], held.wd_hi, held.wd_lo, NP_D, PD)
            if "C" in STAGES:
                stage_c(nc, held, a)
        held.wf_hi = sb("wf_hi", [128, FW], F16)
        held.wf_lo = sb("wf_lo", [128, FW], F16)
        if "D" in STAGES:
            stage_d(nc, held, a)
        if "E" in STAGES:
            stage_e(nc, held, a)
        if "F" in STAGES:
            load_weights(nc, held, "wf", a["w_f"], held.wf_hi, held.wf_lo, NP_F, PF)
            stage_f(nc, held, a, out)
        else:
            done = held.sems.enter_context(nc.semaphore("out_done"))
            with nc.Block() as block:
                @block.sync
                def _(sp):
                    sp.dma_start(out.rearrange("(t p) n -> p t n", p=128), held.X[:]).then_inc(done, 16)
                    sp.wait_ge(done, 16)


def on_partitions(np, w):
    k, n = w.shape[0] // 128, w.shape[1]
    return w.reshape(k, 128, n).transpose(1, 0, 2).reshape(128, k * n)


def kernel(**inputs):
    import numpy as np
    import concourse.bacc as bacc
    from concourse.bass_utils import run_bass_kernel_spmd

    i = {k: np.asarray(v) for k, v in inputs.items()}
    L = lambda w: on_partitions(np, w)
    fuse = i["L1_attn_fuse_weight"]
    ffn_down = i["L1_attn_ffn_down_w"].T
    pad = np.zeros((128 * len(FB) - FD, D), ffn_down.dtype)
    w_d_up = np.concatenate([i["L1_attn_up_w"].T, i["L1_attn_gate_w"].T, i["L1_attn_ffn_gate_w"].T,
                             i["L1_attn_ffn_up_w"].T], 1)
    w_d_dn = np.concatenate([i["L1_attn_local_approx_output"].T, fuse.transpose(2, 1, 0).reshape(G6 * SD, D),
                             ffn_down, pad], 0)
    lora_a = i["L0_ffn_lora_A"].reshape(EX4 * R8, D).T
    ctx = i["ctx_1024"]
    arrays = {
        "x": i["x"].reshape(TOK, D),
        "ctx": ctx.reshape(TOK, 128),
        "ctx_t": ctx.transpose(2, 0, 1).reshape(128, TOK),
        "mask": i["mask_SxS2_ff0"],
        "Wkvq": np.concatenate([i["L0_attn_Wkv_d"], i["L0_attn_Wq_d"]], 1),
        "bq_d": i["L0_attn_bq_d"], "bkv_rep": np.tile(i["L0_attn_bkv_d"], 24),
        "W_qk": i["L0_attn_W_qk"], "b_qkT": i["L0_attn_b_qk"].reshape(4, 32).T,
        "Wv_uT": i["L0_attn_Wv_u"].T, "bv_uT": i["L0_attn_bv_u"].reshape(4, 128).T, "Wo": i["L0_attn_Wo"], "bo": i["L0_attn_bo"],
        "w_c": np.concatenate([L(i["L0_ffn_W_up"].T), L(np.concatenate([i["L0_ffn_gate_w"].T, lora_a], 1))], 1),
        "expert_bias": i["L0_ffn_expert_bias"],
        "lora_B": i["L0_ffn_lora_B"].transpose(0, 2, 1).reshape(EX4 * R8, D),
        "w_d": np.concatenate([L(w_d_up), L(w_d_dn)], 1),
        "local_point": i["L1_attn_local_point"], "discount": i["L1_attn_discount_factor"],
        "Wk": i["L1_xattn_Wk"], "Wq": i["L1_xattn_Wq"], "WvT": i["L1_xattn_Wv"].T, "WskipT": i["L1_xattn_Wskip"].T,
        "w_f": np.concatenate([L(np.concatenate([i["L1_ffn_up_w"], i["L1_ffn_fc1_w"], i["L1_ffn_gate_w"]], 1)),
                               L(i["L1_ffn_down_w"])], 1),
        "expertT": i["L1_ffn_expert_w"].T, "fc2": i["L1_ffn_fc2_w"],
        "gamma": i["L1_ffn_ln_gamma"], "beta": i["L1_ffn_ln_beta"],
    }
    arrays = {k: np.ascontiguousarray(v) for k, v in arrays.items()}
    nc = bacc.Bacc("TRN2", target_bir_lowering=False, num_devices=1)
    a = {k: nc.dram_tensor("in_" + k, v.shape, F32, kind="ExternalInput").ap() for k, v in arrays.items()}
    out = nc.dram_tensor("out_x", (TOK, D), F32, kind="ExternalOutput").ap()
    build(nc, a, out)
    r = run_bass_kernel_spmd(nc, [{"in_" + k: v for k, v in arrays.items()}], core_ids=[0])
    return r.results[0]["out_x"].reshape(NSEQ, S, D)
```

```python
from contextlib import ExitStack

import concourse.bass as bass
from concourse import mybir

F32 = mybir.dt.float32
F16 = mybir.dt.float16
BF16 = mybir.dt.bfloat16
ALU = mybir.AluOpType
ACT = mybir.ActivationFunctionType
AX = mybir.AxisListType

NSEQ, S, D = 32, 64, 512
TOK = NSEQ * S
NT = TOK // 128
KB = D // 128
NC = 4
TC = NT // NC
CH = 128 * TC
EPS = 1e-5
H = 32
DL = 4
QL = 12
DH = D // H
G8 = 8
XS = 2.0 ** 8
WS = 2.0 ** 8
HS = 2.0 ** 2
FS = 2.0 ** 4
PS = 2.0 ** 14
AS = 2.0 ** 6
EX4, R8 = 4, 8
CG = EX4 + EX4 * R8
CW = KB * (D + CG)
SD, G6 = 128, 6
FD = 1248
FB = [(i, min(128, FD - i)) for i in range(0, FD, 128)]
UPD = 2 * SD + 2 * FD
DND = G6 + 1 + len(FB)
DW = KB * UPD + DND * D
INT, LAT, NE = 1024, 256, 8
FU, FL = INT // 128, LAT // 128
FC = INT + LAT + NE
FW = KB * FC + FU * D
NP_D, NP_C, NP_F = 16, 4, 8
PD, PC, PF = DW // NP_D, CW // NP_C, FW // NP_F
assert PD * NP_D == DW and PC * NP_C == CW and PF * NP_F == FW


class Held:
    pass


def row(v):
    return v.rearrange("(a n) -> a n", a=1)


def wait_apart(eng, sem, value, marks):
    eng.wait_ge(sem, value)
    eng.sem_inc(marks, 1)


def norm_tile(nc, held, xn, t):
    return nc.vector.tensor_scalar(xn, held.X[:, t, :], held.mv[:, t, 0:1], held.rstd[:, t, 0:1],
                                   ALU.subtract, ALU.mult)


def transpose_tile(nc, held, ps, xn):
    for k in range(KB):
        last = nc.tensor.transpose(ps[:, 128 * k:128 * k + 128], xn[:, 128 * k:128 * k + 128], held.ident[:])
    return last


def mm3(nc, ps, st, mv, start, stop):
    nc.tensor.matmul(ps, st[0], mv[0], start=start, stop=False)
    nc.tensor.matmul(ps, st[0], mv[1], start=False, stop=False)
    return nc.tensor.matmul(ps, st[1], mv[0], start=False, stop=stop)


def rstd_all(nc, pool, held, ready):
    nc.gpsimd.tensor_scalar(held.ve[:], held.mv[:, :, 1], EPS, None, ALU.add).then_inc(ready, 1)
    pool.wait_ge(ready, 1)
    nc.gpsimd.tensor_tensor(held.rstd[:, :, 0], held.ve[:], held.mhalf[:], ALU.pow).then_inc(ready, 1)


def split_piece(nc, pool, raw, hi, lo, loaded, loaded_at, done, done_at, marks):
    wait_apart(pool, loaded, loaded_at, marks)
    nc.gpsimd.tensor_scalar(raw, raw, WS, None, ALU.mult).then_inc(done, 1)
    wait_apart(pool, done, done_at + 1, marks)
    nc.gpsimd.tensor_copy(hi, raw).then_inc(done, 1)
    wait_apart(pool, done, done_at + 2, marks)
    nc.gpsimd.tensor_tensor(lo, raw, hi, ALU.subtract).then_inc(done, 1)


def setup_stage(nc, held, a):
    with ExitStack() as es:
        def sb(name, shape, dt=F32):
            return es.enter_context(nc.sbuf_tensor(name, shape, dt))

        def sem(name):
            return held.sems.enter_context(nc.semaphore(name))

        def pb(name, shape):
            return es.enter_context(nc.psum_tensor(name, shape, F32))

        sel_wv = sb("sel_wv", [128, 4, H])
        sel_a = sb("sel_a", [96, 8, 3])
        sel_b = sb("sel_b", [128, 2, 4])
        sel_o = sb("sel_o", [128, 128, 3])
        wv_t = sb("wv_t", [128, 4, DL])
        wv_bd = sb("wv_bd", [128, 4, H, DL])
        wo = sb("wo", [128, 4, D])
        bv_col = sb("bv_col", [128, 4])
        bv_rep = sb("bv_rep", [128, 4, 128])
        bo = sb("bo", [1, D])
        wkv = sb("wkv", [128, KB, DL + QL])
        mask4 = sb("mask4", [128, S])
        mask_rest = sb("mask_rest", [128, S])
        disc = sb("disc", [128, G6])
        growth = sb("growth_log", [128, G6])
        p_wvo = pb("p_wvo", [128, D])
        p_bvo = pb("p_bvo", [128, D])
        x_in, par_in, pat, cast, wv_ready, growth_ready, growth_exp, fold_ready = (
            sem("su_" + n) for n in ("x_in", "par_in", "pattern", "cast", "wv_ready", "growth_ready",
                                     "growth_exp", "fold_ready"))
        loads = [
            (wv_t[:], a["Wv_uT"].rearrange("(o p) d -> p o d", p=128)),
            (wo[:], a["Wo"].rearrange("(o p) n -> p o n", p=128)),
            (bv_col[:], a["bv_uT"]),
            (bo[:], row(a["bo"])),
            (wkv[:], a["Wkvq"].rearrange("(k p) n -> p k n", p=128)),
            (disc[:], row(a["discount"]).broadcast_to([128, G6])),
            (held.nlp[:], a["local_point"].rearrange("(p a) -> p a", a=1)),
            (held.gam[:], row(a["gamma"]).broadcast_to([128, D])),
            (held.bet[:], row(a["beta"]).broadcast_to([128, D])),
            (held.ebias[:], row(a["expert_bias"]).broadcast_to([128, EX4])),
            (held.lora_b[:], a["lora_B"]),
            (held.kq_bias[0:96, :], a["bkv_rep"].rearrange("(p a) -> p a", a=1)),
            (held.kq_bias[96:96 + QL, :], a["bq_d"].rearrange("(p a) -> p a", a=1)),
        ]
        loads += [(mask4[64 * j:64 * j + 64, :], a["mask"]) for j in range(2)]
        for part in range(3):
            r = slice(32 * part, 32 * part + 32)
            loads += [(held.wqk[96:96 + QL, :, r], a["W_qk"].rearrange("q (g n) -> q g n", g=4)),
                      (held.wqk[96 + QL:97 + QL, :, r], a["b_qk"].rearrange("(a g n) -> a g n", a=1, g=4))]
        on_sp, on_act = loads[0::2], loads[1::2]
        par_all = 16 * len(loads)
        with nc.Block() as block:
            @block.sync
            def _(sp):
                for dst, src in on_sp:
                    sp.dma_start(dst, src).then_inc(par_in, 16)
                for q in range(NC):
                    sp.dma_start(held.X[:, TC * q:TC * q + TC, :],
                                 a["x"][CH * q:CH * q + CH, :].rearrange("(t p) n -> p t n", p=128)).then_inc(x_in, 16)
                sp.wait_ge(par_in, par_all)
                sp.wait_ge(x_in, 16 * NC)

            @block.gpsimd
            def _(pool):
                built = 0

                def put(ins):
                    nonlocal built
                    built += 1
                    ins.then_inc(pat, 1)

                def band(t, base, pattern, width):
                    put(nc.gpsimd.affine_select(out=t, in_=t, compare_op=ALU.is_ge, fill=0.0, base=base,
                                                pattern=pattern, channel_multiplier=1))
                    pool.wait_ge(pat, built)
                    put(nc.gpsimd.affine_select(out=t, in_=t, compare_op=ALU.is_ge, fill=0.0,
                                                base=width - 1 - base, pattern=[[-st, n] for st, n in pattern],
                                                channel_multiplier=-1))
                for t in (held.ident, sel_wv, sel_a, sel_b, sel_o, held.ones):
                    put(nc.gpsimd.memset(t[:], 1.0))
                put(nc.gpsimd.memset(held.mhalf[:], -0.5))
                put(nc.gpsimd.memset(held.units[:], AS))
                pool.wait_ge(pat, built)
                band(held.ident[:], 0, [[-1, 128]], 1)
                band(sel_wv[:], 0, [[128, 4], [-DH, H]], DH)
                band(sel_a[:], 0, [[-DL, 8], [-32, 3]], DL)
                band(sel_b[:], 0, [[-DH, 2], [-32, 4]], DH)
                band(sel_o[:], -64, [[-1, 128], [64, 3]], 1)
                assert built == 18

            @block.vector
            def _(v):
                made = 0

                def step(ins):
                    nonlocal made
                    made += 1
                    ins.then_inc(cast, 1)
                v.wait_ge(pat, 18)
                step(nc.vector.tensor_reduce(held.mask_a[:], sel_a[:], AX.X, ALU.add))
                step(nc.vector.tensor_reduce(held.mask_b[:], sel_b[:], AX.X, ALU.add))
                v.wait_ge(cast, made)
                step(nc.vector.tensor_scalar(held.mask_bs[:], held.mask_b[:], AS, None, ALU.mult))
                step(nc.vector.tensor_reduce(held.onehot[:], sel_o[:], AX.X, ALU.max))
                for e in range(EX4):
                    step(nc.vector.memset(held.rank[:, e:e + 1], float(EX4 - e)))
                v.wait_ge(par_in, par_all)
                for o in range(4):
                    nc.vector.tensor_tensor(
                        wv_bd[:, o, :, :], wv_t[:, o:o + 1, :].broadcast_to([128, H, DL]),
                        sel_wv[:, o, :].rearrange("p (h a) -> p h a", a=1).broadcast_to([128, H, DL]),
                        ALU.mult).then_inc(wv_ready, 1)
                    nc.vector.tensor_scalar(bv_rep[:, o, :], held.ones[:], bv_col[:, o:o + 1], None,
                                            ALU.mult).then_inc(wv_ready, 1)
                nc.vector.tensor_copy(growth[:, 0:1], disc[:, 0:1]).then_inc(growth_ready, 1)
                nc.vector.tensor_tensor(growth[:, 1:G6], disc[:, 1:G6], disc[:, 0:G6 - 1],
                                        ALU.subtract).then_inc(growth_ready, 1)
                step(nc.vector.tensor_scalar(held.nlp[:], held.nlp[:], -1.0, None, ALU.mult))
                step(nc.vector.tensor_copy(
                    held.wkq[:, :, 0:96].rearrange("p k (r d) -> p k r d", d=DL),
                    wkv[:, :, 0:DL].rearrange("p k (a d) -> p k a d", a=1).broadcast_to([128, KB, 24, DL])))
                step(nc.vector.tensor_copy(held.wkq[:, :, 96:96 + QL], wkv[:, :, DL:DL + QL]))
                step(nc.vector.tensor_scalar(mask4[:], mask4[:], DH ** 0.5 * XS * AS, None, ALU.mult))
                v.wait_ge(cast, made)
                step(nc.vector.tensor_copy(held.mk01[:], mask4[:]))
                v.wait_ge(cast, made)
                step(nc.vector.tensor_tensor(mask_rest[:], mask4[:], held.mk01[:], ALU.subtract))
                v.wait_ge(cast, made)
                step(nc.vector.tensor_copy(held.mk01[64:128, :], mask_rest[64:128, :]))
                step(nc.vector.tensor_copy(held.mk2[:], mask_rest[0:64, :]))
                v.wait_ge(cast, made)
                step(nc.vector.tensor_tensor(held.mk2[:], mask_rest[0:64, :], held.mk2[:], ALU.subtract))
                for t in range(NT):
                    v.wait_ge(x_in, 16 * NC)
                    step(nc.vector.bn_stats(held.st[:, t % TC, :], held.X[:, t, :]))
                    v.wait_ge(cast, made)
                    step(nc.vector.bn_aggr(held.mv[:, t, :], held.st[:, t % TC, :]))
                v.wait_ge(fold_ready, 1)
                step(nc.vector.tensor_scalar(held.wvo[0][:], p_wvo[:], WS, None, ALU.mult))
                v.wait_ge(fold_ready, 2)
                step(nc.vector.tensor_scalar(held.bvo[0][:], p_bvo[0:1, :], WS, None, ALU.mult))
                v.wait_ge(cast, made)
                step(nc.vector.scalar_tensor_tensor(held.wvo[1][:], p_wvo[:], WS, held.wvo[0][:],
                                                    ALU.mult, ALU.subtract))
                step(nc.vector.scalar_tensor_tensor(held.bvo[1][:], p_bvo[0:1, :], WS, held.bvo[0][:],
                                                    ALU.mult, ALU.subtract))
                v.wait_ge(cast, made)

            @block.tensor
            def _(pe):
                pe.wait_ge(par_in, par_all)
                pe.wait_ge(wv_ready, 8)
                for o in range(4):
                    last = nc.tensor.matmul(p_wvo[:], wv_bd[:, o, :, :].rearrange("p h d -> p (h d)"), wo[:, o, :],
                                            start=o == 0, stop=o == 3)
                last.then_inc(fold_ready, 1)
                for o in range(4):
                    nc.tensor.matmul(p_bvo[:], bv_rep[:, o, :], wo[:, o, :], start=o == 0, stop=False)
                pe.wait_ge(pat, 18)
                nc.tensor.matmul(p_bvo[:], held.ones[0:1, :], bo[:], start=False, stop=True).then_inc(fold_ready, 1)

            @block.scalar
            def _(act):
                for dst, src in on_act:
                    act.dma_start(dst, src).then_inc(par_in, 16)
                act.wait_ge(growth_ready, 2)
                nc.scalar.activation(held.growth[:], growth[:], ACT.Exp, scale=-1.0).then_inc(growth_exp, 1)
                act.wait_ge(growth_exp, 1)


def high(act, nc, c, i, t_ready, hi_ready, xt, ps):
    act.wait_ge(t_ready, TC * c + i + 3)
    nc.scalar.activation(xt[0][:, :, 128 * i:128 * i + 128], ps[:, i, :].rearrange("p (k n) -> p k n", k=KB),
                         ACT.Copy, scale=XS).then_inc(hi_ready, 1)


def low(v, nc, c, i, hi_ready, xt_ready, xt, ps):
    tile = slice(128 * i, 128 * i + 128)
    v.wait_ge(hi_ready, TC * c + i + 1)
    nc.vector.scalar_tensor_tensor(xt[1][:, :, tile], ps[:, i, :].rearrange("p (k n) -> p k n", k=KB), XS,
                                   xt[0][:, :, tile], ALU.mult, ALU.subtract).then_inc(xt_ready, 1)


def silu(act, nc, c, j, n, up_ready, sg_ready, sg, p_up, val_ready):
    act.wait_ge(up_ready, (1 + len(FB)) * c + j + 1)
    if j > 2:
        act.wait_ge(val_ready, (DND - 1) * c + G6 + j - 1)
    nc.scalar.activation(sg[0:n, (j + G6) % 2, :], p_up[0:n, 2 * (j % 2), :], ACT.Silu,
                         scale=1.0 / (XS * WS)).then_inc(sg_ready, 1)


def update_tile(v, nc, held, c, i, ready, x_sum, scale, read, marks):
    t = TC * c + i
    v.wait_ge(ready, t + 1)
    nc.vector.scalar_tensor_tensor(held.X[:, t, :], x_sum, 1.0 / scale, held.X[:, t, :],
                                   ALU.mult, ALU.add).then_inc(read, 1)
    stats_tile(v, nc, held, c, i, read, t + 2, marks)


def stats_tile(v, nc, held, c, i, read, read_at, marks):
    apart, stats = marks
    k = (2 * TC + 1) * c + 2 * i
    wait_apart(v, read, read_at, apart)
    nc.vector.bn_stats(held.st[:, i, :], held.X[:, TC * c + i, :]).then_inc(stats, 1)
    wait_apart(v, stats, k + 1, apart)
    nc.vector.bn_aggr(held.mvc[:, i, :], held.st[:, i, :]).then_inc(stats, 1)
    if i == TC - 1:
        v.wait_ge(stats, k + 2)
        nc.vector.tensor_scalar(held.mv[:, bass.ds(TC * c, TC), :], held.mvc[:], 1.0, None, ALU.mult).then_inc(stats, 1)


class Weights:

    def __init__(self, nc, held, es, name, dram, hi, lo, pieces, width):
        self.nc, self.held, self.dram, self.hi, self.lo, self.pieces, self.width = nc, held, dram, hi, lo, pieces, width
        self.raw = es.enter_context(nc.sbuf_tensor(name + "_raw", [128, 2, width], F32))
        self.loaded = [held.sems.enter_context(nc.semaphore(f"{name}_loaded_{j}")) for j in range(2)]
        self.split = held.sems.enter_context(nc.semaphore(name + "_split"))

    def fetch(self, sp):
        width = self.width
        with sp.Fori(0, self.pieces // 2) as q:
            for j in range(2):
                sp.wait_ge(self.split, 6 * q + 3 * j + 3)
                sp.dma_start(self.raw[:, j, :],
                             self.dram[:, bass.ds((2 * q + j) * width, width)]).then_inc(self.loaded[j], 16)

    def divide(self, pool):
        nc, width = self.nc, self.width
        pool.sem_inc(self.split, 6)
        with pool.Fori(0, self.pieces // 2) as q:
            for j in range(2):
                part = bass.ds((2 * q + j) * width, width)
                split_piece(nc, pool, self.raw[:, j, :], self.hi[:, part], self.lo[:, part], self.loaded[j],
                            16 * q + 16, self.split, 6 * q + 3 * j + 6, self.held.apart)
        pool.wait_ge(self.split, 3 * self.pieces + 6)


NU = 2 * TC
UH = H // 2


def soft_unit(nc, v, sems, bufs, u, slot):
    s_ready, top_ready, t_ready, sub_ready = sems
    p_s, top, prob = bufs
    scores = p_s[:, 2 * slot:2 * slot + 2, :].rearrange("p b (h k) -> p (b h) k", k=S)
    v.wait_ge(s_ready, u + 1)
    nc.vector.tensor_reduce(top[:, slot, :], scores, AX.X, ALU.max).then_inc(top_ready, 1)
    v.wait_ge(top_ready, u + 1)
    v.wait_ge(t_ready, 2 * u + 2)
    nc.vector.tensor_tensor(prob[:, slot, :, :], scores,
                            top[:, slot, :].rearrange("p (h a) -> p h a", a=1).broadcast_to([128, UH, S]),
                            ALU.subtract).then_inc(sub_ready, 1)


def exp_unit(nc, act, sub_ready, exp_ready, prob, u, slot, scale):
    act.wait_ge(sub_ready, u + 3)
    nc.scalar.activation(prob[:, slot, :, :], prob[:, slot, :, :], ACT.Exp, scale=scale).then_inc(exp_ready, 1)


def transpose_unit(nc, pe, held, sems, p_t, prob, u, slot):
    exp_ready, pt_ready, t_ready = sems
    pe.wait_ge(exp_ready, u + 1)
    for b in range(2):
        pe.wait_ge(pt_ready, 2 * u + b + 1)
        for j in range(UH // 4):
            last = nc.tensor.transpose(p_t[:, b, 128 * j:128 * j + 128],
                                       prob[:, slot, UH // 2 * b + 2 * j:UH // 2 * b + 2 * j + 2, :]
                                       .rearrange("p h k -> p (h k)"), held.ident[:])
        last.then_inc(t_ready, 1)


def high_pt(nc, act, sems, pt, p_t, u, slot):
    t_ready, v_ready, pt_high = sems
    for b in range(2):
        act.wait_ge(t_ready, 2 * u + b + 5)
        if b == 0:
            act.wait_ge(v_ready, u + 1)
        nc.scalar.activation(pt[0][:, slot, b, :], p_t[:, b, :], ACT.Copy, scale=PS).then_inc(pt_high, 1)


def low_pt(nc, v, pt_high, pt_ready, pt, p_t, u, slot):
    for b in range(2):
        v.wait_ge(pt_high, 2 * u + b + 1)
        nc.vector.scalar_tensor_tensor(pt[1][:, slot, b, :], p_t[:, b, :], PS, pt[0][:, slot, b, :],
                                       ALU.mult, ALU.subtract).then_inc(pt_ready, 1)


def stage_a(nc, held, a):
    with ExitStack() as es:
        def sb(name, shape, dt=F32):
            return es.enter_context(nc.sbuf_tensor("a_" + name, shape, dt))

        def sem(name):
            return held.sems.enter_context(nc.semaphore("a_" + name))

        def pb(name, shape):
            return es.enter_context(nc.psum_tensor("a_" + name, shape, F32))

        PR = 96
        PREP = 19
        VC = 2 * (DL + 1)
        xn = sb("xn", [128, 2, D])
        xt = sb("xt", [128, KB, CH])
        kf = sb("kf", [128, CH])
        keys = sb("keys", [PR, CH], F16)
        bd = sb("bd", [PR, 8, CH], F16)
        qs = sb("qs", [PR, 4, CH], F16)
        vb = [sb("vb_high", [128, 2 * TC, 2, DL + 1], F16), sb("vb_low", [128, 2 * TC, 2, DL + 1], F16)]
        top = sb("top", [128, 2, UH])
        prob = sb("prob", [128, 2, UH, S])
        pt = [sb("pt_high", [128, 2, 2, D], F16), sb("pt_low", [128, 2, 2, D], F16)]
        rec = sb("rec", [128, 2, UH])
        z = sb("z", [128, TC, H, DL])
        zt = [sb("zt_high", [128, CH], F16), sb("zt_low", [128, CH], F16)]
        p_s = pb("p_s", [128, 4, D])
        p_t = pb("p_t", [128, 2, D])
        p_v = pb("p_v", [128, 2, D])
        p_x = p_v[:, 1, :]
        rs_ready, vb_clear, xn_ready, tr_ready, xt_ready, lat_ready, cq_ready, prep, vt_ready, q_ready, q_high, \
            s_ready, top_ready, sub_ready, exp_ready, t_ready, pt_high, pt_ready, v_ready, rec_ready, z_part, \
            z_ready, zt_ready, zt_high, zt_low, o_ready, x_read, stats = (sem(n) for n in (
                "rs_ready", "vb_clear", "xn_ready", "tr_ready", "xt_ready", "lat_ready", "cq_ready", "prep",
                "vt_ready", "q_ready", "q_high", "s_ready", "top_ready", "sub_ready", "exp_ready", "t_ready",
                "pt_high", "pt_ready", "v_ready", "rec_ready", "z_part", "z_ready", "zt_ready", "zt_high",
                "zt_low", "o_ready", "x_read", "stats"))
        VU = UH // 2 * 2 * VC

        late = [Weights(nc, held, es, "wd", a["w_d"], held.wd_hi, held.wd_lo, NP_D, PD),
                Weights(nc, held, es, "wc", a["w_c"], held.wc_hi, held.wc_lo, NP_C, PC)]

        with nc.Block() as block:
            @block.sync
            def _(sp):
                for w in late:
                    w.fetch(sp)

            @block.gpsimd
            def _(pool):
                for w in vb:
                    nc.gpsimd.memset(w[:], 0.0).then_inc(vb_clear, 1)
                pool.wait_ge(vb_clear, 2)
                nc.gpsimd.memset(kf[96:128, :], 1.0).then_inc(vb_clear, 1)
                pool.wait_ge(vb_clear, 3)
                for h in range(2):
                    nc.gpsimd.memset(vb[0][64 * h:64 * h + 64, :, h, DL:DL + 1], AS).then_inc(vb_clear, 1)
                pool.wait_ge(vb_clear, 5)
                rstd_all(nc, pool, held, rs_ready)
                for w in late:
                    w.divide(pool)

            @block.vector
            def _(v):
                v.wait_ge(rs_ready, 2)
                v.wait_ge(vb_clear, 5)
                v.sem_inc(sub_ready, 2)
                v.sem_inc(pt_ready, 2)
                v.sem_inc(z_ready, 2)
                v.sem_inc(x_read, 1)
                with v.Fori(0, NC) as c:
                    for i in range(TC):
                        v.wait_ge(tr_ready, TC * c + i + 1)
                        norm_tile(nc, held, xn[:, i % 2, :], TC * c + i).then_inc(xn_ready, 1)
                    v.wait_ge(lat_ready, c + 1)
                    nc.vector.tensor_scalar(kf[0:PR, :], p_x[0:PR, :], held.kq_bias[0:PR, 0:1], AS,
                                            ALU.add, ALU.mult).then_inc(prep, 1)
                    v.wait_ge(prep, PREP * c + 1)
                    nc.vector.tensor_copy(keys[:], kf[0:PR, :]).then_inc(prep, 1)
                    v.wait_ge(prep, PREP * c + 2)
                    nc.vector.tensor_tensor(keys[32:64, :], kf[32:64, :], keys[32:64, :], ALU.subtract).then_inc(prep, 1)
                    v.wait_ge(prep, PREP * c + 3)
                    for h in range(8):
                        nc.vector.tensor_scalar(bd[:, h, :], keys[:], held.mask_a[:, h:h + 1], None,
                                                ALU.mult).then_inc(prep, 1)
                    v.wait_ge(vt_ready, c + 1)
                    for h in range(2):
                        r = slice(64 * h, 64 * h + 64)
                        vt = p_v[r, 0, 0:8 * DL].rearrange("p (b d) -> p b d", d=DL)
                        nc.vector.tensor_copy(vb[0][r, :, h, 0:DL], vt).then_inc(prep, 1)
                        v.wait_ge(prep, PREP * c + 12 + 2 * h)
                        nc.vector.tensor_tensor(vb[1][r, :, h, 0:DL], vt, vb[0][r, :, h, 0:DL],
                                                ALU.subtract).then_inc(prep, 1)
                    for g in range(4):
                        r = slice(64, 96)
                        v.wait_ge(q_high, 4 * c + g + 1)
                        nc.vector.scalar_tensor_tensor(qs[r, g, :], p_s[r, g, :], AS, qs[r, g, :],
                                                       ALU.mult, ALU.subtract).then_inc(prep, 1)

                    def norm_z(j):
                        u, slot, i = NU * c + j, j % 2, j // 2
                        sums = p_v[:, slot, 0:VU].rearrange("p (b s h n) -> p b s h n", s=2, h=2,
                                                                             n=DL + 1)
                        v.wait_ge(v_ready, u + 3)
                        for s in range(2):
                            r = slice(64 * s, 64 * s + 64)
                            nc.vector.reciprocal(rec[r, slot, :].rearrange("p (b h) -> p b h", h=2),
                                                 sums[r, :, s, :, DL]).then_inc(rec_ready, 1)
                        v.wait_ge(rec_ready, 2 * u + 2)
                        for s in range(2):
                            r = slice(64 * s, 64 * s + 64)
                            last = nc.vector.tensor_tensor(
                                z[r, i, UH * slot:UH * slot + UH, :].rearrange("p (b h) n -> p b h n", h=2),
                                sums[r, :, s, :, 0:DL],
                                rec[r, slot, :].rearrange("p (b h a) -> p b h a", h=2, a=1)
                                .broadcast_to([64, UH // 2, 2, DL]), ALU.mult)
                            last.then_inc(z_ready if s else z_part, 1)
                    for j in range(NU):
                        soft_unit(nc, v, (s_ready, top_ready, t_ready, sub_ready), (p_s, top, prob),
                                  NU * c + j, j % 2)
                        if j >= 1:
                            low_pt(nc, v, pt_high, pt_ready, pt, p_t, NU * c + j - 1, (j - 1) % 2)
                        if j >= 2:
                            norm_z(j - 2)
                    low_pt(nc, v, pt_high, pt_ready, pt, p_t, NU * c + NU - 1, (NU - 1) % 2)
                    norm_z(NU - 2)
                    norm_z(NU - 1)
                    v.wait_ge(zt_high, c + 1)
                    nc.vector.scalar_tensor_tensor(zt[1][:], p_x, AS, zt[0][:], ALU.mult,
                                                   ALU.subtract).then_inc(zt_low, 1)
                    for i in range(TC):
                        update_tile(v, nc, held, c, i, o_ready, p_s[:, i, :], AS * WS, x_read, (held.apart, stats))
                v.wait_ge(stats, NC * (2 * TC + 1))

            @block.scalar
            def _(act):
                act.wait_ge(vb_clear, 5)
                with act.Fori(0, NC) as c:
                    for i in range(TC):
                        act.wait_ge(tr_ready, TC * c + i + 3)
                        nc.scalar.activation(xt[:, :, 128 * i:128 * i + 128],
                                             p_s[:, i, :].rearrange("p (k n) -> p k n", k=KB),
                                             ACT.Copy).then_inc(xt_ready, 1)
                    act.wait_ge(lat_ready, c + 1)
                    nc.scalar.activation(kf[96:96 + QL, :], p_x[96:96 + QL, :], ACT.Identity,
                                         bias=held.kq_bias[96:96 + QL, 0:1]).then_inc(cq_ready, 1)
                    for g in range(4):
                        act.wait_ge(q_ready, 4 * c + g + 1)
                        nc.scalar.activation(qs[:, g, :], p_s[0:PR, g, :], ACT.Copy, scale=AS).then_inc(q_high, 1)
                    for j in range(NU):
                        if j:
                            high_pt(nc, act, (t_ready, v_ready, pt_high), pt, p_t, NU * c + j - 1, (j - 1) % 2)
                        exp_unit(nc, act, sub_ready, exp_ready, prob, NU * c + j, j % 2, DL ** -0.5 / (AS * AS))
                    high_pt(nc, act, (t_ready, v_ready, pt_high), pt, p_t, NU * c + NU - 1, (NU - 1) % 2)
                    act.wait_ge(zt_ready, c + 1)
                    nc.scalar.activation(zt[0][:], p_x, ACT.Copy, scale=AS).then_inc(zt_high, 1)

            @block.tensor
            def _(pe):
                pe.sem_inc(tr_ready, 2)
                pe.sem_inc(t_ready, 4)
                pe.sem_inc(v_ready, 2)
                with pe.Fori(0, NC) as c:
                    pe.wait_ge(x_read, TC * c + 1)
                    for i in range(TC):
                        pe.wait_ge(xn_ready, TC * c + i + 1)
                        transpose_tile(nc, held, p_s[:, i, :], xn[:, i % 2, :]).then_inc(tr_ready, 1)
                    pe.wait_ge(xt_ready, TC * c + TC)
                    for k in range(KB):
                        last = nc.tensor.matmul(p_x[0:96 + QL, :], held.wkq[:, k, :], xt[:, k, :],
                                                start=k == 0, stop=k == KB - 1)
                    last.then_inc(lat_ready, 1)
                    pe.wait_ge(cq_ready, c + 1)
                    for g in range(4):
                        nc.tensor.matmul(p_s[0:PR, g, :], held.wqk[96:97 + QL, g, :], kf[96:97 + QL, :],
                                         start=True, stop=True).then_inc(q_ready, 1)
                    pe.wait_ge(prep, PREP * c + 1)
                    for b in range(2 * TC):
                        for h in range(2):
                            last = nc.tensor.matmul(p_v[64 * h:64 * h + 64, 0, DL * b:DL * b + DL],
                                                    kf[0:DL, 64 * b:64 * b + 64], held.ident[0:DL, 0:DL],
                                                    start=True, stop=True)
                    last.then_inc(vt_ready, 1)
                    pe.wait_ge(prep, PREP * c + PREP)

                    def scores(j):
                        u, slot, i = NU * c + j, j % 2, j // 2
                        pe.wait_ge(sub_ready, u + 1)
                        for gi in range(2):
                            for s in range(2):
                                seq = slice(128 * i + 64 * s, 128 * i + 64 * s + 64)
                                last = nc.tensor.matmul(p_s[64 * s:64 * s + 64, 2 * slot + gi, :],
                                                        qs[:, 2 * slot + gi, seq], bd[:, :, seq],
                                                        start=True, stop=True)
                        last.then_inc(s_ready, 1)

                    def attend(j):
                        u, slot, i = NU * c + j, j % 2, j // 2
                        pe.wait_ge(pt_ready, 2 * u + 4)
                        pe.wait_ge(z_ready, u + 1)
                        for b in range(UH // 2):
                            last = mm3(nc, p_v[:, slot, 2 * VC * b:2 * VC * b + 2 * VC],
                                       [w[:, slot, b // 4, 128 * (b % 4):128 * (b % 4) + 128] for w in pt],
                                       [w[:, 2 * i:2 * i + 2, :, :].rearrange("p s h n -> p (s h n)") for w in vb],
                                       True, True)
                        last.then_inc(v_ready, 1)
                    scores(0)
                    scores(1)
                    for j in range(NU):
                        transpose_unit(nc, pe, held, (exp_ready, pt_ready, t_ready), p_t, prob, NU * c + j, j % 2)
                        if j:
                            attend(j - 1)
                        if j + 2 < NU:
                            scores(j + 2)
                    attend(NU - 1)
                    pe.wait_ge(z_ready, NU * c + NU + 2)
                    for i in range(TC):
                        last = nc.tensor.transpose(p_x[:, 128 * i:128 * i + 128],
                                                   z[:, i, :, :].rearrange("p h d -> p (h d)"), held.ident[:])
                    last.then_inc(zt_ready, 1)
                    pe.wait_ge(zt_low, c + 1)
                    for i in range(TC):
                        mm3(nc, p_s[:, i, :], [w[:, 128 * i:128 * i + 128] for w in zt],
                            [w[:] for w in held.wvo], True, False)
                        nc.tensor.matmul(p_s[:, i, :], held.units[:], held.bvo[0][:], start=False, stop=False)
                        nc.tensor.matmul(p_s[:, i, :], held.units[:], held.bvo[1][:], start=False,
                                         stop=True).then_inc(o_ready, 1)


def stage_b(nc, held, a):
    with ExitStack() as es:
        def sb(name, shape, dt=F32):
            return es.enter_context(nc.sbuf_tensor("b_" + name, shape, dt))

        def sem(name):
            return held.sems.enter_context(nc.semaphore("b_" + name))

        def pb(name, shape):
            return es.enter_context(nc.psum_tensor("b_" + name, shape, F32))

        VC = 2 * 2 * (DH + 1)
        xn = sb("xn", [128, 2, D])
        xt = [sb("xt_high", [128, KB, CH], F16), sb("xt_low", [128, KB, CH], F16)]
        kt = sb("kt", [128, KB, CH])
        bd = [sb("bd_high", [128, 2, KB, CH], F16), sb("bd_low", [128, 2, KB, CH], F16)]
        cd = sb("cd", [128, 2 * TC, 128])
        vb = [sb("vb_high", [128, 2 * TC, G8, 2, DH + 1], F16), sb("vb_low", [128, 2 * TC, G8, 2, DH + 1], F16)]
        top = sb("top", [128, 2, UH])
        prob = sb("prob", [128, 2, UH, S])
        pt = [sb("pt_high", [128, 2, 2, D], F16), sb("pt_low", [128, 2, 2, D], F16)]
        rec = sb("rec", [128, 2, UH])
        o = sb("o", [128, 2, KB, 4, 2, DH])
        p_s = pb("p_s", [128, 4, D])
        p_t = pb("p_t", [128, 2, D])
        p_v = pb("p_v", [128, 2, D])
        rs_ready, vb_clear, kt_in, cd_in, vb_ready, xn_ready, tr_ready, hi_ready, xt_ready, bd_high, bd_ready, \
            s_ready, top_ready, sub_ready, exp_ready, t_ready, pt_high, pt_ready, v_ready, rec_ready, o_part, \
            z_ready, x_ready, vb_read, stats = (sem(n) for n in (
                "rs_ready", "vb_clear", "kt_in", "cd_in", "vb_ready", "xn_ready", "tr_ready", "hi_ready",
                "xt_ready", "bd_high", "bd_ready", "s_ready", "top_ready", "sub_ready", "exp_ready", "t_ready",
                "pt_high", "pt_ready", "v_ready", "rec_ready", "o_part", "z_ready", "x_ready", "vb_read",
                "stats"))
        VB = 5
        ctx_b = a["ctx"].rearrange("(b k) n -> k b n", k=S)

        with nc.Block() as block:
            @block.sync
            def _(sp):
                sp.sem_inc(kt_in, 16)
                with sp.Fori(0, NC) as c:
                    sp.wait_ge(bd_ready, 2 * c + 1)
                    for k in range(KB):
                        for g in range(2):
                            for r in range(4):
                                at = 64 * g + 16 * r
                                sp.dma_start(kt[at:at + DH, k, :],
                                             a["ctx_t"][DH * (2 * k + g):DH * (2 * k + g) + DH, bass.ds(CH * c, CH)]
                                             ).then_inc(kt_in, 16)
                    sp.wait_ge(vb_ready, VB * c + 1)
                    for h in range(2):
                        sp.dma_start(cd[64 * h:64 * h + 64, :, :],
                                     ctx_b[:, bass.ds(2 * TC * c, 2 * TC), :]).then_inc(cd_in, 16)

            @block.gpsimd
            def _(pool):
                for w in vb:
                    nc.gpsimd.memset(w[:], 0.0).then_inc(vb_clear, 1)
                pool.wait_ge(vb_clear, 2)
                for h in range(2):
                    nc.gpsimd.memset(vb[0][64 * h:64 * h + 64, :, :, h, DH:DH + 1], AS).then_inc(vb_clear, 1)
                pool.wait_ge(vb_clear, 4)
                rstd_all(nc, pool, held, rs_ready)
                pool.sem_inc(vb_ready, 1)
                with pool.Fori(0, NC) as c:
                    wait_apart(pool, cd_in, 32 * c + 32, held.apart)
                    nc.gpsimd.tensor_scalar(cd[:], cd[:], AS, None, ALU.mult).then_inc(vb_ready, 1)
                    wait_apart(pool, vb_ready, VB * c + 2, held.apart)
                    wait_apart(pool, vb_read, c + 1, held.apart)
                    halves = [(slice(64 * h, 64 * h + 64), h) for h in range(2)]
                    for r, h in halves:
                        nc.gpsimd.tensor_copy(vb[0][r, :, :, h, 0:DH],
                                              cd[r, :, :].rearrange("p b (g d) -> p b g d", g=G8)).then_inc(vb_ready, 1)
                    for r, h in halves:
                        wait_apart(pool, vb_ready, VB * c + 3 + h, held.apart)
                        nc.gpsimd.tensor_tensor(vb[1][r, :, :, h, 0:DH],
                                                cd[r, :, :].rearrange("p b (g d) -> p b g d", g=G8),
                                                vb[0][r, :, :, h, 0:DH], ALU.subtract).then_inc(vb_ready, 1)

            @block.vector
            def _(v):
                v.wait_ge(rs_ready, 2)
                v.sem_inc(sub_ready, 2)
                v.sem_inc(pt_ready, 2)
                v.sem_inc(z_ready, 1)
                v.sem_inc(bd_ready, 1)
                with v.Fori(0, NC) as c:
                    for i in range(TC):
                        v.wait_ge(tr_ready, TC * c + i + 1)
                        norm_tile(nc, held, xn[:, i % 2, :], TC * c + i).then_inc(xn_ready, 1)
                        if i:
                            low(v, nc, c, i - 1, hi_ready, xt_ready, xt, p_s)
                    low(v, nc, c, TC - 1, hi_ready, xt_ready, xt, p_s)
                    for h in range(2):
                        v.wait_ge(bd_high, 2 * c + h + 1)
                        nc.vector.scalar_tensor_tensor(bd[1][:, h, :, :], kt[:], held.mask_bs[:, h:h + 1],
                                                       bd[0][:, h, :, :], ALU.mult, ALU.subtract).then_inc(bd_ready, 1)

                    def norm_o(j):
                        u, slot, i = NU * c + j, j % 2, j // 2
                        v.wait_ge(v_ready, u + 3)
                        for s in range(2):
                            r = slice(64 * s, 64 * s + 64)
                            for q in range(2):
                                sums = p_v[r, q, 0:KB * VC].rearrange("p (k s h n) -> p k s h n", s=2, h=2, n=DH + 1)
                                nc.vector.reciprocal(rec[r, slot, 8 * q:8 * q + 8].rearrange("p (k h) -> p k h", h=2),
                                                     sums[:, :, s, :, DH]).then_inc(rec_ready, 1)
                        v.wait_ge(rec_ready, 4 * u + 4)
                        for s in range(2):
                            r = slice(64 * s, 64 * s + 64)
                            for q in range(2):
                                sums = p_v[r, q, 0:KB * VC].rearrange("p (k s h n) -> p k s h n", s=2, h=2, n=DH + 1)
                                last = nc.vector.tensor_tensor(
                                    o[r, i % 2, :, 2 * slot + q, :, :], sums[:, :, s, :, 0:DH],
                                    rec[r, slot, 8 * q:8 * q + 8].rearrange("p (k h a) -> p k h a", h=2, a=1)
                                    .broadcast_to([64, KB, 2, DH]), ALU.mult)
                                last.then_inc(z_ready if s and q else o_part, 1)

                    def update(i):
                        t = TC * c + i
                        v.wait_ge(z_ready, 2 * t + 3)
                        nc.vector.tensor_tensor(held.X[:, t, :], held.X[:, t, :],
                                                o[:, i % 2, :, :, :, :].rearrange("p k q h d -> p (k q h d)"),
                                                ALU.add).then_inc(x_ready, 1)
                        stats_tile(v, nc, held, c, i, x_ready, t + 1, (held.apart, stats))
                    for j in range(NU):
                        soft_unit(nc, v, (s_ready, top_ready, t_ready, sub_ready), (p_s, top, prob),
                                  NU * c + j, j % 2)
                        if j >= 1:
                            low_pt(nc, v, pt_high, pt_ready, pt, p_t, NU * c + j - 1, (j - 1) % 2)
                        if j >= 2:
                            norm_o(j - 2)
                            if j % 2:
                                update((j - 2) // 2)
                    low_pt(nc, v, pt_high, pt_ready, pt, p_t, NU * c + NU - 1, (NU - 1) % 2)
                    norm_o(NU - 2)
                    norm_o(NU - 1)
                    update(TC - 1)
                v.wait_ge(stats, NC * (2 * TC + 1))

            @block.scalar
            def _(act):
                with act.Fori(0, NC) as c:
                    for i in range(TC):
                        high(act, nc, c, i, tr_ready, hi_ready, xt, p_s)
                    act.wait_ge(kt_in, 16 * 32 * c + 16 * 33)
                    for h in range(2):
                        nc.scalar.activation(bd[0][:, h, :, :], kt[:], ACT.Copy,
                                             scale=held.mask_bs[:, h:h + 1]).then_inc(bd_high, 1)
                    for j in range(NU):
                        if j:
                            high_pt(nc, act, (t_ready, v_ready, pt_high), pt, p_t, NU * c + j - 1, (j - 1) % 2)
                        exp_unit(nc, act, sub_ready, exp_ready, prob, NU * c + j, j % 2, DH ** -0.5 / (XS * AS))
                    high_pt(nc, act, (t_ready, v_ready, pt_high), pt, p_t, NU * c + NU - 1, (NU - 1) % 2)

            @block.tensor
            def _(pe):
                pe.sem_inc(tr_ready, 2)
                pe.sem_inc(t_ready, 4)
                pe.sem_inc(v_ready, 2)
                pe.sem_inc(vb_read, 1)
                with pe.Fori(0, NC) as c:
                    pe.wait_ge(sub_ready, NU * c + 2)
                    for i in range(TC):
                        pe.wait_ge(xn_ready, TC * c + i + 1)
                        transpose_tile(nc, held, p_s[:, i, :], xn[:, i % 2, :]).then_inc(tr_ready, 1)
                    pe.wait_ge(xt_ready, TC * c + TC)
                    pe.wait_ge(bd_ready, 2 * c + 3)

                    def scores(j):
                        u, slot, i = NU * c + j, j % 2, j // 2
                        pe.wait_ge(sub_ready, u + 1)
                        for r in (2 * slot, 2 * slot + 1):
                            nc.tensor.matmul(p_s[:, r, :], held.onehot[:],
                                             held.mk01[:].rearrange("p (a k) -> p a k", a=1).broadcast_to([128, 8, S]),
                                             start=True, stop=False)
                            nc.tensor.matmul(p_s[:, r, :], held.onehot[0:64, :],
                                             held.mk2[:].rearrange("p (a k) -> p a k", a=1).broadcast_to([64, 8, S]),
                                             start=False, stop=False)
                            pair = slice(32 * r, 32 * r + 32)
                            for k in range(KB):
                                for s in range(2):
                                    seq = slice(128 * i + 64 * s, 128 * i + 64 * s + 64)
                                    last = mm3(nc, p_s[64 * s:64 * s + 64, r, 128 * k:128 * k + 128],
                                               [x[pair, k, seq] for x in xt], [x[pair, :, k, seq] for x in bd],
                                               False, k == KB - 1)
                        last.then_inc(s_ready, 1)

                    def attend(j):
                        u, slot, i = NU * c + j, j % 2, j // 2
                        pe.wait_ge(pt_ready, 2 * u + 4)
                        pe.wait_ge(z_ready, u + 1)
                        if j == 0:
                            pe.wait_ge(vb_ready, VB * c + VB + 1)
                        for b in range(UH // 2):
                            q, k = b // KB, b % KB
                            last = mm3(nc, p_v[:, q, VC * k:VC * k + VC],
                                       [w[:, slot, q, 128 * k:128 * k + 128] for w in pt],
                                       [w[:, 2 * i:2 * i + 2, 2 * k + slot, :, :].rearrange("p s h n -> p s (h n)")
                                        for w in vb], True, True)
                        last.then_inc(v_ready, 1)
                        if j == NU - 1:
                            pe.wait_ge(v_ready, u + 3)
                            pe.sem_inc(vb_read, 1)
                    scores(0)
                    scores(1)
                    for j in range(NU):
                        transpose_unit(nc, pe, held, (exp_ready, pt_ready, t_ready), p_t, prob, NU * c + j, j % 2)
                        if j:
                            attend(j - 1)
                        if j + 2 < NU:
                            scores(j + 2)
                    attend(NU - 1)


def stage_c(nc, held, a):
    with ExitStack() as es:
        def sb(name, shape, dt=F32):
            return es.enter_context(nc.sbuf_tensor(name, shape, dt))

        def sem(name):
            return held.sems.enter_context(nc.semaphore("c_" + name))

        def pb(name, shape):
            return es.enter_context(nc.psum_tensor(name, shape, F32))

        xn = sb("c_xn", [128, 2, D])
        xt = [sb("c_xt_high", [128, 2, KB, 128], F16), sb("c_xt_low", [128, 2, KB, 128], F16)]
        logit = sb("c_logit", [128, EX4])
        top = sb("c_top", [128, 2])
        pick = sb("c_pick", [128, EX4])
        zp = sb("c_zp", [128, 2, EX4, R8])
        zt = sb("c_zt", [EX4 * R8, 2, 128])
        p_t = pb("c_p_t", [128, 2, D])
        p_out = pb("c_p_out", [128, 2, D])
        p_aux = pb("c_p_aux", [128, 2, D])
        p_zt = pb("c_p_zt", [128, D])
        rs_ready, xn_ready, t_ready, hi_ready, xt_ready, aux_ready, gated, zp_ready, zt_ready, zt_sb, \
            out_ready, updated, stats = (sem(n) for n in (
                "rs_ready", "xn_ready", "t_ready", "hi_ready", "xt_ready", "aux_ready", "gated", "zp_ready",
                "zt_ready", "zt_sb", "out_ready", "updated", "stats"))
        whl = [w[:, 0:KB * D].rearrange("p (k n) -> p k n", k=KB) for w in (held.wc_hi, held.wc_lo)]
        ghl = [w[:, KB * D:CW].rearrange("p (k n) -> p k n", k=KB) for w in (held.wc_hi, held.wc_lo)]

        with nc.Block() as block:
            @block.gpsimd
            def _(pool):
                rstd_all(nc, pool, held, rs_ready)

            @block.vector
            def _(v):
                v.wait_ge(rs_ready, 2)
                v.sem_inc(xt_ready, 2)
                v.sem_inc(updated, 2)
                v.sem_inc(zp_ready, 2)
                with v.Fori(0, NC) as c:
                    def norm(i):
                        v.wait_ge(t_ready, TC * c + i + 1)
                        norm_tile(nc, held, xn[:, i % 2, :], TC * c + i).then_inc(xn_ready, 1)

                    def low(i):
                        v.wait_ge(hi_ready, TC * c + i + 1)
                        nc.vector.scalar_tensor_tensor(
                            xt[1][:, i % 2, :, :].rearrange("p k n -> p (k n)"), p_t[:, i % 2, :], XS,
                            xt[0][:, i % 2, :, :].rearrange("p k n -> p (k n)"),
                            ALU.mult, ALU.subtract).then_inc(xt_ready, 1)

                    def gate(i):
                        k = 7 * (TC * c + i)
                        v.wait_ge(aux_ready, TC * c + i + 1)
                        nc.vector.scalar_tensor_tensor(logit[:], p_aux[:, i % 2, 0:EX4], 1.0 / (XS * WS),
                                                       held.ebias[:], ALU.mult, ALU.add).then_inc(gated, 1)
                        v.wait_ge(gated, k + 1)
                        nc.vector.tensor_reduce(top[:, 0:1], logit[:], AX.X, ALU.max).then_inc(gated, 1)
                        v.wait_ge(gated, k + 2)
                        nc.vector.tensor_scalar(pick[:], logit[:], top[:, 0:1], None,
                                                ALU.is_equal).then_inc(gated, 1)
                        v.wait_ge(gated, k + 3)
                        nc.vector.tensor_tensor(pick[:], pick[:], held.rank[:], ALU.mult).then_inc(gated, 1)
                        v.wait_ge(gated, k + 4)
                        nc.vector.tensor_reduce(top[:, 1:2], pick[:], AX.X, ALU.max).then_inc(gated, 1)
                        v.wait_ge(gated, k + 5)
                        nc.vector.tensor_scalar(pick[:], pick[:], top[:, 1:2], None,
                                                ALU.is_equal).then_inc(gated, 1)
                        v.wait_ge(gated, k + 6)
                        nc.vector.tensor_copy(zp[:, i % 2, :, :],
                                              p_aux[:, i % 2, EX4:CG].rearrange("p (e r) -> p e r", e=EX4)
                                              ).then_inc(gated, 1)
                        v.wait_ge(gated, k + 7)
                        nc.vector.tensor_tensor(
                            zp[:, i % 2, :, :], zp[:, i % 2, :, :],
                            pick[:].rearrange("p (e b) -> p e b", b=1).broadcast_to([128, EX4, R8]),
                            ALU.mult).then_inc(zp_ready, 1)

                    def update(i):
                        t = TC * c + i
                        v.wait_ge(out_ready, t + 1)
                        nc.vector.scalar_tensor_tensor(held.X[:, t, :], p_out[:, i % 2, :], 1.0 / (XS * WS),
                                                       held.X[:, t, :], ALU.mult, ALU.add).then_inc(updated, 1)
                        stats_tile(v, nc, held, c, i, updated, t + 3, (held.apart, stats))
                    norm(0)
                    for i in range(TC):
                        if i + 1 < TC:
                            norm(i + 1)
                        low(i)
                        gate(i)
                        if i:
                            update(i - 1)
                    update(TC - 1)
                v.wait_ge(stats, NC * (2 * TC + 1))

            @block.scalar
            def _(act):
                with act.Fori(0, NC) as c:
                    def high(i):
                        act.wait_ge(t_ready, TC * c + i + 3)
                        nc.scalar.activation(xt[0][:, i % 2, :, :].rearrange("p k n -> p (k n)"), p_t[:, i % 2, :],
                                             ACT.Copy, scale=XS).then_inc(hi_ready, 1)

                    def zcopy(i):
                        act.wait_ge(zt_ready, TC * c + i + 1)
                        nc.scalar.activation(zt[:, i % 2, :], p_zt[0:EX4 * R8, 0:128], ACT.Copy).then_inc(zt_sb, 1)
                    for i in range(TC):
                        act.wait_ge(updated, TC * c + i + 1)
                        high(i)
                        if i:
                            zcopy(i - 1)
                    zcopy(TC - 1)

            @block.tensor
            def _(pe):
                pe.sem_inc(t_ready, 2)
                with pe.Fori(0, NC) as c:
                    def trans(i):
                        pe.wait_ge(xn_ready, TC * c + i + 1)
                        pe.wait_ge(xt_ready, TC * c + i + 1)
                        transpose_tile(nc, held, p_t[:, i % 2, :], xn[:, i % 2, :]).then_inc(t_ready, 1)

                    def products(i):
                        st = [x[:, i % 2, :, :] for x in xt]
                        pe.wait_ge(xt_ready, TC * c + i + 3)
                        pe.wait_ge(zp_ready, TC * c + i + 1)
                        for k in range(KB):
                            last = mm3(nc, p_aux[:, i % 2, 0:CG], [x[:, k, :] for x in st],
                                       [w[:, k, :] for w in ghl], k == 0, k == KB - 1)
                        last.then_inc(aux_ready, 1)
                        pe.wait_ge(updated, TC * c + i + 1)
                        for k in range(KB):
                            mm3(nc, p_out[:, i % 2, :], [x[:, k, :] for x in st],
                                [w[:, k, :] for w in whl], k == 0, False)

                    def delta(i):
                        pe.wait_ge(zp_ready, TC * c + i + 3)
                        nc.tensor.transpose(p_zt[0:EX4 * R8, 0:128],
                                            zp[:, i % 2, :, :].rearrange("p e r -> p (e r)"),
                                            held.ident[:]).then_inc(zt_ready, 1)
                        pe.wait_ge(zt_sb, TC * c + i + 1)
                        nc.tensor.matmul(p_out[:, i % 2, :], zt[:, i % 2, :], held.lora_b[:], start=False,
                                         stop=True).then_inc(out_ready, 1)
                    trans(0)
                    for i in range(TC):
                        if i + 1 < TC:
                            trans(i + 1)
                        products(i)
                        if i:
                            delta(i - 1)
                    delta(TC - 1)


def stage_d(nc, held, a):
    with ExitStack() as es:
        def sb(name, shape, dt=F32):
            return es.enter_context(nc.sbuf_tensor(name, shape, dt))

        def sem(name):
            return held.sems.enter_context(nc.semaphore("d_" + name))

        NH = 3
        NF = len(FB)
        xn = sb("d_xn", [128, 2, D])
        xt = [sb("d_xt_high", [128, KB, CH], F16), sb("d_xt_low", [128, KB, CH], F16)]
        hid = [sb("d_h_high", [128, NH, CH], F16), sb("d_h_low", [128, NH, CH], F16)]
        term = sb("d_term", [128, 2, CH])
        kept = sb("d_kept", [128, CH])
        delta = sb("d_delta", [128, CH])
        keep = sb("d_keep", [128, CH])
        sg = sb("d_sg", [128, 2, CH])
        hf = sb("d_hf", [128, 2, CH])
        p_up = es.enter_context(nc.psum_tensor("d_p_up", [128, 4, D], F32))
        p_y = es.enter_context(nc.psum_tensor("d_p_y", [128, TC, D], F32))
        rs_ready, xn_ready, t_ready, hi_ready, xt_ready, up_ready, terms_in, sg_ready, keep_ready, val_ready, \
            hh_ready, h_ready, down_done, y_ready, y_read, stats = (sem(n) for n in (
                "rs_ready", "xn_ready", "t_ready", "hi_ready", "xt_ready", "up_ready", "terms_in", "sg_ready",
                "keep_ready", "val_ready", "hh_ready", "h_ready", "down_done", "y_ready", "y_read", "stats"))
        NU = 1 + NF
        NV = DND - 1
        up_w = [w[:, 0:KB * UPD].rearrange("p (k n) -> p k n", k=KB) for w in (held.wd_hi, held.wd_lo)]
        dn_w = [w[:, KB * UPD:DW].rearrange("p (b n) -> p b n", b=DND) for w in (held.wd_hi, held.wd_lo)]
        rows = [128] * (G6 + 1) + [n for _, n in FB]

        late = Weights(nc, held, es, "wf", a["w_f"], held.wf_hi, held.wf_lo, NP_F, PF)

        with nc.Block() as block:
            @block.sync
            def _(sp):
                late.fetch(sp)

            @block.gpsimd
            def _(pool):
                rstd_all(nc, pool, held, rs_ready)
                late.divide(pool)

            @block.vector
            def _(v):
                v.wait_ge(rs_ready, 2)
                v.sem_inc(val_ready, 1)
                v.sem_inc(y_read, 1)

                def prepare(c):
                    for i in range(TC):
                        v.wait_ge(t_ready, TC * c + i + 1)
                        norm_tile(nc, held, xn[:, i % 2, :], TC * c + i).then_inc(xn_ready, 1)
                        if i:
                            low(v, nc, c, i - 1, hi_ready, xt_ready, xt, p_up)
                    low(v, nc, c, TC - 1, hi_ready, xt_ready, xt, p_up)

                def values(c):
                    v.wait_ge(terms_in, 2 * c + 2)
                    nc.vector.tensor_scalar(keep[:], delta[:], 2.5, None, ALU.is_le).then_inc(keep_ready, 1)
                    v.wait_ge(keep_ready, 3 * c + 1)
                    nc.vector.scalar_tensor_tensor(keep[:], delta[:], -2.5, keep[:], ALU.is_ge,
                                                   ALU.mult).then_inc(keep_ready, 1)
                    for d in range(DND):
                        n = rows[d]
                        if d == 0:
                            value = term[:, 0, :]
                        elif d <= G6:
                            before = term[:, (d - 1) % 2, :]
                            if d > 1:
                                v.wait_ge(val_ready, NV * c + d)
                            if d == 5:
                                v.wait_ge(keep_ready, 3 * c + 2)
                                nc.vector.tensor_tensor(kept[:], before, keep[:], ALU.mult).then_inc(keep_ready, 1)
                                v.wait_ge(keep_ready, 3 * c + 3)
                                before = kept[:]
                            value = term[:, d % 2, :]
                            nc.vector.scalar_tensor_tensor(value, before, held.growth[:, d - 1:d], delta[:],
                                                           ALU.mult, ALU.mult).then_inc(val_ready, 1)
                        else:
                            j = d - G6
                            value = hf[0:n, d % 2, :]
                            v.wait_ge(sg_ready, NF * c + j)
                            nc.vector.scalar_tensor_tensor(value, p_up[0:n, 2 * (j % 2) + 1, :], HS / (XS * WS),
                                                           sg[0:n, d % 2, :], ALU.mult, ALU.mult).then_inc(val_ready, 1)
                        v.wait_ge(hh_ready, DND * c + d + 1)
                        nc.vector.tensor_tensor(hid[1][0:n, d % NH, :], value, hid[0][0:n, d % NH, :],
                                                ALU.subtract).then_inc(h_ready, 1)

                def update(c):
                    for i in range(TC):
                        update_tile(v, nc, held, c, i, y_ready, p_y[:, i, :], HS * WS, y_read, (held.apart, stats))
                prepare(0)
                with v.Fori(0, NC - 1) as c:
                    values(c)
                    prepare(c + 1)
                    update(c)
                values(NC - 1)
                update(NC - 1)
                v.wait_ge(stats, NC * (2 * TC + 1))

            @block.scalar
            def _(act):
                def prepare(c):
                    for i in range(TC):
                        high(act, nc, c, i, t_ready, hi_ready, xt, p_up)

                def values(c):
                    act.wait_ge(up_ready, NU * c + 1)
                    nc.scalar.activation(term[:, 0, :], p_up[:, 0, :], ACT.Copy,
                                         scale=HS / (XS * WS)).then_inc(terms_in, 1)
                    nc.scalar.activation(delta[:], p_up[:, 1, :], ACT.Identity, bias=held.nlp[:, 0:1],
                                         scale=1.0 / (XS * WS)).then_inc(terms_in, 1)
                    for d in range(DND):
                        n = rows[d]
                        j = d - G6
                        if j == 0:
                            silu(act, nc, c, 1, FB[0][1], up_ready, sg_ready, sg, p_up, val_ready)
                        if j >= 1 and j < NF:
                            silu(act, nc, c, j + 1, FB[j][1], up_ready, sg_ready, sg, p_up, val_ready)
                        if d == 0:
                            act.wait_ge(terms_in, 2 * c + 1)
                            value = term[:, 0, :]
                        else:
                            act.wait_ge(val_ready, NV * c + d + 1)
                            value = term[:, d % 2, :] if d <= G6 else hf[0:n, d % 2, :]
                        act.wait_ge(down_done, DND * c + (NH if d < NH else d + 1))
                        nc.scalar.activation(hid[0][0:n, d % NH, :], value, ACT.Copy).then_inc(hh_ready, 1)
                prepare(0)
                with act.Fori(0, NC - 1) as c:
                    values(c)
                    prepare(c + 1)
                values(NC - 1)

            @block.tensor
            def _(pe):
                pe.sem_inc(t_ready, 2)
                pe.sem_inc(down_done, NH)

                def turn(c):
                    pe.wait_ge(val_ready, NV * c + 1)
                    for i in range(TC):
                        pe.wait_ge(xn_ready, TC * c + i + 1)
                        transpose_tile(nc, held, p_up[:, i, :], xn[:, i % 2, :]).then_inc(t_ready, 1)

                def up(c, j):
                    slot = 2 * (j % 2)
                    if j == 2:
                        pe.wait_ge(terms_in, 2 * c + 2)
                    if j > 2:
                        pe.wait_ge(val_ready, NV * c + G6 + j - 1)
                    at, n = (0, SD) if j == 0 else (2 * SD + FB[j - 1][0], FB[j - 1][1])
                    step = SD if j == 0 else FD
                    for half in range(2):
                        cols = slice(at + half * step, at + half * step + n)
                        for k in range(KB):
                            last = mm3(nc, p_up[0:n, slot + half, :], [w[:, k, cols] for w in up_w],
                                       [x[:, k, :] for x in xt], k == 0, k == KB - 1)
                    last.then_inc(up_ready, 1)

                def down(c, d):
                    n = rows[d]
                    pe.wait_ge(h_ready, DND * c + d + 1)
                    if d == 0:
                        pe.wait_ge(y_read, TC * c + 1)
                    for i in range(TC):
                        last = mm3(nc, p_y[:, i, :], [h[0:n, d % NH, 128 * i:128 * i + 128] for h in hid],
                                   [w[0:n, d, :] for w in dn_w], d == 0, d == DND - 1)
                        if d == DND - 1:
                            last.then_inc(y_ready, 1)
                    if d < DND - 1:
                        last.then_inc(down_done, 1)

                def products(c, more):
                    pe.wait_ge(xt_ready, TC * c + TC)
                    for j in range(3):
                        up(c, j)
                    for d in range(G6 + 1):
                        down(c, d)
                    for j in range(3, NU):
                        up(c, j)
                        down(c, G6 + j - 2)
                    down(c, DND - 2)
                    if more:
                        turn(c + 1)
                    down(c, DND - 1)
                    pe.wait_ge(y_ready, TC * c + TC)
                    pe.sem_inc(down_done, 1)
                turn(0)
                with pe.Fori(0, NC - 1) as c:
                    products(c, True)
                products(NC - 1, False)


def stage_e(nc, held, a):
    M = 128
    with ExitStack() as es:
        def sb(name, shape, dt=F32):
            return es.enter_context(nc.sbuf_tensor("e_" + name, shape, dt))

        def sem(name):
            return held.sems.enter_context(nc.semaphore("e_" + name))

        def pb(name, shape):
            return es.enter_context(nc.psum_tensor("e_" + name, shape, F32))

        NJ = 2 * KB
        wq = sb("wq", [S, S])
        wk = sb("wk", [S, S])
        wv = sb("wv", [128, 128])
        wskip = sb("wskip", [128, 128])
        wkq = sb("wkq", [128, 128])
        ctx = sb("ctx", [128, TC, M])
        xn = sb("xn", [128, 2, D])
        keys = sb("keys", [128, 2, 2, M])
        vt = sb("vt", [M, 2, 2, S])
        prob = sb("prob", [128, 2, NJ, M])
        top = sb("top", [128, 2, NJ])
        den = sb("den", [128, 2, NJ])
        pt = sb("pt", [M, 2, 2, D])
        p_s = pb("p_s", [128, 2, 2 * D])
        p_t = pb("p_t", [128, 2, D])
        p_o = pb("p_o", [128, D])
        p_m = pb("p_m", [128, D])
        w_in, clear, wkq_ready, wkq_in, rs_ready, ctx_in, ctx_read, xn_ready, m_ready, keys_ready, s_ready, \
            top_ready, sub_ready, exp_ready, den_ready, prob_ready, t_ready, pt0_ready, pt1_ready, o_ready, \
            o_read, stats = (sem(n) for n in (
                "w_in", "clear", "wkq_ready", "wkq_in", "rs_ready", "ctx_in", "ctx_read", "xn_ready", "m_ready",
                "keys_ready", "s_ready", "top_ready", "sub_ready", "exp_ready", "den_ready", "prob_ready",
                "t_ready", "pt0_ready", "pt1_ready", "o_ready", "o_read", "stats"))
        ctx_d = a["ctx"].rearrange("(t p) n -> p t n", p=128)

        with nc.Block() as block:
            @block.sync
            def _(sp):
                sp.dma_start(wq[:], a["Wq"]).then_inc(w_in, 16)
                sp.dma_start(wk[:], a["Wk"]).then_inc(w_in, 16)
                sp.wait_ge(clear, 2)
                for s in range(2):
                    half = slice(64 * s, 64 * s + 64)
                    sp.dma_start(wskip[half, half], a["WskipT"]).then_inc(w_in, 16)
                    sp.dma_start(wv[half, half], a["WvT"]).then_inc(w_in, 16)
                with sp.Fori(0, NC) as c:
                    sp.wait_ge(ctx_read, c + 1)
                    sp.dma_start(ctx[:], ctx_d[:, bass.ds(TC * c, TC), :]).then_inc(ctx_in, 16)

            @block.gpsimd
            def _(pool):
                nc.gpsimd.memset(wskip[:], 0.0).then_inc(clear, 1)
                nc.gpsimd.memset(wv[:], 0.0).then_inc(clear, 1)
                rstd_all(nc, pool, held, rs_ready)
                with pool.Fori(0, NC) as c:
                    for i in range(TC):
                        b, t = i % 2, TC * c + i
                        pool.wait_ge(den_ready, 2 * t + 2)
                        nc.gpsimd.tensor_tensor(
                            prob[:, b, :, :], prob[:, b, :, :],
                            den[:, b, :].rearrange("p (j a) -> p j a", a=1).broadcast_to([128, NJ, M]),
                            ALU.mult).then_inc(prob_ready, 1)

            @block.vector
            def _(v):
                nc.vector.memset(wkq[:], 0.0).then_inc(wkq_in, 1)
                nc.vector.memset(keys[:], 0.0).then_inc(wkq_in, 1)
                v.wait_ge(wkq_in, 2)
                v.wait_ge(wkq_ready, 1)
                for s in range(2):
                    half = slice(64 * s, 64 * s + 64)
                    nc.vector.tensor_copy(wkq[half, half], p_m[half, half]).then_inc(wkq_in, 1)
                v.wait_ge(rs_ready, 2)
                v.sem_inc(sub_ready, 2)
                v.sem_inc(pt1_ready, 1)
                v.sem_inc(o_read, 1)
                with v.Fori(0, NC) as c:
                    def norm(i):
                        t = TC * c + i
                        v.wait_ge(o_ready, t + 1)
                        norm_tile(nc, held, xn[:, i % 2, :], t).then_inc(xn_ready, 1)

                    def soft(i):
                        b, t = i % 2, TC * c + i
                        scores = p_s[:, b, :].rearrange("p (j m) -> p j m", j=NJ)
                        v.wait_ge(s_ready, t + 1)
                        nc.vector.tensor_reduce(top[:, b, :], scores, AX.X, ALU.max).then_inc(top_ready, 1)
                        v.wait_ge(top_ready, t + 1)
                        v.wait_ge(t_ready, t + 1)
                        nc.vector.tensor_tensor(
                            prob[:, b, :, :], scores,
                            top[:, b, :].rearrange("p (j a) -> p j a", a=1).broadcast_to([128, NJ, M]),
                            ALU.subtract).then_inc(sub_ready, 1)

                    def total(i):
                        b, t = i % 2, TC * c + i
                        v.wait_ge(exp_ready, t + 1)
                        nc.vector.tensor_reduce(den[:, b, :], prob[:, b, :, :], AX.X, ALU.add).then_inc(den_ready, 1)
                        v.wait_ge(den_ready, 2 * t + 1)
                        nc.vector.reciprocal(den[:, b, :], den[:, b, :]).then_inc(den_ready, 1)

                    def values(i):
                        t = TC * c + i
                        v.wait_ge(t_ready, t + 3)
                        v.wait_ge(o_ready, t + 1)
                        nc.vector.tensor_copy(pt[:, i % 2, 1, :], p_t[:, 1, :]).then_inc(pt1_ready, 1)

                    def update(i):
                        t = TC * c + i
                        v.wait_ge(o_ready, t + 3)
                        nc.vector.tensor_tensor(held.X[:, t, :], p_o[:], held.X[:, t, :], ALU.add).then_inc(o_read, 1)
                        stats_tile(v, nc, held, c, i, o_read, t + 2, (held.apart, stats))
                    norm(0)
                    soft(0)
                    for i in range(TC):
                        if i + 1 < TC:
                            if i:
                                update(i - 1)
                            norm(i + 1)
                            total(i)
                            soft(i + 1)
                        else:
                            update(i - 1)
                            total(i)
                        values(i)
                    update(TC - 1)
                v.wait_ge(stats, NC * (2 * TC + 1))

            @block.scalar
            def _(act):
                act.wait_ge(wkq_in, 4)
                act.sem_inc(keys_ready, 4)
                act.sem_inc(pt0_ready, 1)
                with act.Fori(0, NC) as c:
                    def keys_in(i):
                        b, t = i % 2, TC * c + i
                        act.wait_ge(m_ready, t + 1)
                        act.wait_ge(o_ready, t + 1)
                        for s in range(2):
                            half = slice(64 * s, 64 * s + 64)
                            nc.scalar.activation(keys[half, b, s, :], p_m[half, 0:M], ACT.Copy)
                        nc.scalar.activation(vt[:, b, :, :], p_m[:, M:2 * M].rearrange("p (s n) -> p s n", s=2),
                                             ACT.Copy).then_inc(keys_ready, 1)

                    def expo(i):
                        b, t = i % 2, TC * c + i
                        act.wait_ge(sub_ready, t + 3)
                        nc.scalar.activation(prob[:, b, :, :], prob[:, b, :, :], ACT.Exp,
                                             scale=S ** -0.5).then_inc(exp_ready, 1)

                    def values(i):
                        t = TC * c + i
                        act.wait_ge(t_ready, t + 3)
                        act.wait_ge(o_ready, t + 1)
                        nc.scalar.activation(pt[:, i % 2, 0, :], p_t[:, 0, :], ACT.Copy).then_inc(pt0_ready, 1)
                    keys_in(0)
                    expo(0)
                    for i in range(TC):
                        if i + 1 < TC:
                            keys_in(i + 1)
                            expo(i + 1)
                        values(i)

            @block.tensor
            def _(pe):
                pe.wait_ge(w_in, 96)
                for s in range(2):
                    half = slice(64 * s, 64 * s + 64)
                    last = nc.tensor.matmul(p_m[half, half], wk[:], wq[:], start=True, stop=True)
                last.then_inc(wkq_ready, 1)
                pe.wait_ge(wkq_in, 4)
                pe.sem_inc(o_ready, 2)
                pe.sem_inc(t_ready, 2)
                pe.sem_inc(ctx_read, 1)
                pe.wait_ge(keys_ready, 4)
                with pe.Fori(0, NC) as c:
                    def make_keys(i):
                        t = TC * c + i
                        if i == 0:
                            pe.wait_ge(ctx_in, 16 * c + 16)
                        pe.wait_ge(keys_ready, t + 4)
                        nc.tensor.matmul(p_m[:, 0:M], wkq[:], ctx[:, i, :], start=True, stop=True)
                        nc.tensor.matmul(p_m[:, M:2 * M], ctx[:, i, :], wv[:], start=True,
                                         stop=True).then_inc(m_ready, 1)
                        if i == TC - 1:
                            pe.wait_ge(m_ready, t + 1)
                            pe.sem_inc(ctx_read, 1)

                    def scores(i):
                        b, t = i % 2, TC * c + i
                        pe.wait_ge(xn_ready, t + 1)
                        pe.wait_ge(keys_ready, t + 5)
                        pe.wait_ge(sub_ready, t + 1)
                        for k in range(KB):
                            last = nc.tensor.matmul(p_s[:, b, 256 * k:256 * k + 256], xn[:, b, 128 * k:128 * k + 128],
                                                    keys[:, b, :, :].rearrange("p s m -> p (s m)"),
                                                    start=True, stop=True)
                        last.then_inc(s_ready, 1)

                    def transposes(i):
                        b, t = i % 2, TC * c + i
                        pe.wait_ge(prob_ready, t + 1)
                        pe.wait_ge(pt1_ready, t + 1)
                        pe.wait_ge(pt0_ready, t + 1)
                        for s in range(2):
                            for k in range(KB):
                                last = nc.tensor.transpose(p_t[:, s, 128 * k:128 * k + 128], prob[:, b, 2 * k + s, :],
                                                           held.ident[:])
                        last.then_inc(t_ready, 1)

                    def output(i):
                        b, t = i % 2, TC * c + i
                        pe.wait_ge(o_read, t + 1)
                        nc.tensor.matmul(p_o[:], wskip[:], xn[:, b, :], start=True, stop=False)
                        pe.wait_ge(pt0_ready, t + 2)
                        pe.wait_ge(pt1_ready, t + 2)
                        for s in range(2):
                            half = slice(64 * s, 64 * s + 64)
                            last = nc.tensor.matmul(p_o[half, :], vt[:, b, s, :], pt[:, b, s, :], start=False,
                                                    stop=True)
                        last.then_inc(o_ready, 1)
                    make_keys(0)
                    scores(0)
                    for i in range(TC):
                        if i + 1 < TC:
                            make_keys(i + 1)
                            scores(i + 1)
                        transposes(i)
                        output(i)


def stage_f(nc, held, a, out):
    with ExitStack() as es:
        def sb(name, shape, dt=F32):
            return es.enter_context(nc.sbuf_tensor("f_" + name, shape, dt))

        def sem(name):
            return held.sems.enter_context(nc.semaphore("f_" + name))

        NH = 3
        xn = sb("xn", [128, 2, D])
        xt = [sb("xt_high", [128, KB, CH], F16), sb("xt_low", [128, KB, CH], F16)]
        lat = [sb("lat_high", [128, FL, CH], F16), sb("lat_low", [128, FL, CH], F16)]
        hid = [sb("h_high", [128, NH, CH], F16), sb("h_low", [128, NH, CH], F16)]
        w2 = [sb("w2_high", [128, FL, D], F16), sb("w2_low", [128, FL, D], F16)]
        relu = sb("relu", [128, 2, CH])
        sq = sb("sq", [128, 2, CH])
        routed = sb("routed", [128, TC, D])
        top8 = sb("top8", [128, TC, NE])
        route = sb("route", [128, TC])
        y = sb("y", [128, TC, D])
        fc2, expert_t = y[:, 0:FL, :], y[:, FL, :].rearrange("p (k n) -> p k n", k=FL)
        yst = sb("yst", [128, TC, 6])
        ymv = sb("ymv", [128, TC, 2])
        yve = sb("yve", [128, TC])
        yrs = sb("yrs", [128, TC])
        p_up = es.enter_context(nc.psum_tensor("f_p_up", [128, 4, D], F32))
        p_y = es.enter_context(nc.psum_tensor("f_p_y", [128, TC, D], F32))
        rs_ready, w2_in, w2_ready, w2_split, xn_ready, t_ready, hi_ready, xt_ready, logit_ready, route_ready, \
            lat_ready, lat_hi, lat_lo, r_ready, r_read, up_ready, relu_ready, sq_ready, hh_ready, h_ready, \
            down_done, y_ready, y_read, y_steps, yrs_ready, normed, scaled, final = (sem(n) for n in (
                "rs_ready", "w2_in", "w2_ready", "w2_split", "xn_ready", "t_ready", "hi_ready", "xt_ready",
                "logit_ready", "route_ready", "lat_ready", "lat_hi", "lat_lo", "r_ready", "r_read", "up_ready",
                "relu_ready", "sq_ready", "hh_ready", "h_ready", "down_done", "y_ready", "y_read", "y_steps",
                "yrs_ready", "normed", "scaled", "final"))
        stored = [sem(f"stored_{b}") for b in range(2)]
        up_w = [w[:, 0:KB * FC].rearrange("p (k n) -> p k n", k=KB) for w in (held.wf_hi, held.wf_lo)]
        dn_w = [w[:, KB * FC:FW].rearrange("p (b n) -> p b n", b=FU) for w in (held.wf_hi, held.wf_lo)]
        out_t = out.rearrange("(t p) n -> p t n", p=128)

        with nc.Block() as block:
            @block.sync
            def _(sp):
                sp.dma_start(expert_t, a["expertT"].rearrange("(k p) n -> p k n", p=128)).then_inc(w2_in, 16)
                sp.dma_start(fc2, a["fc2"].rearrange("(k p) n -> p k n", p=128)).then_inc(w2_in, 16)
                with sp.Fori(0, NC) as c:
                    for i in range(TC):
                        sp.wait_ge(final, TC * c + i + 1)
                        sp.dma_start(out_t[:, TC * c + i, :], y[:, i, :]).then_inc(stored[i % 2], 16)
                for b in range(2):
                    sp.wait_ge(stored[b], 16 * (NT // 2) + 16)

            @block.gpsimd
            def _(pool):
                rstd_all(nc, pool, held, rs_ready)
                for b in range(2):
                    pool.sem_inc(stored[b], 16)
                with pool.Fori(0, NC) as c:
                    wait_apart(pool, y_steps, 2 * TC * c + 2 * TC, held.apart)
                    nc.gpsimd.tensor_scalar(yve[:], ymv[:, :, 1], EPS, None, ALU.add).then_inc(yrs_ready, 1)
                    wait_apart(pool, yrs_ready, 2 * c + 1, held.apart)
                    nc.gpsimd.tensor_tensor(yrs[:], yve[:], held.mhalf[:, 0:TC], ALU.pow).then_inc(yrs_ready, 1)
                    for i in range(TC):
                        t = TC * c + i
                        wait_apart(pool, normed, t + 1, held.apart)
                        nc.gpsimd.tensor_tensor(y[:, i, :], y[:, i, :], held.gam[:], ALU.mult).then_inc(scaled, 1)
                        wait_apart(pool, scaled, 2 * t + 1, held.apart)
                        nc.gpsimd.tensor_tensor(y[:, i, :], y[:, i, :], held.bet[:], ALU.add).then_inc(scaled, 1)
                        wait_apart(pool, scaled, 2 * t + 2, held.apart)
                        nc.gpsimd.tensor_tensor(y[:, i, :], y[:, i, :], held.X[:, t, :], ALU.add).then_inc(final, 1)

            @block.vector
            def _(v):
                for k in range(FL):
                    v.wait_ge(w2_ready, k + 1)
                    nc.vector.tensor_scalar(w2[0][:, k, :], p_y[:, k, :], WS, None, ALU.mult).then_inc(w2_split, 1)
                    v.wait_ge(w2_split, 2 * k + 1)
                    nc.vector.scalar_tensor_tensor(w2[1][:, k, :], p_y[:, k, :], WS, w2[0][:, k, :],
                                                   ALU.mult, ALU.subtract).then_inc(w2_split, 1)
                v.wait_ge(rs_ready, 2)
                v.sem_inc(sq_ready, 1)
                v.sem_inc(y_read, 1)

                def prepare(c):
                    for i in range(TC):
                        v.wait_ge(t_ready, TC * c + i + 1)
                        norm_tile(nc, held, xn[:, i % 2, :], TC * c + i).then_inc(xn_ready, 1)
                        if i:
                            low(v, nc, c, i - 1, hi_ready, xt_ready, xt, p_up)
                    low(v, nc, c, TC - 1, hi_ready, xt_ready, xt, p_up)

                def front(c):
                    wait_apart(v, logit_ready, c + 1, held.apart)
                    for i in range(TC):
                        nc.vector.max(top8[:, i, :], p_up[:, 0, NE * i:NE * i + NE]).then_inc(route_ready, 1)
                    v.wait_ge(route_ready, (TC + 2) * c + TC)
                    nc.vector.tensor_tensor(route[:], top8[:, :, 0], top8[:, :, 1], ALU.add).then_inc(route_ready, 1)
                    v.wait_ge(route_ready, (TC + 2) * c + TC + 1)
                    nc.vector.tensor_scalar(route[:], route[:], 1.0 / (XS * WS * AS * WS), None,
                                            ALU.mult).then_inc(route_ready, 1)
                    for l in range(FL):
                        v.wait_ge(lat_hi, FL * c + l + 1)
                        nc.vector.scalar_tensor_tensor(lat[1][:, l, :], p_up[:, 1 + l, :], AS / (XS * WS),
                                                       lat[0][:, l, :], ALU.mult, ALU.subtract).then_inc(lat_lo, 1)

                def blocks(c):
                    for f in range(FU):
                        v.wait_ge(relu_ready, FU * c + f + 1)
                        nc.vector.tensor_tensor(sq[:, f % 2, :], relu[:, f % 2, :], relu[:, f % 2, :],
                                                ALU.mult).then_inc(sq_ready, 1)
                        v.wait_ge(hh_ready, FU * c + f + 1)
                        nc.vector.tensor_tensor(hid[1][:, f % NH, :], sq[:, f % 2, :], hid[0][:, f % NH, :],
                                                ALU.subtract).then_inc(h_ready, 1)

                def add_routed(c):
                    for i in range(TC):
                        t = TC * c + i
                        v.wait_ge(y_ready, t + 1)
                        v.wait_ge(r_read, t + 1)
                        v.wait_ge(stored[i % 2], 16 * (TC // 2) * c + 16)
                        nc.vector.scalar_tensor_tensor(y[:, i, :], p_y[:, i, :], 1.0 / (FS * WS), routed[:, i, :],
                                                       ALU.mult, ALU.add).then_inc(y_read, 1)

                def norm_out(c):
                    for i in range(TC):
                        wait_apart(v, y_read, TC * c + i + 2, held.apart)
                        nc.vector.bn_stats(yst[:, i, :], y[:, i, :]).then_inc(y_steps, 1)
                    for i in range(TC):
                        wait_apart(v, y_steps, 2 * TC * c + TC + i, held.apart)
                        nc.vector.bn_aggr(ymv[:, i, :], yst[:, i, :]).then_inc(y_steps, 1)
                    v.wait_ge(yrs_ready, 2 * c + 2)
                    for i in range(TC):
                        nc.vector.tensor_scalar(y[:, i, :], y[:, i, :], ymv[:, i, 0:1], yrs[:, i:i + 1],
                                                ALU.subtract, ALU.mult).then_inc(normed, 1)
                prepare(0)
                front(0)
                with v.Fori(0, NC - 1) as c:
                    blocks(c)
                    prepare(c + 1)
                    add_routed(c)
                    front(c + 1)
                    norm_out(c)
                blocks(NC - 1)
                add_routed(NC - 1)
                norm_out(NC - 1)

            @block.scalar
            def _(act):
                def front(c):
                    for i in range(TC):
                        high(act, nc, c, i, t_ready, hi_ready, xt, p_up)
                    for l in range(FL):
                        act.wait_ge(lat_ready, FL * c + l + 1)
                        nc.scalar.activation(lat[0][:, l, :], p_up[:, 1 + l, :], ACT.Copy,
                                             scale=AS / (XS * WS)).then_inc(lat_hi, 1)
                    act.wait_ge(route_ready, (TC + 2) * c + TC + 2)
                    for i in range(TC):
                        act.wait_ge(r_ready, TC * c + i + 1)
                        nc.scalar.activation(routed[:, i, :], p_y[:, i, :], ACT.Copy,
                                             scale=route[:, i:i + 1]).then_inc(r_read, 1)

                def blocks(c):
                    for f in range(FU + 1):
                        if f < FU:
                            act.wait_ge(up_ready, FU * c + f + 1)
                            act.wait_ge(sq_ready, FU * c + (f if f >= 2 else 1))
                            nc.scalar.activation(relu[:, f % 2, :], p_up[:, f % 4, :], ACT.Relu,
                                                 scale=FS ** 0.5 / (XS * WS)).then_inc(relu_ready, 1)
                        if f:
                            g = f - 1
                            act.wait_ge(sq_ready, FU * c + g + 2)
                            act.wait_ge(down_done, FU * c + (NH if g < NH else g + 1))
                            nc.scalar.activation(hid[0][:, g % NH, :], sq[:, g % 2, :], ACT.Copy).then_inc(hh_ready, 1)
                front(0)
                with act.Fori(0, NC - 1) as c:
                    blocks(c)
                    front(c + 1)
                blocks(NC - 1)

            @block.tensor
            def _(pe):
                pe.wait_ge(w2_in, 32)
                for l in range(FL):
                    for k in range(FL):
                        last = nc.tensor.matmul(p_y[:, l, :], expert_t[:, k, 128 * l:128 * l + 128], fc2[:, k, :],
                                                start=k == 0, stop=k == FL - 1)
                    last.then_inc(w2_ready, 1)
                pe.wait_ge(w2_split, 2 * FL)
                pe.sem_inc(t_ready, 2)
                pe.sem_inc(down_done, NH)

                def turn(c):
                    pe.wait_ge(sq_ready, FU * c + 1)
                    for i in range(TC):
                        pe.wait_ge(xn_ready, TC * c + i + 1)
                        transpose_tile(nc, held, p_up[:, i, :], xn[:, i % 2, :]).then_inc(t_ready, 1)

                def front(c):
                    pe.wait_ge(xt_ready, TC * c + TC)
                    for i in range(TC):
                        for k in range(KB):
                            last = mm3(nc, p_up[:, 0, NE * i:NE * i + NE],
                                       [x[:, k, 128 * i:128 * i + 128] for x in xt],
                                       [w[:, k, INT + LAT:FC] for w in up_w], k == 0, k == KB - 1)
                    last.then_inc(logit_ready, 1)
                    for l in range(FL):
                        for k in range(KB):
                            last = mm3(nc, p_up[:, 1 + l, :], [w[:, k, INT + 128 * l:INT + 128 * l + 128] for w in up_w],
                                       [x[:, k, :] for x in xt], k == 0, k == KB - 1)
                        last.then_inc(lat_ready, 1)
                    up(c, 0)
                    pe.wait_ge(lat_lo, FL * c + FL)
                    pe.wait_ge(y_read, TC * c + 1)
                    for i in range(TC):
                        for l in range(FL):
                            last = mm3(nc, p_y[:, i, :], [x[:, l, 128 * i:128 * i + 128] for x in lat],
                                       [w[:, l, :] for w in w2], l == 0, l == FL - 1)
                        last.then_inc(r_ready, 1)

                def up(c, f):
                    if f == 0:
                        pe.wait_ge(route_ready, (TC + 2) * c + TC)
                    elif f <= 2:
                        pe.wait_ge(lat_lo, FL * c + f)
                    elif f >= 4:
                        pe.wait_ge(sq_ready, FU * c + f - 2)
                    for k in range(KB):
                        last = mm3(nc, p_up[:, f % 4, :], [w[:, k, 128 * f:128 * f + 128] for w in up_w],
                                   [x[:, k, :] for x in xt], k == 0, k == KB - 1)
                    last.then_inc(up_ready, 1)

                def down(c, f):
                    pe.wait_ge(h_ready, FU * c + f + 1)
                    if f == 0:
                        pe.wait_ge(r_read, TC * c + TC)
                    for i in range(TC):
                        last = mm3(nc, p_y[:, i, :], [h[:, f % NH, 128 * i:128 * i + 128] for h in hid],
                                   [w[:, f, :] for w in dn_w], f == 0, f == FU - 1)
                        if f == FU - 1:
                            last.then_inc(y_ready, 1)
                    if f < FU - 1:
                        last.then_inc(down_done, 1)

                def blocks(c, more):
                    up(c, 1)
                    for f in range(2, FU):
                        up(c, f)
                        down(c, f - 2)
                    down(c, FU - 2)
                    if more:
                        turn(c + 1)
                    down(c, FU - 1)
                    pe.wait_ge(y_ready, TC * c + TC)
                    pe.sem_inc(down_done, 1)
                turn(0)
                front(0)
                with pe.Fori(0, NC - 1) as c:
                    blocks(c, True)
                    front(c + 1)
                blocks(NC - 1, False)


STAGES = "ABCDEF"


def build(nc, a, out):
    held = Held()
    with ExitStack() as es:
        def sb(name, shape, dt=F32):
            return es.enter_context(nc.sbuf_tensor(name, shape, dt))

        held.sems = es
        held.apart = es.enter_context(nc.semaphore("apart"))
        held.X = sb("X", [128, NT, D])
        held.mv = sb("mv", [128, NT, 2])
        held.st = sb("st", [128, TC, 6])
        held.mvc = sb("mvc", [128, TC, 2])
        held.ve = sb("ve", [128, NT])
        held.rstd = sb("rstd", [128, NT, 1])
        held.mhalf = sb("mhalf", [128, NT])
        held.ident = sb("ident", [128, 128])
        held.ones = sb("ones", [128, 128])
        held.onehot = sb("onehot", [128, 128], BF16)
        held.mask_a = sb("mask_a", [96, 8])
        held.mask_b = sb("mask_b", [128, 2])
        held.mask_bs = sb("mask_bs", [128, 2])
        held.mk01 = sb("mk01", [128, S], BF16)
        held.mk2 = sb("mk2", [S, S], BF16)
        held.nlp = sb("nlp", [128, 1])
        held.growth = sb("growth", [128, G6])
        held.gam = sb("gam", [128, D])
        held.bet = sb("bet", [128, D])
        held.ebias = sb("ebias", [128, EX4])
        held.rank = sb("rank", [128, EX4])
        held.lora_b = sb("lora_b", [EX4 * R8, D])
        held.wd_hi = sb("wd_hi", [128, DW], F16)
        held.wd_lo = sb("wd_lo", [128, DW], F16)
        with ExitStack() as early:
            def se(name, shape, dt=F32):
                return early.enter_context(nc.sbuf_tensor(name, shape, dt))
            held.wc_hi = se("wc_hi", [128, CW], F16)
            held.wc_lo = se("wc_lo", [128, CW], F16)
            held.kq_bias = se("kq_bias", [128, 1])
            held.wkq = se("wkq", [128, KB, 96 + QL])
            held.wqk = se("wqk", [128, 4, 96])
            held.wvo = [se("wvo_high", [128, D], F16), se("wvo_low", [128, D], F16)]
            held.bvo = [se("bvo_high", [1, D], F16), se("bvo_low", [1, D], F16)]
            held.units = se("units", [1, 128], F16)
            setup_stage(nc, held, a)
            if "A" in STAGES:
                stage_a(nc, held, a)
            if "B" in STAGES:
                stage_b(nc, held, a)
            if "C" in STAGES:
                stage_c(nc, held, a)
        held.wf_hi = sb("wf_hi", [128, FW], F16)
        held.wf_lo = sb("wf_lo", [128, FW], F16)
        if "D" in STAGES:
            stage_d(nc, held, a)
        if "E" in STAGES:
            stage_e(nc, held, a)
        if "F" in STAGES:
            stage_f(nc, held, a, out)
        else:
            done = held.sems.enter_context(nc.semaphore("out_done"))
            with nc.Block() as block:
                @block.sync
                def _(sp):
                    sp.dma_start(out.rearrange("(t p) n -> p t n", p=128), held.X[:]).then_inc(done, 16)
                    sp.wait_ge(done, 16)


def on_partitions(np, w):
    k, n = w.shape[0] // 128, w.shape[1]
    return w.reshape(k, 128, n).transpose(1, 0, 2).reshape(128, k * n)


def kernel(**inputs):
    import numpy as np
    import concourse.bacc as bacc
    from concourse.bass_utils import run_bass_kernel_spmd

    i = {k: np.asarray(v) for k, v in inputs.items()}
    L = lambda w: on_partitions(np, w)
    fuse = i["L1_attn_fuse_weight"]
    ffn_down = i["L1_attn_ffn_down_w"].T
    pad = np.zeros((128 * len(FB) - FD, D), ffn_down.dtype)
    w_d_up = np.concatenate([i["L1_attn_up_w"].T, i["L1_attn_gate_w"].T, i["L1_attn_ffn_gate_w"].T,
                             i["L1_attn_ffn_up_w"].T], 1)
    w_d_dn = np.concatenate([i["L1_attn_local_approx_output"].T, fuse.transpose(2, 1, 0).reshape(G6 * SD, D),
                             ffn_down, pad], 0)
    lora_a = i["L0_ffn_lora_A"].reshape(EX4 * R8, D).T
    ctx = i["ctx_1024"]
    arrays = {
        "x": i["x"].reshape(TOK, D),
        "ctx": ctx.reshape(TOK, 128),
        "ctx_t": ctx.transpose(2, 0, 1).reshape(128, TOK),
        "mask": i["mask_SxS2_ff0"],
        "Wkvq": np.concatenate([i["L0_attn_Wkv_d"], i["L0_attn_Wq_d"]], 1),
        "bq_d": i["L0_attn_bq_d"], "bkv_rep": np.tile(i["L0_attn_bkv_d"], 24),
        "W_qk": i["L0_attn_W_qk"], "b_qk": i["L0_attn_b_qk"],
        "Wv_uT": i["L0_attn_Wv_u"].T, "bv_uT": i["L0_attn_bv_u"].reshape(4, 128).T, "Wo": i["L0_attn_Wo"], "bo": i["L0_attn_bo"],
        "w_c": np.concatenate([L(i["L0_ffn_W_up"].T), L(np.concatenate([i["L0_ffn_gate_w"].T, lora_a], 1))], 1),
        "expert_bias": i["L0_ffn_expert_bias"],
        "lora_B": i["L0_ffn_lora_B"].transpose(0, 2, 1).reshape(EX4 * R8, D),
        "w_d": np.concatenate([L(w_d_up), L(w_d_dn)], 1),
        "local_point": i["L1_attn_local_point"], "discount": i["L1_attn_discount_factor"],
        "Wk": i["L1_xattn_Wk"], "Wq": i["L1_xattn_Wq"], "WvT": i["L1_xattn_Wv"].T, "WskipT": i["L1_xattn_Wskip"].T,
        "w_f": np.concatenate([L(np.concatenate([i["L1_ffn_up_w"], i["L1_ffn_fc1_w"], i["L1_ffn_gate_w"]], 1)),
                               L(i["L1_ffn_down_w"])], 1),
        "expertT": i["L1_ffn_expert_w"].T, "fc2": i["L1_ffn_fc2_w"],
        "gamma": i["L1_ffn_ln_gamma"], "beta": i["L1_ffn_ln_beta"],
    }
    arrays = {k: np.ascontiguousarray(v) for k, v in arrays.items()}
    nc = bacc.Bacc("TRN2", target_bir_lowering=False, num_devices=1)
    a = {k: nc.dram_tensor("in_" + k, v.shape, F32, kind="ExternalInput").ap() for k, v in arrays.items()}
    out = nc.dram_tensor("out_x", (TOK, D), F32, kind="ExternalOutput").ap()
    build(nc, a, out)
    r = run_bass_kernel_spmd(nc, [{"in_" + k: v for k, v in arrays.items()}], core_ids=[0])
    return r.results[0]["out_x"].reshape(NSEQ, S, D)
```

```python
from contextlib import ExitStack

import concourse.bass as bass
from concourse import mybir

F32 = mybir.dt.float32
F16 = mybir.dt.float16
BF16 = mybir.dt.bfloat16
ALU = mybir.AluOpType
ACT = mybir.ActivationFunctionType
AX = mybir.AxisListType

NSEQ, S, D = 32, 64, 512
TOK = NSEQ * S
NT = TOK // 128
KB = D // 128
NC = 4
TC = NT // NC
CH = 128 * TC
EPS = 1e-5
H = 32
DL = 4
QL = 12
DH = D // H
G8 = 8
XS = 2.0 ** 8
WS = 2.0 ** 8
HS = 2.0 ** 2
FS = 2.0 ** 4
PS = 2.0 ** 14
AS = 2.0 ** 6
EX4, R8 = 4, 8
CG = EX4 + EX4 * R8
CW = KB * (D + CG)
SD, G6 = 128, 6
FD = 1248
FB = [(i, min(128, FD - i)) for i in range(0, FD, 128)]
UPD = 2 * SD + 2 * FD
DND = G6 + 1 + len(FB)
DW = KB * UPD + DND * D
INT, LAT, NE = 1024, 256, 8
FU, FL = INT // 128, LAT // 128
FC = INT + LAT + NE
FW = KB * FC + FU * D
NP_D, NP_C, NP_F = 16, 4, 8
PD, PC, PF = DW // NP_D, CW // NP_C, FW // NP_F
assert PD * NP_D == DW and PC * NP_C == CW and PF * NP_F == FW


class Held:
    pass


def row(v):
    return v.rearrange("(a n) -> a n", a=1)


def wait_apart(eng, sem, value, marks):
    eng.wait_ge(sem, value)
    eng.sem_inc(marks, 1)


def norm_tile(nc, held, xn, t):
    return nc.vector.tensor_scalar(xn, held.X[:, t, :], held.mv[:, t, 0:1], held.rstd[:, t, 0:1],
                                   ALU.subtract, ALU.mult)


def transpose_tile(nc, held, ps, xn):
    for k in range(KB):
        last = nc.tensor.transpose(ps[:, 128 * k:128 * k + 128], xn[:, 128 * k:128 * k + 128], held.ident[:])
    return last


def mm3(nc, ps, st, mv, start, stop):
    nc.tensor.matmul(ps, st[0], mv[0], start=start, stop=False)
    nc.tensor.matmul(ps, st[0], mv[1], start=False, stop=False)
    return nc.tensor.matmul(ps, st[1], mv[0], start=False, stop=stop)


def rstd_all(nc, pool, held, at):
    nc.gpsimd.tensor_scalar(held.ve[:], held.mv[:, :, 1], EPS, None, ALU.add).then_inc(held.rs_ready, 1)
    pool.wait_ge(held.rs_ready, at - 1)
    nc.gpsimd.tensor_tensor(held.rstd[:, :, 0], held.ve[:], held.mhalf[:], ALU.pow).then_inc(held.rs_ready, 1)


def split_piece(nc, pool, raw, hi, lo, loaded, loaded_at, done, done_at, marks):
    wait_apart(pool, loaded, loaded_at, marks)
    nc.gpsimd.tensor_scalar(raw, raw, WS, None, ALU.mult).then_inc(done, 1)
    wait_apart(pool, done, done_at + 1, marks)
    nc.gpsimd.tensor_copy(hi, raw).then_inc(done, 1)
    wait_apart(pool, done, done_at + 2, marks)
    nc.gpsimd.tensor_tensor(lo, raw, hi, ALU.subtract).then_inc(done, 1)


def setup_stage(nc, held, a):
    with ExitStack() as es:
        def sb(name, shape, dt=F32):
            return es.enter_context(nc.sbuf_tensor(name, shape, dt))

        def sem(name):
            return held.sems.enter_context(nc.semaphore(name))

        def pb(name, shape):
            return es.enter_context(nc.psum_tensor(name, shape, F32))

        sel_wv = sb("sel_wv", [128, 4, H])
        sel_a = sb("sel_a", [96, 8, 3])
        sel_b = sb("sel_b", [128, 2, 4])
        sel_o = sb("sel_o", [128, 128, 3])
        wv_t = sb("wv_t", [128, 4, DL])
        wv_bd = sb("wv_bd", [128, 4, H, DL])
        wo = sb("wo", [128, 4, D])
        bv_col = sb("bv_col", [128, 4])
        bv_rep = sb("bv_rep", [128, 4, 128])
        bo = sb("bo", [1, D])
        wkv = sb("wkv", [128, KB, DL + QL])
        mask4 = sb("mask4", [128, S])
        mask_rest = sb("mask_rest", [128, S])
        disc = sb("disc", [128, G6])
        growth = sb("growth_log", [128, G6])
        p_wvo = pb("p_wvo", [128, D])
        p_bvo = pb("p_bvo", [128, D])
        x_in = [sem(f"su_x_in_{q}") for q in range(NC)]
        par_in, pat, cast, wv_ready, growth_ready, growth_exp, fold_ready = (
            sem("su_" + n) for n in ("par_in", "pattern", "cast", "wv_ready", "growth_ready",
                                     "growth_exp", "fold_ready"))
        loads = [
            (wv_t[:], a["Wv_uT"].rearrange("(o p) d -> p o d", p=128)),
            (wo[:], a["Wo"].rearrange("(o p) n -> p o n", p=128)),
            (bv_col[:], a["bv_uT"]),
            (bo[:], row(a["bo"])),
            (wkv[:], a["Wkvq"].rearrange("(k p) n -> p k n", p=128)),
            (disc[:], row(a["discount"]).broadcast_to([128, G6])),
            (held.nlp[:], a["local_point"].rearrange("(p a) -> p a", a=1)),
            (held.gam[:], row(a["gamma"]).broadcast_to([128, D])),
            (held.bet[:], row(a["beta"]).broadcast_to([128, D])),
            (held.ebias[:], row(a["expert_bias"]).broadcast_to([128, EX4])),
            (held.lora_b[:], a["lora_B"]),
            (held.kq_bias[0:96, :], a["bkv_rep"].rearrange("(p a) -> p a", a=1)),
            (held.kq_bias[96:96 + QL, :], a["bq_d"].rearrange("(p a) -> p a", a=1)),
        ]
        loads += [(mask4[64 * j:64 * j + 64, :], a["mask"]) for j in range(2)]
        for part in range(3):
            r = slice(32 * part, 32 * part + 32)
            loads += [(held.wqk[96:96 + QL, :, r], a["W_qk"].rearrange("q (g n) -> q g n", g=4)),
                      (held.wqk[96 + QL:97 + QL, :, r], a["b_qk"].rearrange("(a g n) -> a g n", a=1, g=4))]
        on_sp, on_act = loads[0::2], loads[1::2]
        par_all = 16 * len(loads)
        with nc.Block() as block:
            @block.sync
            def _(sp):
                for dst, src in on_sp:
                    sp.dma_start(dst, src).then_inc(par_in, 16)
                for q in range(NC):
                    sp.dma_start(held.X[:, TC * q:TC * q + TC, :],
                                 a["x"][CH * q:CH * q + CH, :].rearrange("(t p) n -> p t n", p=128)).then_inc(x_in[q], 16)
                sp.wait_ge(par_in, par_all)
                for q in range(NC):
                    sp.wait_ge(x_in[q], 16)

            @block.gpsimd
            def _(pool):
                built = 0

                def put(ins):
                    nonlocal built
                    built += 1
                    ins.then_inc(pat, 1)

                def band(t, base, pattern, width):
                    put(nc.gpsimd.affine_select(out=t, in_=t, compare_op=ALU.is_ge, fill=0.0, base=base,
                                                pattern=pattern, channel_multiplier=1))
                    pool.wait_ge(pat, built)
                    put(nc.gpsimd.affine_select(out=t, in_=t, compare_op=ALU.is_ge, fill=0.0,
                                                base=width - 1 - base, pattern=[[-st, n] for st, n in pattern],
                                                channel_multiplier=-1))
                for t in (held.ident, sel_wv, sel_a, sel_b, sel_o, held.ones):
                    put(nc.gpsimd.memset(t[:], 1.0))
                put(nc.gpsimd.memset(held.mhalf[:], -0.5))
                put(nc.gpsimd.memset(held.units[:], AS))
                pool.wait_ge(pat, built)
                band(held.ident[:], 0, [[-1, 128]], 1)
                band(sel_wv[:], 0, [[128, 4], [-DH, H]], DH)
                band(sel_a[:], 0, [[-DL, 8], [-32, 3]], DL)
                band(sel_b[:], 0, [[-DH, 2], [-32, 4]], DH)
                band(sel_o[:], -64, [[-1, 128], [64, 3]], 1)
                assert built == 18

            @block.vector
            def _(v):
                made = 0

                def step(ins):
                    nonlocal made
                    made += 1
                    ins.then_inc(cast, 1)
                v.wait_ge(pat, 18)
                step(nc.vector.tensor_reduce(held.mask_a[:], sel_a[:], AX.X, ALU.add))
                step(nc.vector.tensor_reduce(held.mask_b[:], sel_b[:], AX.X, ALU.add))
                v.wait_ge(cast, made)
                step(nc.vector.tensor_scalar(held.mask_bs[:], held.mask_b[:], AS, None, ALU.mult))
                step(nc.vector.tensor_reduce(held.onehot[:], sel_o[:], AX.X, ALU.max))
                for e in range(EX4):
                    step(nc.vector.memset(held.rank[:, e:e + 1], float(EX4 - e)))
                v.wait_ge(par_in, par_all)
                for o in range(4):
                    nc.vector.tensor_tensor(
                        wv_bd[:, o, :, :], wv_t[:, o:o + 1, :].broadcast_to([128, H, DL]),
                        sel_wv[:, o, :].rearrange("p (h a) -> p h a", a=1).broadcast_to([128, H, DL]),
                        ALU.mult).then_inc(wv_ready, 1)
                    nc.vector.tensor_scalar(bv_rep[:, o, :], held.ones[:], bv_col[:, o:o + 1], None,
                                            ALU.mult).then_inc(wv_ready, 1)
                nc.vector.tensor_copy(growth[:, 0:1], disc[:, 0:1]).then_inc(growth_ready, 1)
                nc.vector.tensor_tensor(growth[:, 1:G6], disc[:, 1:G6], disc[:, 0:G6 - 1],
                                        ALU.subtract).then_inc(growth_ready, 1)
                step(nc.vector.tensor_scalar(held.nlp[:], held.nlp[:], -1.0, None, ALU.mult))
                step(nc.vector.tensor_copy(
                    held.wkq[:, :, 0:96].rearrange("p k (r d) -> p k r d", d=DL),
                    wkv[:, :, 0:DL].rearrange("p k (a d) -> p k a d", a=1).broadcast_to([128, KB, 24, DL])))
                step(nc.vector.tensor_copy(held.wkq[:, :, 96:96 + QL], wkv[:, :, DL:DL + QL]))
                step(nc.vector.tensor_scalar(mask4[:], mask4[:], DH ** 0.5 * XS * AS, None, ALU.mult))
                v.wait_ge(cast, made)
                step(nc.vector.tensor_copy(held.mk01[:], mask4[:]))
                v.wait_ge(cast, made)
                step(nc.vector.tensor_tensor(mask_rest[:], mask4[:], held.mk01[:], ALU.subtract))
                v.wait_ge(cast, made)
                step(nc.vector.tensor_copy(held.mk01[64:128, :], mask_rest[64:128, :]))
                step(nc.vector.tensor_copy(held.mk2[:], mask_rest[0:64, :]))
                v.wait_ge(cast, made)
                step(nc.vector.tensor_tensor(held.mk2[:], mask_rest[0:64, :], held.mk2[:], ALU.subtract))
                for q in range(NC):
                    v.wait_ge(x_in[q], 16)
                    for i in range(TC):
                        step(nc.vector.bn_stats(held.st[:, i, :], held.X[:, TC * q + i, :]))
                    v.wait_ge(cast, made)
                    for i in range(TC):
                        step(nc.vector.bn_aggr(held.mv[:, TC * q + i, :], held.st[:, i, :]))
                    v.wait_ge(cast, made)
                v.wait_ge(fold_ready, 1)
                step(nc.vector.tensor_scalar(held.wvo[0][:], p_wvo[:], WS, None, ALU.mult))
                v.wait_ge(fold_ready, 2)
                step(nc.vector.tensor_scalar(held.bvo[0][:], p_bvo[0:1, :], WS, None, ALU.mult))
                v.wait_ge(cast, made)
                step(nc.vector.scalar_tensor_tensor(held.wvo[1][:], p_wvo[:], WS, held.wvo[0][:],
                                                    ALU.mult, ALU.subtract))
                step(nc.vector.scalar_tensor_tensor(held.bvo[1][:], p_bvo[0:1, :], WS, held.bvo[0][:],
                                                    ALU.mult, ALU.subtract))
                v.wait_ge(cast, made)

            @block.tensor
            def _(pe):
                pe.wait_ge(par_in, par_all)
                pe.wait_ge(wv_ready, 8)
                for o in range(4):
                    last = nc.tensor.matmul(p_wvo[:], wv_bd[:, o, :, :].rearrange("p h d -> p (h d)"), wo[:, o, :],
                                            start=o == 0, stop=o == 3)
                last.then_inc(fold_ready, 1)
                for o in range(4):
                    nc.tensor.matmul(p_bvo[:], bv_rep[:, o, :], wo[:, o, :], start=o == 0, stop=False)
                pe.wait_ge(pat, 18)
                nc.tensor.matmul(p_bvo[:], held.ones[0:1, :], bo[:], start=False, stop=True).then_inc(fold_ready, 1)

            @block.scalar
            def _(act):
                for dst, src in on_act:
                    act.dma_start(dst, src).then_inc(par_in, 16)
                act.wait_ge(growth_ready, 2)
                nc.scalar.activation(held.growth[:], growth[:], ACT.Exp, scale=-1.0).then_inc(growth_exp, 1)
                act.wait_ge(growth_exp, 1)


def high(act, nc, c, i, t_ready, hi_ready, xt, ps):
    act.wait_ge(t_ready, TC * c + i + 3)
    nc.scalar.activation(xt[0][:, :, 128 * i:128 * i + 128], ps[:, i, :].rearrange("p (k n) -> p k n", k=KB),
                         ACT.Copy, scale=XS).then_inc(hi_ready, 1)


def low(v, nc, c, i, hi_ready, xt_ready, xt, ps):
    tile = slice(128 * i, 128 * i + 128)
    v.wait_ge(hi_ready, TC * c + i + 1)
    nc.vector.scalar_tensor_tensor(xt[1][:, :, tile], ps[:, i, :].rearrange("p (k n) -> p k n", k=KB), XS,
                                   xt[0][:, :, tile], ALU.mult, ALU.subtract).then_inc(xt_ready, 1)


def silu(act, nc, c, j, n, up_ready, sg_ready, sg, p_up, val_ready):
    act.wait_ge(up_ready, (1 + len(FB)) * c + j + 1)
    if j > 2:
        act.wait_ge(val_ready, (DND - 1) * c + G6 + j - 1)
    nc.scalar.activation(sg[0:n, (j + G6) % 2, :], p_up[0:n, 2 * (j % 2), :], ACT.Silu,
                         scale=1.0 / (XS * WS)).then_inc(sg_ready, 1)


def update_tile(v, nc, held, c, i, ready, x_sum, scale, read, marks, credit=1):
    t = TC * c + i
    v.wait_ge(ready, t + 1)
    nc.vector.scalar_tensor_tensor(held.X[:, t, :], x_sum, 1.0 / scale, held.X[:, t, :],
                                   ALU.mult, ALU.add).then_inc(read, 1)
    stats_tile(v, nc, held, c, i, read, t + 1 + credit, marks)


def stats_tile(v, nc, held, c, i, read, read_at, marks):
    apart, stats = marks
    k = (2 * TC + 1) * c + 2 * i
    wait_apart(v, read, read_at, apart)
    nc.vector.bn_stats(held.st[:, i, :], held.X[:, TC * c + i, :]).then_inc(stats, 1)
    wait_apart(v, stats, k + 1, apart)
    nc.vector.bn_aggr(held.mvc[:, i, :], held.st[:, i, :]).then_inc(stats, 1)
    if i == TC - 1:
        v.wait_ge(stats, k + 2)
        nc.vector.tensor_scalar(held.mv[:, bass.ds(TC * c, TC), :], held.mvc[:], 1.0, None, ALU.mult).then_inc(stats, 1)


class Weights:

    def __init__(self, nc, held, es, name, dram, hi, lo, pieces, width):
        self.nc, self.held, self.dram, self.hi, self.lo, self.pieces, self.width = nc, held, dram, hi, lo, pieces, width
        self.raw = es.enter_context(nc.sbuf_tensor(name + "_raw", [128, 2, width], F32))
        self.loaded = [held.sems.enter_context(nc.semaphore(f"{name}_loaded_{j}")) for j in range(2)]
        self.split = held.sems.enter_context(nc.semaphore(name + "_split"))

    def fetch(self, sp):
        width = self.width
        with sp.Fori(0, self.pieces // 2) as q:
            for j in range(2):
                sp.wait_ge(self.split, 6 * q + 3 * j + 3)
                sp.dma_start(self.raw[:, j, :],
                             self.dram[:, bass.ds((2 * q + j) * width, width)]).then_inc(self.loaded[j], 16)

    def divide(self, pool):
        nc, width = self.nc, self.width
        pool.sem_inc(self.split, 6)
        with pool.Fori(0, self.pieces // 2) as q:
            for j in range(2):
                part = bass.ds((2 * q + j) * width, width)
                split_piece(nc, pool, self.raw[:, j, :], self.hi[:, part], self.lo[:, part], self.loaded[j],
                            16 * q + 16, self.split, 6 * q + 3 * j + 6, self.held.apart)
        pool.wait_ge(self.split, 3 * self.pieces + 6)


NU = 2 * TC
UH = H // 2


def soft_unit(nc, v, sems, bufs, u, slot, credit=0):
    s_ready, top_ready, t_ready, sub_ready = sems
    p_s, top, prob = bufs
    scores = p_s[:, 2 * slot:2 * slot + 2, :].rearrange("p b (h k) -> p (b h) k", k=S)
    v.wait_ge(s_ready, u + 1 + credit)
    nc.vector.tensor_reduce(top[:, slot, :], scores, AX.X, ALU.max).then_inc(top_ready, 1)
    v.wait_ge(top_ready, u + 1)
    v.wait_ge(t_ready, 2 * u + 2)
    nc.vector.tensor_tensor(prob[:, slot, :, :], scores,
                            top[:, slot, :].rearrange("p (h a) -> p h a", a=1).broadcast_to([128, UH, S]),
                            ALU.subtract).then_inc(sub_ready, 1)


def exp_unit(nc, act, sub_ready, exp_ready, prob, u, slot, scale):
    act.wait_ge(sub_ready, u + 3)
    nc.scalar.activation(prob[:, slot, :, :], prob[:, slot, :, :], ACT.Exp, scale=scale).then_inc(exp_ready, 1)


def transpose_unit(nc, pe, held, sems, p_t, prob, u, slot):
    exp_ready, pt_ready, t_ready = sems
    pe.wait_ge(exp_ready, u + 1)
    for b in range(2):
        pe.wait_ge(pt_ready, 2 * u + b + 1)
        for j in range(UH // 4):
            last = nc.tensor.transpose(p_t[:, b, 128 * j:128 * j + 128],
                                       prob[:, slot, UH // 2 * b + 2 * j:UH // 2 * b + 2 * j + 2, :]
                                       .rearrange("p h k -> p (h k)"), held.ident[:])
        last.then_inc(t_ready, 1)


def high_pt(nc, act, sems, pt, p_t, u, slot, credit=0):
    t_ready, v_ready, pt_high = sems
    for b in range(2):
        act.wait_ge(t_ready, 2 * u + b + 5)
        if b == 0:
            act.wait_ge(v_ready, u + 1 + credit)
        nc.scalar.activation(pt[0][:, slot, b, :], p_t[:, b, :], ACT.Copy, scale=PS).then_inc(pt_high, 1)


def low_pt(nc, v, pt_high, pt_ready, pt, p_t, u, slot):
    for b in range(2):
        v.wait_ge(pt_high, 2 * u + b + 1)
        nc.vector.scalar_tensor_tensor(pt[1][:, slot, b, :], p_t[:, b, :], PS, pt[0][:, slot, b, :],
                                       ALU.mult, ALU.subtract).then_inc(pt_ready, 1)


def stage_a(nc, held, a):
    with ExitStack() as es:
        def sb(name, shape, dt=F32):
            return es.enter_context(nc.sbuf_tensor("a_" + name, shape, dt))

        def sem(name):
            return held.sems.enter_context(nc.semaphore("a_" + name))

        def pb(name, shape):
            return es.enter_context(nc.psum_tensor("a_" + name, shape, F32))

        PR = 96
        PREP = 19
        VC = 2 * (DL + 1)
        xn = sb("xn", [128, 2, D])
        xt = sb("xt", [128, KB, CH])
        kf = sb("kf", [128, CH])
        keys = sb("keys", [PR, CH], F16)
        bd = sb("bd", [PR, 8, CH], F16)
        qs = sb("qs", [PR, 4, CH], F16)
        vb = [sb("vb_high", [128, 2 * TC, 2, DL + 1], F16), sb("vb_low", [128, 2 * TC, 2, DL + 1], F16)]
        top = sb("top", [128, 2, UH])
        prob = sb("prob", [128, 2, UH, S])
        pt = [sb("pt_high", [128, 2, 2, D], F16), sb("pt_low", [128, 2, 2, D], F16)]
        rec = sb("rec", [128, 2, UH])
        z = sb("z", [128, TC, H, DL])
        zt = [sb("zt_high", [128, CH], F16), sb("zt_low", [128, CH], F16)]
        p_s = pb("p_s", [128, 4, D])
        p_t = pb("p_t", [128, 2, D])
        p_v = pb("p_v", [128, 2, D])
        p_x = p_t[:, 0, :]
        p_z = p_v[:, 1, :]
        vb_clear, xn_ready, tr_ready, xt_ready, lat_ready, cq_ready, prep, vt_ready, q_ready, q_high, \
            s_ready, top_ready, sub_ready, exp_ready, t_ready, pt_high, pt_ready, v_ready, rec_ready, z_part, \
            z_ready, zt_ready, zt_high, zt_low, o_ready, x_read, stats = (sem(n) for n in (
                "vb_clear", "xn_ready", "tr_ready", "xt_ready", "lat_ready", "cq_ready", "prep",
                "vt_ready", "q_ready", "q_high", "s_ready", "top_ready", "sub_ready", "exp_ready", "t_ready",
                "pt_high", "pt_ready", "v_ready", "rec_ready", "z_part", "z_ready", "zt_ready", "zt_high",
                "zt_low", "o_ready", "x_read", "stats"))
        VU = UH // 2 * 2 * VC

        late = [Weights(nc, held, es, "wd", a["w_d"], held.wd_hi, held.wd_lo, NP_D, PD),
                Weights(nc, held, es, "wc", a["w_c"], held.wc_hi, held.wc_lo, NP_C, PC)]

        rs_at = held.rs_steps = held.rs_steps + 2

        with nc.Block() as block:
            @block.sync
            def _(sp):
                for w in late:
                    w.fetch(sp)

            @block.gpsimd
            def _(pool):
                for w in vb:
                    nc.gpsimd.memset(w[:], 0.0).then_inc(vb_clear, 1)
                pool.wait_ge(vb_clear, 2)
                nc.gpsimd.memset(kf[96:128, :], 1.0).then_inc(vb_clear, 1)
                pool.wait_ge(vb_clear, 3)
                for h in range(2):
                    nc.gpsimd.memset(vb[0][64 * h:64 * h + 64, :, h, DL:DL + 1], AS).then_inc(vb_clear, 1)
                pool.wait_ge(vb_clear, 5)
                rstd_all(nc, pool, held, rs_at)
                for w in late:
                    w.divide(pool)

            @block.vector
            def _(v):
                v.wait_ge(held.rs_ready, rs_at)
                v.wait_ge(vb_clear, 5)
                v.sem_inc(sub_ready, 2)
                v.sem_inc(pt_ready, 2)
                v.sem_inc(z_ready, 2)
                v.sem_inc(x_read, TC)

                def norm(c, i):
                    v.wait_ge(tr_ready, TC * c + i + 1)
                    norm_tile(nc, held, xn[:, i % 2, :], TC * c + i).then_inc(xn_ready, 1)

                def make_keys(c):
                    v.wait_ge(lat_ready, c + 1)
                    nc.vector.tensor_scalar(kf[0:PR, :], p_x[0:PR, :], held.kq_bias[0:PR, 0:1], AS,
                                            ALU.add, ALU.mult).then_inc(prep, 1)
                    v.wait_ge(prep, PREP * c + 1)
                    nc.vector.tensor_copy(keys[:], kf[0:PR, :]).then_inc(prep, 1)
                    v.wait_ge(prep, PREP * c + 2)
                    nc.vector.tensor_tensor(keys[32:64, :], kf[32:64, :], keys[32:64, :], ALU.subtract).then_inc(prep, 1)

                def spread(c):
                    v.wait_ge(prep, PREP * c + 3)
                    for h in range(8):
                        nc.vector.tensor_scalar(bd[:, h, :], keys[:], held.mask_a[:, h:h + 1], None,
                                                ALU.mult).then_inc(prep, 1)
                    v.wait_ge(vt_ready, c + 1)
                    for h in range(2):
                        r = slice(64 * h, 64 * h + 64)
                        vt = p_t[r, 1, 0:8 * DL].rearrange("p (b d) -> p b d", d=DL)
                        nc.vector.tensor_copy(vb[0][r, :, h, 0:DL], vt).then_inc(prep, 1)
                        v.wait_ge(prep, PREP * c + 12 + 2 * h)
                        nc.vector.tensor_tensor(vb[1][r, :, h, 0:DL], vt, vb[0][r, :, h, 0:DL],
                                                ALU.subtract).then_inc(prep, 1)

                def low_queries(c):
                    for g in range(4):
                        r = slice(64, 96)
                        v.wait_ge(q_high, 4 * c + g + 1)
                        nc.vector.scalar_tensor_tensor(qs[r, g, :], p_s[r, g, :], AS, qs[r, g, :],
                                                       ALU.mult, ALU.subtract).then_inc(prep, 1)

                def norm_z(c, j):
                    u, slot, i = NU * c + j, j % 2, j // 2
                    sums = p_v[:, slot, 0:VU].rearrange("p (b s h n) -> p b s h n", s=2, h=2,
                                                                         n=DL + 1)
                    v.wait_ge(v_ready, u + 3)
                    for s in range(2):
                        r = slice(64 * s, 64 * s + 64)
                        nc.vector.reciprocal(rec[r, slot, :].rearrange("p (b h) -> p b h", h=2),
                                             sums[r, :, s, :, DL]).then_inc(rec_ready, 1)
                    v.wait_ge(rec_ready, 2 * u + 2)
                    for s in range(2):
                        r = slice(64 * s, 64 * s + 64)
                        last = nc.vector.tensor_tensor(
                            z[r, i, UH * slot:UH * slot + UH, :].rearrange("p (b h) n -> p b h n", h=2),
                            sums[r, :, s, :, 0:DL],
                            rec[r, slot, :].rearrange("p (b h a) -> p b h a", h=2, a=1)
                            .broadcast_to([64, UH // 2, 2, DL]), ALU.mult)
                        last.then_inc(z_ready if s else z_part, 1)
                def low_p(c, j):
                    low_pt(nc, v, pt_high, pt_ready, pt, p_t, NU * c + j, j % 2)

                def units(c, more):
                    for j in range(NU):
                        soft_unit(nc, v, (s_ready, top_ready, t_ready, sub_ready), (p_s, top, prob),
                                  NU * c + j, j % 2)
                        if j >= 1:
                            low_p(c, j - 1)
                        if j >= 2:
                            norm_z(c, j - 2)
                    if more:
                        norm(c + 1, 0)
                        norm(c + 1, 1)
                    low_p(c, NU - 1)
                    norm_z(c, NU - 2)
                    norm_z(c, NU - 1)
                    if more:
                        norm(c + 1, 2)
                        norm(c + 1, 3)
                    v.wait_ge(zt_high, c + 1)
                    nc.vector.scalar_tensor_tensor(zt[1][:], p_z, AS, zt[0][:], ALU.mult,
                                                   ALU.subtract).then_inc(zt_low, 1)
                    if more:
                        make_keys(c + 1)
                    for i in range(TC):
                        update_tile(v, nc, held, c, i, o_ready, p_s[:, i, :], AS * WS, x_read,
                                    (held.apart, stats), TC)
                    if more:
                        spread(c + 1)
                        low_queries(c + 1)
                for i in range(TC):
                    norm(0, i)
                make_keys(0)
                spread(0)
                low_queries(0)
                with v.Fori(0, NC - 1) as c:
                    units(c, True)
                units(NC - 1, False)
                v.wait_ge(stats, NC * (2 * TC + 1))

            @block.scalar
            def _(act):
                act.wait_ge(vb_clear, 5)

                def copy_x(c):
                    for i in range(TC):
                        act.wait_ge(tr_ready, TC * c + i + 3)
                        nc.scalar.activation(xt[:, :, 128 * i:128 * i + 128],
                                             p_t[:, i % 2, :].rearrange("p (k n) -> p k n", k=KB),
                                             ACT.Copy).then_inc(xt_ready, 1)

                def queries(c):
                    act.wait_ge(lat_ready, c + 1)
                    nc.scalar.activation(kf[96:96 + QL, :], p_x[96:96 + QL, :], ACT.Identity,
                                         bias=held.kq_bias[96:96 + QL, 0:1]).then_inc(cq_ready, 1)
                    for g in range(4):
                        act.wait_ge(q_ready, 4 * c + g + 1)
                        nc.scalar.activation(qs[:, g, :], p_s[0:PR, g, :], ACT.Copy, scale=AS).then_inc(q_high, 1)

                def units(c, more):
                    for j in range(NU):
                        if j:
                            high_pt(nc, act, (t_ready, v_ready, pt_high), pt, p_t, NU * c + j - 1, (j - 1) % 2)
                        exp_unit(nc, act, sub_ready, exp_ready, prob, NU * c + j, j % 2, DL ** -0.5 / (AS * AS))
                    high_pt(nc, act, (t_ready, v_ready, pt_high), pt, p_t, NU * c + NU - 1, (NU - 1) % 2)
                    if more:
                        copy_x(c + 1)
                    act.wait_ge(zt_ready, c + 1)
                    nc.scalar.activation(zt[0][:], p_z, ACT.Copy, scale=AS).then_inc(zt_high, 1)
                    if more:
                        queries(c + 1)
                copy_x(0)
                queries(0)
                with act.Fori(0, NC - 1) as c:
                    units(c, True)
                units(NC - 1, False)

            @block.tensor
            def _(pe):
                pe.sem_inc(tr_ready, 2)
                pe.sem_inc(t_ready, 4)
                pe.sem_inc(v_ready, 2)

                def turn(c):
                    for i in range(TC):
                        pe.wait_ge(xn_ready, TC * c + i + 1)
                        if i < 2:
                            pe.wait_ge(pt_ready, 2 * NU * c + i + 1)
                        else:
                            pe.wait_ge(xt_ready, TC * c + i - 1)
                        transpose_tile(nc, held, p_t[:, i % 2, :], xn[:, i % 2, :]).then_inc(tr_ready, 1)

                def latents(c):
                    pe.wait_ge(xt_ready, TC * c + TC)
                    for k in range(KB):
                        last = nc.tensor.matmul(p_x[0:96 + QL, :], held.wkq[:, k, :], xt[:, k, :],
                                                start=k == 0, stop=k == KB - 1)
                    last.then_inc(lat_ready, 1)

                def values_queries(c):
                    pe.wait_ge(prep, PREP * c + 1)
                    for b in range(2 * TC):
                        for h in range(2):
                            last = nc.tensor.matmul(p_t[64 * h:64 * h + 64, 1, DL * b:DL * b + DL],
                                                    kf[0:DL, 64 * b:64 * b + 64], held.ident[0:DL, 0:DL],
                                                    start=True, stop=True)
                    last.then_inc(vt_ready, 1)
                    pe.wait_ge(cq_ready, c + 1)
                    for g in range(4):
                        pe.wait_ge(x_read, TC * c + g + 1)
                        nc.tensor.matmul(p_s[0:PR, g, :], held.wqk[96:97 + QL, g, :], kf[96:97 + QL, :],
                                         start=True, stop=True).then_inc(q_ready, 1)

                def scores(c, j):
                    u, slot, i = NU * c + j, j % 2, j // 2
                    pe.wait_ge(sub_ready, u + 1)
                    for gi in range(2):
                        for s in range(2):
                            seq = slice(128 * i + 64 * s, 128 * i + 64 * s + 64)
                            last = nc.tensor.matmul(p_s[64 * s:64 * s + 64, 2 * slot + gi, :],
                                                    qs[:, 2 * slot + gi, seq], bd[:, :, seq],
                                                    start=True, stop=True)
                    last.then_inc(s_ready, 1)

                def attend(c, j):
                    u, slot, i = NU * c + j, j % 2, j // 2
                    pe.wait_ge(pt_ready, 2 * u + 4)
                    pe.wait_ge(z_ready, u + 1)
                    for b in range(UH // 2):
                        last = mm3(nc, p_v[:, slot, 2 * VC * b:2 * VC * b + 2 * VC],
                                   [w[:, slot, b // 4, 128 * (b % 4):128 * (b % 4) + 128] for w in pt],
                                   [w[:, 2 * i:2 * i + 2, :, :].rearrange("p s h n -> p (s h n)") for w in vb],
                                   True, True)
                    last.then_inc(v_ready, 1)

                def units(c, more):
                    pe.wait_ge(prep, PREP * c + PREP)
                    scores(c, 0)
                    scores(c, 1)
                    for j in range(NU):
                        transpose_unit(nc, pe, held, (exp_ready, pt_ready, t_ready), p_t, prob, NU * c + j, j % 2)
                        if j:
                            attend(c, j - 1)
                        if j + 2 < NU:
                            scores(c, j + 2)
                    attend(c, NU - 1)
                    if more:
                        turn(c + 1)
                    pe.wait_ge(z_ready, NU * c + NU + 2)
                    for i in range(TC):
                        last = nc.tensor.transpose(p_z[:, 128 * i:128 * i + 128],
                                                   z[:, i, :, :].rearrange("p h d -> p (h d)"), held.ident[:])
                    last.then_inc(zt_ready, 1)
                    if more:
                        latents(c + 1)
                    pe.wait_ge(zt_low, c + 1)
                    for i in range(TC):
                        mm3(nc, p_s[:, i, :], [w[:, 128 * i:128 * i + 128] for w in zt],
                            [w[:] for w in held.wvo], True, False)
                        nc.tensor.matmul(p_s[:, i, :], held.units[:], held.bvo[0][:], start=False, stop=False)
                        nc.tensor.matmul(p_s[:, i, :], held.units[:], held.bvo[1][:], start=False,
                                         stop=True).then_inc(o_ready, 1)
                    if more:
                        values_queries(c + 1)
                turn(0)
                latents(0)
                values_queries(0)
                with pe.Fori(0, NC - 1) as c:
                    units(c, True)
                units(NC - 1, False)


def stage_b(nc, held, a):
    with ExitStack() as es:
        def sb(name, shape, dt=F32):
            return es.enter_context(nc.sbuf_tensor("b_" + name, shape, dt))

        def sem(name):
            return held.sems.enter_context(nc.semaphore("b_" + name))

        def pb(name, shape):
            return es.enter_context(nc.psum_tensor("b_" + name, shape, F32))

        VC = 2 * 2 * (DH + 1)
        xn = sb("xn", [128, 2, D])
        xt = [sb("xt_high", [128, KB, CH], F16), sb("xt_low", [128, KB, CH], F16)]
        kt = sb("kt", [128, 2, KB, 128])
        bd = [sb("bd_high", [128, 2, KB, CH], F16), sb("bd_low", [128, 2, KB, CH], F16)]
        ks = sb("ks", [128, KB * 128])
        cd = sb("cd", [128, 2, 2, 128])
        vb = [sb("vb_high", [128, 2 * TC, G8, 2, DH + 1], F16), sb("vb_low", [128, 2 * TC, G8, 2, DH + 1], F16)]
        top = sb("top", [128, 2, UH])
        prob = sb("prob", [128, 2, UH, S])
        pt = [sb("pt_high", [128, 2, 2, D], F16), sb("pt_low", [128, 2, 2, D], F16)]
        rec = sb("rec", [128, 2, UH])
        o = sb("o", [128, 2, KB, 4, 2, DH])
        p_s = pb("p_s", [128, 4, D])
        p_t = pb("p_t", [128, 2, D])
        p_v = pb("p_v", [128, 2, D])
        vb_clear, vb_ready, xn_ready, tr_ready, hi_ready, xt_ready, bd_high, bd_ready, ks_ready, \
            s_ready, top_ready, sub_ready, exp_ready, t_ready, pt_high, pt_ready, v_ready, rec_ready, o_part, \
            z_ready, x_ready, stats = (sem(n) for n in (
                "vb_clear", "vb_ready", "xn_ready", "tr_ready", "hi_ready",
                "xt_ready", "bd_high", "bd_ready", "ks_ready", "s_ready", "top_ready", "sub_ready", "exp_ready", "t_ready",
                "pt_high", "pt_ready", "v_ready", "rec_ready", "o_part", "z_ready", "x_ready", "stats"))
        kt_in = [sem(f"kt_in_{b}") for b in range(2)]
        cd_in = [sem(f"cd_in_{b}") for b in range(2)]
        VB = 5
        XB = 2
        ctx_b = a["ctx"].rearrange("(b k) n -> k b n", k=S)

        rs_at = held.rs_steps = held.rs_steps + 2

        with nc.Block() as block:
            @block.sync
            def _(sp):
                with sp.Fori(0, NC) as c:
                    for i in range(TC):
                        t, b = TC * c + i, i % 2
                        sp.wait_ge(bd_ready, 2 * t + 1)
                        for k in range(KB):
                            for g in range(2):
                                at = DH * (2 * k + g)
                                sp.dma_start(kt[64 * g:64 * g + 64, b, k, :],
                                             a["ctx_t"][at:at + DH, bass.ds(128 * t, 128)]
                                             .rearrange("(a d) n -> a d n", a=1).broadcast_to([4, DH, 128])
                                             ).then_inc(kt_in[b], 16)
                        sp.wait_ge(vb_ready, VB * t + VB)
                        for h in range(2):
                            sp.dma_start(cd[64 * h:64 * h + 64, b, :, :],
                                         ctx_b[:, bass.ds(2 * t, 2), :]).then_inc(cd_in[b], 16)

            @block.gpsimd
            def _(pool):
                for w in vb:
                    nc.gpsimd.memset(w[:], 0.0).then_inc(vb_clear, 1)
                pool.wait_ge(vb_clear, 2)
                for h in range(2):
                    nc.gpsimd.memset(vb[0][64 * h:64 * h + 64, :, :, h, DH:DH + 1], AS).then_inc(vb_clear, 1)
                pool.wait_ge(vb_clear, 4)
                rstd_all(nc, pool, held, rs_at)
                pool.sem_inc(vb_ready, 2 * VB)
                pool.sem_inc(bd_ready, 3)
                with pool.Fori(0, NC) as c:
                    for i in range(TC):
                        t, b = TC * c + i, i % 2
                        wait_apart(pool, kt_in[b], 128 * (TC // 2 * c + i // 2) + 128, held.apart)
                        for h in range(2):
                            wait_apart(pool, vb_ready if h == 0 else bd_ready, VB * t + 2 * VB if h == 0 else 2 * t + 4,
                                       held.apart)
                            nc.gpsimd.tensor_scalar(ks[:], kt[:, b, :, :].rearrange("p k n -> p (k n)"),
                                                    held.mask_bs[:, h:h + 1], None, ALU.mult).then_inc(ks_ready, 1)
                            wait_apart(pool, ks_ready, 2 * t + h + 1, held.apart)
                            wait_apart(pool, bd_high, 2 * t + h + 1, held.apart)
                            nc.gpsimd.tensor_tensor(bd[1][:, h, :, 128 * i:128 * i + 128],
                                                    ks[:].rearrange("p (k n) -> p k n", k=KB),
                                                    bd[0][:, h, :, 128 * i:128 * i + 128],
                                                    ALU.subtract).then_inc(bd_ready, 1)
                        made = VB * t + 2 * VB
                        wait_apart(pool, cd_in[b], 32 * (TC // 2 * c + i // 2) + 32, held.apart)
                        wait_apart(pool, bd_ready, 2 * t + 5, held.apart)
                        nc.gpsimd.tensor_scalar(cd[:, b, :, :], cd[:, b, :, :], AS, None, ALU.mult).then_inc(vb_ready, 1)
                        wait_apart(pool, vb_ready, made + 1, held.apart)
                        wait_apart(pool, v_ready, 2 * t + 2, held.apart)
                        halves = [(slice(64 * h, 64 * h + 64), h) for h in range(2)]
                        part = slice(2 * i, 2 * i + 2)
                        for r, h in halves:
                            nc.gpsimd.tensor_copy(vb[0][r, part, :, h, 0:DH],
                                                  cd[r, b, :, :].rearrange("p b (g d) -> p b g d", g=G8)
                                                  ).then_inc(vb_ready, 1)
                        for r, h in halves:
                            wait_apart(pool, vb_ready, made + 2 + h, held.apart)
                            nc.gpsimd.tensor_tensor(vb[1][r, part, :, h, 0:DH],
                                                    cd[r, b, :, :].rearrange("p b (g d) -> p b g d", g=G8),
                                                    vb[0][r, part, :, h, 0:DH], ALU.subtract).then_inc(vb_ready, 1)

            @block.vector
            def _(v):
                v.wait_ge(held.rs_ready, rs_at)
                v.sem_inc(sub_ready, 2)
                v.sem_inc(pt_ready, 2)
                v.sem_inc(z_ready, 1)

                def norm(c, i):
                    v.wait_ge(tr_ready, TC * c + i + 1)
                    norm_tile(nc, held, xn[:, i % 2, :], TC * c + i).then_inc(xn_ready, 1)

                def low_x(c, i):
                    tile = slice(128 * (i % TC), 128 * (i % TC) + 128)
                    v.wait_ge(hi_ready, TC * c + i + 1)
                    nc.vector.scalar_tensor_tensor(xt[1][:, :, tile], p_s[:, XB, :].rearrange("p (k n) -> p k n", k=KB),
                                                   XS, xt[0][:, :, tile], ALU.mult, ALU.subtract).then_inc(xt_ready, 1)

                def soft(c, j):
                    soft_unit(nc, v, (s_ready, top_ready, t_ready, sub_ready), (p_s, top, prob), NU * c + j, j % 2, 6)

                def low_p(c, j):
                    low_pt(nc, v, pt_high, pt_ready, pt, p_t, NU * c + j, j % 2)

                def norm_o(c, j):
                    u, slot, i = NU * c + j, j % 2, j // 2
                    v.wait_ge(v_ready, u + 9)
                    for s in range(2):
                        r = slice(64 * s, 64 * s + 64)
                        for q in range(2):
                            sums = p_v[r, q, 0:KB * VC].rearrange("p (k s h n) -> p k s h n", s=2, h=2, n=DH + 1)
                            nc.vector.reciprocal(rec[r, slot, 8 * q:8 * q + 8].rearrange("p (k h) -> p k h", h=2),
                                                 sums[:, :, s, :, DH]).then_inc(rec_ready, 1)
                    v.wait_ge(rec_ready, 4 * u + 4)
                    for s in range(2):
                        r = slice(64 * s, 64 * s + 64)
                        for q in range(2):
                            sums = p_v[r, q, 0:KB * VC].rearrange("p (k s h n) -> p k s h n", s=2, h=2, n=DH + 1)
                            last = nc.vector.tensor_tensor(
                                o[r, i % 2, :, 2 * slot + q, :, :], sums[:, :, s, :, 0:DH],
                                rec[r, slot, 8 * q:8 * q + 8].rearrange("p (k h a) -> p k h a", h=2, a=1)
                                .broadcast_to([64, KB, 2, DH]), ALU.mult)
                            last.then_inc(z_ready if s and q else o_part, 1)

                def update(c, i):
                    t = TC * c + i
                    v.wait_ge(z_ready, 2 * t + 3)
                    nc.vector.tensor_tensor(held.X[:, t, :], held.X[:, t, :],
                                            o[:, i % 2, :, :, :, :].rearrange("p k q h d -> p (k q h d)"),
                                            ALU.add).then_inc(x_ready, 1)
                    stats_tile(v, nc, held, c, i, x_ready, t + 1, (held.apart, stats))

                def units(c, more):
                    for j in range(NU):
                        i = (j + 5) // 2
                        if more or j + 2 < NU:
                            soft(c, j + 2)
                        if more or j + 1 < NU:
                            low_p(c, j + 1)
                        if j % 2 == 0 and (more or i + 1 < TC):
                            norm(c, i + 1)
                        if j % 2 == 1 and (more or i < TC):
                            low_x(c, i)
                        norm_o(c, j)
                        if j % 2:
                            update(c, j // 2)
                norm(0, 0)
                norm(0, 1)
                for i in range(2):
                    low_x(0, i)
                norm(0, 2)
                soft(0, 0)
                soft(0, 1)
                low_p(0, 0)
                low_x(0, 2)
                with v.Fori(0, NC - 1) as c:
                    units(c, True)
                units(NC - 1, False)
                v.wait_ge(stats, NC * (2 * TC + 1))

            @block.scalar
            def _(act):
                def high_x(c, i):
                    tile = slice(128 * (i % TC), 128 * (i % TC) + 128)
                    act.wait_ge(tr_ready, TC * c + i + 3)
                    if i > 2:
                        act.wait_ge(s_ready, 2 * (TC * c + i))
                    nc.scalar.activation(xt[0][:, :, tile], p_s[:, XB, :].rearrange("p (k n) -> p k n", k=KB),
                                         ACT.Copy, scale=XS).then_inc(hi_ready, 1)

                def high_keys(c, i):
                    tile = slice(128 * (i % TC), 128 * (i % TC) + 128)
                    act.wait_ge(kt_in[i % 2], 128 * (TC // 2 * c + i // 2) + 128)
                    if i > 2:
                        act.wait_ge(s_ready, 2 * (TC * c + i))
                    for h in range(2):
                        nc.scalar.activation(bd[0][:, h, :, tile], kt[:, i % 2, :, :], ACT.Copy,
                                             scale=held.mask_bs[:, h:h + 1]).then_inc(bd_high, 1)

                def expo(c, j):
                    exp_unit(nc, act, sub_ready, exp_ready, prob, NU * c + j, j % 2, DH ** -0.5 / (XS * AS))

                def units(c, more):
                    for j in range(NU):
                        high_pt(nc, act, (t_ready, v_ready, pt_high), pt, p_t, NU * c + j, j % 2, 6)
                        if j % 2 == 0 and (more or j // 2 + 2 < TC):
                            high_x(c, j // 2 + 2)
                        if more or j + 1 < NU:
                            expo(c, j + 1)
                        if j % 2 == 1 and (more or (j + 1) // 2 + 2 < TC):
                            high_keys(c, (j + 1) // 2 + 2)
                for i in range(2):
                    high_x(0, i)
                    high_keys(0, i)
                expo(0, 0)
                high_keys(0, 2)
                with act.Fori(0, NC - 1) as c:
                    units(c, True)
                units(NC - 1, False)

            @block.tensor
            def _(pe):
                pe.sem_inc(tr_ready, 2)
                pe.sem_inc(t_ready, 4)
                pe.sem_inc(v_ready, 8)
                pe.sem_inc(s_ready, 6)

                def turn(c, i):
                    pe.wait_ge(xn_ready, TC * c + i + 1)
                    transpose_tile(nc, held, p_s[:, XB, :], xn[:, i % 2, :]).then_inc(tr_ready, 1)

                def scores(c, j, more=True):
                    u, slot, i = NU * c + j, j % 2, j // 2
                    pe.wait_ge(sub_ready, u + 1)
                    pe.wait_ge(xt_ready, TC * c + (j + 1) // 2 + (1 if more or j + 1 < NU else 0))
                    pe.wait_ge(bd_ready, 2 * (TC * c + i) + 5)
                    for r in (2 * slot, 2 * slot + 1):
                        nc.tensor.matmul(p_s[:, r, :], held.onehot[:],
                                         held.mk01[:].rearrange("p (a k) -> p a k", a=1).broadcast_to([128, 8, S]),
                                         start=True, stop=False)
                        nc.tensor.matmul(p_s[:, r, :], held.onehot[0:64, :],
                                         held.mk2[:].rearrange("p (a k) -> p a k", a=1).broadcast_to([64, 8, S]),
                                         start=False, stop=False)
                        pair = slice(32 * r, 32 * r + 32)
                        for k in range(KB):
                            for s in range(2):
                                seq = slice(128 * (i % TC) + 64 * s, 128 * (i % TC) + 64 * s + 64)
                                last = mm3(nc, p_s[64 * s:64 * s + 64, r, 128 * k:128 * k + 128],
                                           [x[pair, k, seq] for x in xt], [x[pair, :, k, seq] for x in bd],
                                           False, k == KB - 1)
                    last.then_inc(s_ready, 1)

                def attend(c, j):
                    u, slot, i = NU * c + j, j % 2, j // 2
                    pe.wait_ge(pt_ready, 2 * u + 4)
                    pe.wait_ge(z_ready, u + 1)
                    if slot == 0:
                        pe.wait_ge(vb_ready, VB * (TC * c + i) + 3 * VB)
                    for b in range(UH // 2):
                        q, k = b // KB, b % KB
                        last = mm3(nc, p_v[:, q, VC * k:VC * k + VC],
                                   [w[:, slot, q, 128 * k:128 * k + 128] for w in pt],
                                   [w[:, 2 * i:2 * i + 2, 2 * k + slot, :, :].rearrange("p s h n -> p s (h n)")
                                    for w in vb], True, True)
                    last.then_inc(v_ready, 1)

                def turn_p(c, j):
                    transpose_unit(nc, pe, held, (exp_ready, pt_ready, t_ready), p_t, prob, NU * c + j, j % 2)

                def units(c, more):
                    for j in range(NU):
                        if more or j + 1 < NU:
                            turn_p(c, j + 1)
                        if more or j + 3 < NU:
                            scores(c, j + 3, more)
                        if j % 2 == 1 and (more or (j + 1) // 2 + 2 < TC):
                            pe.wait_ge(sub_ready, NU * c + j + 5)
                            turn(c, (j + 1) // 2 + 2)
                        attend(c, j)
                turn(0, 0)
                pe.wait_ge(xt_ready, 1)
                turn(0, 1)
                for j in range(2):
                    scores(0, j)
                turn_p(0, 0)
                scores(0, 2)
                pe.wait_ge(sub_ready, 4)
                turn(0, 2)
                with pe.Fori(0, NC - 1) as c:
                    units(c, True)
                units(NC - 1, False)


def stage_c(nc, held, a):
    with ExitStack() as es:
        def sb(name, shape, dt=F32):
            return es.enter_context(nc.sbuf_tensor(name, shape, dt))

        def sem(name):
            return held.sems.enter_context(nc.semaphore("c_" + name))

        def pb(name, shape):
            return es.enter_context(nc.psum_tensor(name, shape, F32))

        xn = sb("c_xn", [128, 2, D])
        xt = [sb("c_xt_high", [128, 2, KB, 128], F16), sb("c_xt_low", [128, 2, KB, 128], F16)]
        logit = sb("c_logit", [128, EX4])
        top = sb("c_top", [128, 2])
        pick = sb("c_pick", [128, EX4])
        zp = sb("c_zp", [128, 2, EX4, R8])
        zt = sb("c_zt", [EX4 * R8, 2, 128])
        p_t = pb("c_p_t", [128, 2, D])
        p_out = pb("c_p_out", [128, 2, D])
        p_aux = pb("c_p_aux", [128, 2, D])
        p_zt = pb("c_p_zt", [128, D])
        xn_ready, t_ready, hi_ready, xt_ready, aux_ready, gated, zp_ready, zt_ready, zt_sb, \
            out_ready, updated, stats = (sem(n) for n in (
                "xn_ready", "t_ready", "hi_ready", "xt_ready", "aux_ready", "gated", "zp_ready",
                "zt_ready", "zt_sb", "out_ready", "updated", "stats"))
        whl = [w[:, 0:KB * D].rearrange("p (k n) -> p k n", k=KB) for w in (held.wc_hi, held.wc_lo)]
        ghl = [w[:, KB * D:CW].rearrange("p (k n) -> p k n", k=KB) for w in (held.wc_hi, held.wc_lo)]

        rs_at = held.rs_steps = held.rs_steps + 2

        with nc.Block() as block:
            @block.gpsimd
            def _(pool):
                rstd_all(nc, pool, held, rs_at)

            @block.vector
            def _(v):
                v.wait_ge(held.rs_ready, rs_at)
                v.sem_inc(xt_ready, 2)
                v.sem_inc(updated, 2)
                v.sem_inc(zp_ready, 2)

                def norm(c, i):
                    v.wait_ge(t_ready, TC * c + i + 1)
                    norm_tile(nc, held, xn[:, i % 2, :], TC * c + i).then_inc(xn_ready, 1)

                def low(c, i):
                    v.wait_ge(hi_ready, TC * c + i + 1)
                    nc.vector.scalar_tensor_tensor(
                        xt[1][:, i % 2, :, :].rearrange("p k n -> p (k n)"), p_t[:, i % 2, :], XS,
                        xt[0][:, i % 2, :, :].rearrange("p k n -> p (k n)"),
                        ALU.mult, ALU.subtract).then_inc(xt_ready, 1)

                def gate(c, i):
                    k = 7 * (TC * c + i)
                    v.wait_ge(aux_ready, TC * c + i + 1)
                    nc.vector.scalar_tensor_tensor(logit[:], p_aux[:, i % 2, 0:EX4], 1.0 / (XS * WS),
                                                   held.ebias[:], ALU.mult, ALU.add).then_inc(gated, 1)
                    v.wait_ge(gated, k + 1)
                    nc.vector.tensor_reduce(top[:, 0:1], logit[:], AX.X, ALU.max).then_inc(gated, 1)
                    v.wait_ge(gated, k + 2)
                    nc.vector.tensor_scalar(pick[:], logit[:], top[:, 0:1], None,
                                            ALU.is_equal).then_inc(gated, 1)
                    v.wait_ge(gated, k + 3)
                    nc.vector.tensor_tensor(pick[:], pick[:], held.rank[:], ALU.mult).then_inc(gated, 1)
                    v.wait_ge(gated, k + 4)
                    nc.vector.tensor_reduce(top[:, 1:2], pick[:], AX.X, ALU.max).then_inc(gated, 1)
                    v.wait_ge(gated, k + 5)
                    nc.vector.tensor_scalar(pick[:], pick[:], top[:, 1:2], None,
                                            ALU.is_equal).then_inc(gated, 1)
                    v.wait_ge(gated, k + 6)
                    nc.vector.tensor_copy(zp[:, i % 2, :, :],
                                          p_aux[:, i % 2, EX4:CG].rearrange("p (e r) -> p e r", e=EX4)
                                          ).then_inc(gated, 1)
                    v.wait_ge(gated, k + 7)
                    nc.vector.tensor_tensor(
                        zp[:, i % 2, :, :], zp[:, i % 2, :, :],
                        pick[:].rearrange("p (e b) -> p e b", b=1).broadcast_to([128, EX4, R8]),
                        ALU.mult).then_inc(zp_ready, 1)

                def update(c, i):
                    t = TC * c + i
                    v.wait_ge(out_ready, t + 1)
                    nc.vector.scalar_tensor_tensor(held.X[:, t, :], p_out[:, i % 2, :], 1.0 / (XS * WS),
                                                   held.X[:, t, :], ALU.mult, ALU.add).then_inc(updated, 1)
                    stats_tile(v, nc, held, c, i, updated, t + 3, (held.apart, stats))
                def tiles(c, more):
                    for i in range(1, TC + 1):
                        if more or i + 1 < TC:
                            low(c, i + 1)
                        if more or i + 2 < TC:
                            norm(c, i + 2)
                        if more or i < TC:
                            gate(c, i)
                        update(c, i - 1)
                norm(0, 0)
                norm(0, 1)
                low(0, 0)
                low(0, 1)
                norm(0, 2)
                gate(0, 0)
                with v.Fori(0, NC - 1) as c:
                    tiles(c, True)
                tiles(NC - 1, False)
                v.wait_ge(stats, NC * (2 * TC + 1))

            @block.scalar
            def _(act):
                def high(c, i):
                    act.wait_ge(t_ready, TC * c + i + 3)
                    nc.scalar.activation(xt[0][:, i % 2, :, :].rearrange("p k n -> p (k n)"), p_t[:, i % 2, :],
                                         ACT.Copy, scale=XS).then_inc(hi_ready, 1)

                def zcopy(c, i):
                    act.wait_ge(zt_ready, TC * c + i + 1)
                    nc.scalar.activation(zt[:, i % 2, :], p_zt[0:EX4 * R8, 0:128], ACT.Copy).then_inc(zt_sb, 1)

                def tiles(c, more):
                    for i in range(1, TC + 1):
                        zcopy(c, i - 1)
                        if more or i + 1 < TC:
                            high(c, i + 1)
                high(0, 0)
                high(0, 1)
                with act.Fori(0, NC - 1) as c:
                    tiles(c, True)
                tiles(NC - 1, False)

            @block.tensor
            def _(pe):
                pe.sem_inc(t_ready, 2)

                def trans(c, i):
                    pe.wait_ge(xn_ready, TC * c + i + 1)
                    pe.wait_ge(xt_ready, TC * c + i + 1)
                    transpose_tile(nc, held, p_t[:, i % 2, :], xn[:, i % 2, :]).then_inc(t_ready, 1)

                def products(c, i):
                    st = [x[:, i % 2, :, :] for x in xt]
                    pe.wait_ge(xt_ready, TC * c + i + 3)
                    pe.wait_ge(zp_ready, TC * c + i + 1)
                    for k in range(KB):
                        last = mm3(nc, p_aux[:, i % 2, 0:CG], [x[:, k, :] for x in st],
                                   [w[:, k, :] for w in ghl], k == 0, k == KB - 1)
                    last.then_inc(aux_ready, 1)
                    pe.wait_ge(updated, TC * c + i + 1)
                    for k in range(KB):
                        mm3(nc, p_out[:, i % 2, :], [x[:, k, :] for x in st],
                            [w[:, k, :] for w in whl], k == 0, False)

                def turn_z(c, i):
                    pe.wait_ge(zp_ready, TC * c + i + 3)
                    nc.tensor.transpose(p_zt[0:EX4 * R8, 0:128],
                                        zp[:, i % 2, :, :].rearrange("p e r -> p (e r)"),
                                        held.ident[:]).then_inc(zt_ready, 1)

                def delta(c, i):
                    pe.wait_ge(zt_sb, TC * c + i + 1)
                    nc.tensor.matmul(p_out[:, i % 2, :], zt[:, i % 2, :], held.lora_b[:], start=False,
                                     stop=True).then_inc(out_ready, 1)

                def tiles(c, more):
                    for i in range(1, TC + 1):
                        turn_z(c, i - 1)
                        if more or i + 1 < TC:
                            trans(c, i + 1)
                        if more or i < TC:
                            products(c, i)
                        delta(c, i - 1)
                trans(0, 0)
                trans(0, 1)
                products(0, 0)
                with pe.Fori(0, NC - 1) as c:
                    tiles(c, True)
                tiles(NC - 1, False)


def stage_d(nc, held, a):
    with ExitStack() as es:
        def sb(name, shape, dt=F32):
            return es.enter_context(nc.sbuf_tensor(name, shape, dt))

        def sem(name):
            return held.sems.enter_context(nc.semaphore("d_" + name))

        NH = 3
        NF = len(FB)
        xn = sb("d_xn", [128, 2, D])
        xt = [sb("d_xt_high", [128, KB, CH], F16), sb("d_xt_low", [128, KB, CH], F16)]
        hid = [sb("d_h_high", [128, NH, CH], F16), sb("d_h_low", [128, NH, CH], F16)]
        term = sb("d_term", [128, 2, CH])
        kept = sb("d_kept", [128, CH])
        delta = sb("d_delta", [128, CH])
        keep = sb("d_keep", [128, CH])
        sg = sb("d_sg", [128, 2, CH])
        hf = sb("d_hf", [128, 2, CH])
        p_up = es.enter_context(nc.psum_tensor("d_p_up", [128, 4, D], F32))
        p_y = es.enter_context(nc.psum_tensor("d_p_y", [128, TC, D], F32))
        xn_ready, t_ready, hi_ready, xt_ready, up_ready, terms_in, sg_ready, keep_ready, val_ready, \
            hh_ready, h_ready, down_done, y_ready, y_read, stats = (sem(n) for n in (
                "xn_ready", "t_ready", "hi_ready", "xt_ready", "up_ready", "terms_in", "sg_ready",
                "keep_ready", "val_ready", "hh_ready", "h_ready", "down_done", "y_ready", "y_read", "stats"))
        NU = 1 + NF
        NV = DND - 1
        up_w = [w[:, 0:KB * UPD].rearrange("p (k n) -> p k n", k=KB) for w in (held.wd_hi, held.wd_lo)]
        dn_w = [w[:, KB * UPD:DW].rearrange("p (b n) -> p b n", b=DND) for w in (held.wd_hi, held.wd_lo)]
        rows = [128] * (G6 + 1) + [n for _, n in FB]

        late = Weights(nc, held, es, "wf", a["w_f"], held.wf_hi, held.wf_lo, NP_F, PF)

        rs_at = held.rs_steps = held.rs_steps + 2

        with nc.Block() as block:
            @block.sync
            def _(sp):
                late.fetch(sp)

            @block.gpsimd
            def _(pool):
                rstd_all(nc, pool, held, rs_at)
                late.divide(pool)

            @block.vector
            def _(v):
                v.wait_ge(held.rs_ready, rs_at)
                v.sem_inc(val_ready, 1)
                v.sem_inc(y_read, 1)

                def prepare(c):
                    for i in range(TC):
                        v.wait_ge(t_ready, TC * c + i + 1)
                        norm_tile(nc, held, xn[:, i % 2, :], TC * c + i).then_inc(xn_ready, 1)
                        if i:
                            low(v, nc, c, i - 1, hi_ready, xt_ready, xt, p_up)
                    low(v, nc, c, TC - 1, hi_ready, xt_ready, xt, p_up)

                def values(c):
                    v.wait_ge(terms_in, 2 * c + 2)
                    nc.vector.tensor_scalar(keep[:], delta[:], 2.5, None, ALU.is_le).then_inc(keep_ready, 1)
                    v.wait_ge(keep_ready, 3 * c + 1)
                    nc.vector.scalar_tensor_tensor(keep[:], delta[:], -2.5, keep[:], ALU.is_ge,
                                                   ALU.mult).then_inc(keep_ready, 1)
                    for d in range(DND):
                        n = rows[d]
                        if d == 0:
                            value = term[:, 0, :]
                        elif d <= G6:
                            before = term[:, (d - 1) % 2, :]
                            if d > 1:
                                v.wait_ge(val_ready, NV * c + d)
                            if d == 5:
                                v.wait_ge(keep_ready, 3 * c + 2)
                                nc.vector.tensor_tensor(kept[:], before, keep[:], ALU.mult).then_inc(keep_ready, 1)
                                v.wait_ge(keep_ready, 3 * c + 3)
                                before = kept[:]
                            value = term[:, d % 2, :]
                            nc.vector.scalar_tensor_tensor(value, before, held.growth[:, d - 1:d], delta[:],
                                                           ALU.mult, ALU.mult).then_inc(val_ready, 1)
                        else:
                            j = d - G6
                            value = hf[0:n, d % 2, :]
                            v.wait_ge(sg_ready, NF * c + j)
                            nc.vector.scalar_tensor_tensor(value, p_up[0:n, 2 * (j % 2) + 1, :], HS / (XS * WS),
                                                           sg[0:n, d % 2, :], ALU.mult, ALU.mult).then_inc(val_ready, 1)
                        v.wait_ge(hh_ready, DND * c + d + 1)
                        nc.vector.tensor_tensor(hid[1][0:n, d % NH, :], value, hid[0][0:n, d % NH, :],
                                                ALU.subtract).then_inc(h_ready, 1)

                def update(c):
                    for i in range(TC):
                        update_tile(v, nc, held, c, i, y_ready, p_y[:, i, :], HS * WS, y_read, (held.apart, stats))
                prepare(0)
                with v.Fori(0, NC - 1) as c:
                    values(c)
                    prepare(c + 1)
                    update(c)
                values(NC - 1)
                update(NC - 1)
                v.wait_ge(stats, NC * (2 * TC + 1))

            @block.scalar
            def _(act):
                def prepare(c):
                    for i in range(TC):
                        high(act, nc, c, i, t_ready, hi_ready, xt, p_up)

                def values(c):
                    act.wait_ge(up_ready, NU * c + 1)
                    nc.scalar.activation(term[:, 0, :], p_up[:, 0, :], ACT.Copy,
                                         scale=HS / (XS * WS)).then_inc(terms_in, 1)
                    nc.scalar.activation(delta[:], p_up[:, 1, :], ACT.Identity, bias=held.nlp[:, 0:1],
                                         scale=1.0 / (XS * WS)).then_inc(terms_in, 1)
                    for d in range(DND):
                        n = rows[d]
                        j = d - G6
                        if j == 0:
                            silu(act, nc, c, 1, FB[0][1], up_ready, sg_ready, sg, p_up, val_ready)
                        if j >= 1 and j < NF:
                            silu(act, nc, c, j + 1, FB[j][1], up_ready, sg_ready, sg, p_up, val_ready)
                        if d == 0:
                            act.wait_ge(terms_in, 2 * c + 1)
                            value = term[:, 0, :]
                        else:
                            act.wait_ge(val_ready, NV * c + d + 1)
                            value = term[:, d % 2, :] if d <= G6 else hf[0:n, d % 2, :]
                        act.wait_ge(down_done, DND * c + (NH if d < NH else d + 1))
                        nc.scalar.activation(hid[0][0:n, d % NH, :], value, ACT.Copy).then_inc(hh_ready, 1)
                prepare(0)
                with act.Fori(0, NC - 1) as c:
                    values(c)
                    prepare(c + 1)
                values(NC - 1)

            @block.tensor
            def _(pe):
                pe.sem_inc(t_ready, 2)
                pe.sem_inc(down_done, NH)

                def turn(c):
                    pe.wait_ge(val_ready, NV * c + 1)
                    for i in range(TC):
                        pe.wait_ge(xn_ready, TC * c + i + 1)
                        transpose_tile(nc, held, p_up[:, i, :], xn[:, i % 2, :]).then_inc(t_ready, 1)

                def up(c, j):
                    slot = 2 * (j % 2)
                    if j == 2:
                        pe.wait_ge(terms_in, 2 * c + 2)
                    if j > 2:
                        pe.wait_ge(val_ready, NV * c + G6 + j - 1)
                    at, n = (0, SD) if j == 0 else (2 * SD + FB[j - 1][0], FB[j - 1][1])
                    step = SD if j == 0 else FD
                    for half in range(2):
                        cols = slice(at + half * step, at + half * step + n)
                        for k in range(KB):
                            last = mm3(nc, p_up[0:n, slot + half, :], [w[:, k, cols] for w in up_w],
                                       [x[:, k, :] for x in xt], k == 0, k == KB - 1)
                    last.then_inc(up_ready, 1)

                def down(c, d):
                    n = rows[d]
                    pe.wait_ge(h_ready, DND * c + d + 1)
                    if d == 0:
                        pe.wait_ge(y_read, TC * c + 1)
                    for i in range(TC):
                        last = mm3(nc, p_y[:, i, :], [h[0:n, d % NH, 128 * i:128 * i + 128] for h in hid],
                                   [w[0:n, d, :] for w in dn_w], d == 0, d == DND - 1)
                        if d == DND - 1:
                            last.then_inc(y_ready, 1)
                    if d < DND - 1:
                        last.then_inc(down_done, 1)

                def products(c, more):
                    pe.wait_ge(xt_ready, TC * c + TC)
                    for j in range(3):
                        up(c, j)
                    for d in range(G6 + 1):
                        down(c, d)
                    for j in range(3, NU):
                        up(c, j)
                        down(c, G6 + j - 2)
                    down(c, DND - 2)
                    if more:
                        turn(c + 1)
                    down(c, DND - 1)
                    pe.wait_ge(y_ready, TC * c + TC)
                    pe.sem_inc(down_done, 1)
                turn(0)
                with pe.Fori(0, NC - 1) as c:
                    products(c, True)
                products(NC - 1, False)


def stage_e(nc, held, a):
    M = 128
    with ExitStack() as es:
        def sb(name, shape, dt=F32):
            return es.enter_context(nc.sbuf_tensor("e_" + name, shape, dt))

        def sem(name):
            return held.sems.enter_context(nc.semaphore("e_" + name))

        def pb(name, shape):
            return es.enter_context(nc.psum_tensor("e_" + name, shape, F32))

        NJ = 2 * KB
        wq = sb("wq", [S, S])
        wk = sb("wk", [S, S])
        wv = sb("wv", [128, 128])
        wskip = sb("wskip", [128, 128])
        wkq = sb("wkq", [128, 128])
        ctx = sb("ctx", [128, TC, M])
        xn = sb("xn", [128, TC, D])
        keys = sb("keys", [128, 2, 2, M])
        vt = sb("vt", [M, TC, 2, S])
        prob = sb("prob", [128, 2, NJ, M])
        top = sb("top", [128, 2, NJ])
        den = sb("den", [128, 2, NJ])
        pt = sb("pt", [M, 2, 2, D])
        p_s = pb("p_s", [128, 2, 2 * D])
        p_t = pb("p_t", [128, 2, D])
        p_o = pb("p_o", [128, D])
        p_m = pb("p_m", [128, D])
        w_in, clear, wkq_ready, wkq_in, xn_ready, m_ready, keys_ready, s_ready, \
            top_ready, sub_ready, exp_ready, den_ready, prob_ready, t_ready, pt0_ready, pt1_ready, o_ready, \
            o_read, stats = (sem(n) for n in (
                "w_in", "clear", "wkq_ready", "wkq_in", "xn_ready", "m_ready",
                "keys_ready", "s_ready", "top_ready", "sub_ready", "exp_ready", "den_ready", "prob_ready",
                "t_ready", "pt0_ready", "pt1_ready", "o_ready", "o_read", "stats"))
        ctx_in = [sem(f"ctx_in_{b}") for b in range(2)]
        ctx_d = a["ctx"].rearrange("(t p) n -> p t n", p=128)

        rs_at = held.rs_steps = held.rs_steps + 2

        with nc.Block() as block:
            @block.sync
            def _(sp):
                sp.dma_start(wq[:], a["Wq"]).then_inc(w_in, 16)
                sp.dma_start(wk[:], a["Wk"]).then_inc(w_in, 16)
                sp.wait_ge(clear, 2)
                for s in range(2):
                    half = slice(64 * s, 64 * s + 64)
                    sp.dma_start(wskip[half, half], a["WskipT"]).then_inc(w_in, 16)
                    sp.dma_start(wv[half, half], a["WvT"]).then_inc(w_in, 16)
                with sp.Fori(0, NC) as c:
                    for i in range(TC):
                        sp.wait_ge(keys_ready, TC * c + i + 3)
                        sp.dma_start(ctx[:, i, :], ctx_d[:, TC * c + i, :]).then_inc(ctx_in[i % 2], 16)

            @block.gpsimd
            def _(pool):
                nc.gpsimd.memset(wskip[:], 0.0).then_inc(clear, 1)
                nc.gpsimd.memset(wv[:], 0.0).then_inc(clear, 1)
                rstd_all(nc, pool, held, rs_at)
                with pool.Fori(0, NC) as c:
                    for i in range(TC):
                        b, t = i % 2, TC * c + i
                        pool.wait_ge(den_ready, 2 * t + 2)
                        nc.gpsimd.tensor_tensor(
                            prob[:, b, :, :], prob[:, b, :, :],
                            den[:, b, :].rearrange("p (j a) -> p j a", a=1).broadcast_to([128, NJ, M]),
                            ALU.mult).then_inc(prob_ready, 1)

            @block.vector
            def _(v):
                nc.vector.memset(wkq[:], 0.0).then_inc(wkq_in, 1)
                nc.vector.memset(keys[:], 0.0).then_inc(wkq_in, 1)
                v.wait_ge(wkq_in, 2)
                v.wait_ge(wkq_ready, 1)
                for s in range(2):
                    half = slice(64 * s, 64 * s + 64)
                    nc.vector.tensor_copy(wkq[half, half], p_m[half, half]).then_inc(wkq_in, 1)
                v.wait_ge(held.rs_ready, rs_at)
                v.sem_inc(sub_ready, 2)
                v.sem_inc(pt1_ready, 1)
                v.sem_inc(o_read, 1)

                def norm(c, i):
                    t = TC * c + i
                    v.wait_ge(o_ready, t + 1)
                    norm_tile(nc, held, xn[:, i % TC, :], t).then_inc(xn_ready, 1)

                def soft(c, i):
                    b, t = i % 2, TC * c + i
                    scores = p_s[:, b, :].rearrange("p (j m) -> p j m", j=NJ)
                    v.wait_ge(s_ready, t + 3)
                    nc.vector.tensor_reduce(top[:, b, :], scores, AX.X, ALU.max).then_inc(top_ready, 1)
                    v.wait_ge(top_ready, t + 1)
                    v.wait_ge(t_ready, t + 1)
                    nc.vector.tensor_tensor(
                        prob[:, b, :, :], scores,
                        top[:, b, :].rearrange("p (j a) -> p j a", a=1).broadcast_to([128, NJ, M]),
                        ALU.subtract).then_inc(sub_ready, 1)

                def total(c, i):
                    b, t = i % 2, TC * c + i
                    v.wait_ge(exp_ready, t + 1)
                    nc.vector.tensor_reduce(den[:, b, :], prob[:, b, :, :], AX.X, ALU.add).then_inc(den_ready, 1)
                    v.wait_ge(den_ready, 2 * t + 1)
                    nc.vector.reciprocal(den[:, b, :], den[:, b, :]).then_inc(den_ready, 1)

                def values(c, i):
                    t = TC * c + i
                    v.wait_ge(t_ready, t + 3)
                    v.wait_ge(o_ready, t + 3)
                    nc.vector.tensor_copy(pt[:, i % 2, 1, :], p_t[:, 1, :]).then_inc(pt1_ready, 1)

                def update(c, i):
                    t = TC * c + i
                    v.wait_ge(o_ready, t + 5)
                    nc.vector.tensor_tensor(held.X[:, t, :], p_o[:], held.X[:, t, :], ALU.add).then_inc(o_read, 1)
                    stats_tile(v, nc, held, c, i, o_read, t + 2, (held.apart, stats))
                def tiles(c, more):
                    for i in range(1, TC + 1):
                        values(c, i - 1)
                        if more or i + 1 < TC:
                            soft(c, i + 1)
                        if more or i + 2 < TC:
                            norm(c, i + 2)
                        update(c, i - 1)
                        if more or i + 1 < TC:
                            total(c, i + 1)
                norm(0, 0)
                for i in range(2):
                    soft(0, i)
                    norm(0, i + 1)
                    total(0, i)
                with v.Fori(0, NC - 1) as c:
                    tiles(c, True)
                tiles(NC - 1, False)
                v.wait_ge(stats, NC * (2 * TC + 1))

            @block.scalar
            def _(act):
                act.wait_ge(wkq_in, 4)
                act.sem_inc(keys_ready, 4)
                act.sem_inc(pt0_ready, 1)

                def keys_in(c, i):
                    b, t = i % 2, TC * c + i
                    act.wait_ge(m_ready, t + 1)
                    act.wait_ge(o_ready, t + 1)
                    act.wait_ge(s_ready, t + 1)
                    for s in range(2):
                        half = slice(64 * s, 64 * s + 64)
                        nc.scalar.activation(keys[half, b, s, :], p_m[half, 0:M], ACT.Copy)
                    nc.scalar.activation(vt[:, i % TC, :, :], p_m[:, M:2 * M].rearrange("p (s n) -> p s n", s=2),
                                         ACT.Copy).then_inc(keys_ready, 1)

                def expo(c, i):
                    b, t = i % 2, TC * c + i
                    act.wait_ge(sub_ready, t + 3)
                    nc.scalar.activation(prob[:, b, :, :], prob[:, b, :, :], ACT.Exp,
                                         scale=S ** -0.5).then_inc(exp_ready, 1)

                def values(c, i):
                    t = TC * c + i
                    act.wait_ge(t_ready, t + 3)
                    act.wait_ge(o_ready, t + 3)
                    nc.scalar.activation(pt[:, i % 2, 0, :], p_t[:, 0, :], ACT.Copy).then_inc(pt0_ready, 1)

                def tiles(c, more):
                    for i in range(1, TC + 1):
                        values(c, i - 1)
                        if more or i + 2 < TC:
                            keys_in(c, i + 2)
                        if more or i + 1 < TC:
                            expo(c, i + 1)
                keys_in(0, 0)
                for i in range(2):
                    keys_in(0, i + 1)
                    expo(0, i)
                with act.Fori(0, NC - 1) as c:
                    tiles(c, True)
                tiles(NC - 1, False)

            @block.tensor
            def _(pe):
                pe.wait_ge(w_in, 96)
                for s in range(2):
                    half = slice(64 * s, 64 * s + 64)
                    last = nc.tensor.matmul(p_m[half, half], wk[:], wq[:], start=True, stop=True)
                last.then_inc(wkq_ready, 1)
                pe.wait_ge(wkq_in, 4)
                pe.sem_inc(o_ready, 4)
                pe.sem_inc(s_ready, 2)
                pe.sem_inc(t_ready, 2)
                pe.wait_ge(keys_ready, 4)

                def make_keys(c, i):
                    t = TC * c + i
                    pe.wait_ge(ctx_in[i % 2], 16 * (TC // 2 * c + i // 2) + 16)
                    pe.wait_ge(keys_ready, t + 4)
                    nc.tensor.matmul(p_m[:, 0:M], wkq[:], ctx[:, i % TC, :], start=True, stop=True)
                    nc.tensor.matmul(p_m[:, M:2 * M], ctx[:, i % TC, :], wv[:], start=True,
                                     stop=True).then_inc(m_ready, 1)

                def scores(c, i):
                    b, t = i % 2, TC * c + i
                    pe.wait_ge(xn_ready, t + 1)
                    pe.wait_ge(keys_ready, t + 5)
                    pe.wait_ge(sub_ready, t + 1)
                    for k in range(KB):
                        last = nc.tensor.matmul(p_s[:, b, 256 * k:256 * k + 256], xn[:, i % TC, 128 * k:128 * k + 128],
                                                keys[:, b, :, :].rearrange("p s m -> p (s m)"),
                                                start=True, stop=True)
                    last.then_inc(s_ready, 1)

                def transposes(c, i):
                    b, t = i % 2, TC * c + i
                    pe.wait_ge(prob_ready, t + 1)
                    pe.wait_ge(pt1_ready, t + 1)
                    pe.wait_ge(pt0_ready, t + 1)
                    for s in range(2):
                        for k in range(KB):
                            last = nc.tensor.transpose(p_t[:, s, 128 * k:128 * k + 128], prob[:, b, 2 * k + s, :],
                                                       held.ident[:])
                    last.then_inc(t_ready, 1)

                def output(c, i):
                    b, t = i % 2, TC * c + i
                    pe.wait_ge(o_read, t + 1)
                    nc.tensor.matmul(p_o[:], wskip[:], xn[:, i % TC, :], start=True, stop=False)
                    pe.wait_ge(pt0_ready, t + 2)
                    pe.wait_ge(pt1_ready, t + 2)
                    for s in range(2):
                        half = slice(64 * s, 64 * s + 64)
                        last = nc.tensor.matmul(p_o[half, :], vt[:, i % TC, s, :], pt[:, b, s, :], start=False,
                                                stop=True)
                    last.then_inc(o_ready, 1)

                def tiles(c, more):
                    for i in range(1, TC + 1):
                        if more or i + 2 < TC:
                            make_keys(c, i + 2)
                        output(c, i - 1)
                        if more or i < TC:
                            transposes(c, i)
                        if more or i + 2 < TC:
                            scores(c, i + 2)
                make_keys(0, 0)
                scores(0, 0)
                make_keys(0, 1)
                scores(0, 1)
                make_keys(0, 2)
                transposes(0, 0)
                scores(0, 2)
                with pe.Fori(0, NC - 1) as c:
                    tiles(c, True)
                tiles(NC - 1, False)


def stage_f(nc, held, a, out):
    with ExitStack() as es:
        def sb(name, shape, dt=F32):
            return es.enter_context(nc.sbuf_tensor("f_" + name, shape, dt))

        def sem(name):
            return held.sems.enter_context(nc.semaphore("f_" + name))

        NH = 3
        LP = TC // 2
        xn = sb("xn", [128, 2, D])
        xt = [sb("xt_high", [128, KB, CH], F16), sb("xt_low", [128, KB, CH], F16)]
        lat = [sb("lat_high", [128, FL, CH], F16), sb("lat_low", [128, FL, CH], F16)]
        hid = [sb("h_high", [128, NH, CH], F16), sb("h_low", [128, NH, CH], F16)]
        w2 = [sb("w2_high", [128, FL, D], F16), sb("w2_low", [128, FL, D], F16)]
        relu = sb("relu", [128, 2, CH])
        sq = sb("sq", [128, 2, CH])
        routed = sb("routed", [128, TC, D])
        top8 = sb("top8", [128, TC, NE])
        route = sb("route", [128, TC])
        y = sb("y", [128, TC, D])
        fc2, expert_t = y[:, 0:FL, :], y[:, FL, :].rearrange("p (k n) -> p k n", k=FL)
        yst = sb("yst", [128, TC, 6])
        ymv = sb("ymv", [128, TC, 2])
        yve = sb("yve", [128, TC])
        yrs = sb("yrs", [128, TC])
        p_up = es.enter_context(nc.psum_tensor("f_p_up", [128, 4, D], F32))
        p_y = es.enter_context(nc.psum_tensor("f_p_y", [128, TC, D], F32))
        w2_in, w2_ready, w2_split, xn_ready, t_ready, hi_ready, xt_ready, logit_ready, route_ready, \
            lat_ready, lat_hi, lat_lo, r_ready, r_read, up_ready, relu_ready, sq_ready, hh_ready, h_ready, \
            down_done, y_ready, y_read, y_steps, yrs_ready, normed, scaled, final, scaled_v, final_v = (sem(n) for n in (
                "w2_in", "w2_ready", "w2_split", "xn_ready", "t_ready", "hi_ready", "xt_ready",
                "logit_ready", "route_ready", "lat_ready", "lat_hi", "lat_lo", "r_ready", "r_read", "up_ready",
                "relu_ready", "sq_ready", "hh_ready", "h_ready", "down_done", "y_ready", "y_read", "y_steps",
                "yrs_ready", "normed", "scaled", "final", "scaled_v", "final_v"))
        stored = [sem(f"stored_{b}") for b in range(2)]
        up_w = [w[:, 0:KB * FC].rearrange("p (k n) -> p k n", k=KB) for w in (held.wf_hi, held.wf_lo)]
        dn_w = [w[:, KB * FC:FW].rearrange("p (b n) -> p b n", b=FU) for w in (held.wf_hi, held.wf_lo)]
        out_t = out.rearrange("(t p) n -> p t n", p=128)

        rs_at = held.rs_steps = held.rs_steps + 2

        with nc.Block() as block:
            @block.sync
            def _(sp):
                sp.dma_start(expert_t, a["expertT"].rearrange("(k p) n -> p k n", p=128)).then_inc(w2_in, 16)
                sp.dma_start(fc2, a["fc2"].rearrange("(k p) n -> p k n", p=128)).then_inc(w2_in, 16)

                def store(c, i, ready, at):
                    sp.wait_ge(ready, at)
                    sp.dma_start(out_t[:, TC * c + i, :], y[:, i, :]).then_inc(stored[i % 2], 16)
                with sp.Fori(0, NC - 1) as c:
                    for i in range(TC):
                        store(c, i, final, TC * c + i + 1)
                for i in range(LP, TC):
                    store(NC - 1, i, final_v, i - LP + 1)
                for i in range(LP):
                    store(NC - 1, i, final, TC * (NC - 1) + i + 1)
                for b in range(2):
                    sp.wait_ge(stored[b], 16 * (NT // 2) + 16)

            @block.gpsimd
            def _(pool):
                rstd_all(nc, pool, held, rs_at)
                for b in range(2):
                    pool.sem_inc(stored[b], 16)

                def finish(c, tiles):
                    wait_apart(pool, y_steps, 2 * TC * c + 2 * TC, held.apart)
                    nc.gpsimd.tensor_scalar(yve[:], ymv[:, :, 1], EPS, None, ALU.add).then_inc(yrs_ready, 1)
                    wait_apart(pool, yrs_ready, 2 * c + 1, held.apart)
                    nc.gpsimd.tensor_tensor(yrs[:], yve[:], held.mhalf[:, 0:TC], ALU.pow).then_inc(yrs_ready, 1)
                    for i in range(tiles):
                        t = TC * c + i
                        wait_apart(pool, normed, t + 1, held.apart)
                        nc.gpsimd.tensor_tensor(y[:, i, :], y[:, i, :], held.gam[:], ALU.mult).then_inc(scaled, 1)
                        wait_apart(pool, scaled, 2 * t + 1, held.apart)
                        nc.gpsimd.tensor_tensor(y[:, i, :], y[:, i, :], held.bet[:], ALU.add).then_inc(scaled, 1)
                        wait_apart(pool, scaled, 2 * t + 2, held.apart)
                        nc.gpsimd.tensor_tensor(y[:, i, :], y[:, i, :], held.X[:, t, :], ALU.add).then_inc(final, 1)
                with pool.Fori(0, NC - 1) as c:
                    finish(c, TC)
                finish(NC - 1, LP)

            @block.vector
            def _(v):
                for k in range(FL):
                    v.wait_ge(w2_ready, k + 1)
                    nc.vector.tensor_scalar(w2[0][:, k, :], p_y[:, k, :], WS, None, ALU.mult).then_inc(w2_split, 1)
                    v.wait_ge(w2_split, 2 * k + 1)
                    nc.vector.scalar_tensor_tensor(w2[1][:, k, :], p_y[:, k, :], WS, w2[0][:, k, :],
                                                   ALU.mult, ALU.subtract).then_inc(w2_split, 1)
                v.wait_ge(held.rs_ready, rs_at)
                v.sem_inc(sq_ready, 1)
                v.sem_inc(y_read, 1)

                def prepare(c):
                    for i in range(TC):
                        v.wait_ge(t_ready, TC * c + i + 1)
                        norm_tile(nc, held, xn[:, i % 2, :], TC * c + i).then_inc(xn_ready, 1)
                        if i:
                            low(v, nc, c, i - 1, hi_ready, xt_ready, xt, p_up)
                    low(v, nc, c, TC - 1, hi_ready, xt_ready, xt, p_up)

                def front(c):
                    wait_apart(v, logit_ready, c + 1, held.apart)
                    for i in range(TC):
                        nc.vector.max(top8[:, i, :], p_up[:, 0, NE * i:NE * i + NE]).then_inc(route_ready, 1)
                    v.wait_ge(route_ready, (TC + 2) * c + TC)
                    nc.vector.tensor_tensor(route[:], top8[:, :, 0], top8[:, :, 1], ALU.add).then_inc(route_ready, 1)
                    v.wait_ge(route_ready, (TC + 2) * c + TC + 1)
                    nc.vector.tensor_scalar(route[:], route[:], 1.0 / (XS * WS * AS * WS), None,
                                            ALU.mult).then_inc(route_ready, 1)
                    for l in range(FL):
                        v.wait_ge(lat_hi, FL * c + l + 1)
                        nc.vector.scalar_tensor_tensor(lat[1][:, l, :], p_up[:, 1 + l, :], AS / (XS * WS),
                                                       lat[0][:, l, :], ALU.mult, ALU.subtract).then_inc(lat_lo, 1)

                def blocks(c):
                    for f in range(FU):
                        v.wait_ge(relu_ready, FU * c + f + 1)
                        nc.vector.tensor_tensor(sq[:, f % 2, :], relu[:, f % 2, :], relu[:, f % 2, :],
                                                ALU.mult).then_inc(sq_ready, 1)
                        v.wait_ge(hh_ready, FU * c + f + 1)
                        nc.vector.tensor_tensor(hid[1][:, f % NH, :], sq[:, f % 2, :], hid[0][:, f % NH, :],
                                                ALU.subtract).then_inc(h_ready, 1)

                def add_routed(c):
                    for i in range(TC):
                        t = TC * c + i
                        v.wait_ge(y_ready, t + 1)
                        v.wait_ge(r_read, t + 1)
                        v.wait_ge(stored[i % 2], 16 * (TC // 2) * c + 16)
                        nc.vector.scalar_tensor_tensor(y[:, i, :], p_y[:, i, :], 1.0 / (FS * WS), routed[:, i, :],
                                                       ALU.mult, ALU.add).then_inc(y_read, 1)

                def norm_out(c):
                    for i in range(TC):
                        wait_apart(v, y_read, TC * c + i + 2, held.apart)
                        nc.vector.bn_stats(yst[:, i, :], y[:, i, :]).then_inc(y_steps, 1)
                    for i in range(TC):
                        wait_apart(v, y_steps, 2 * TC * c + TC + i, held.apart)
                        nc.vector.bn_aggr(ymv[:, i, :], yst[:, i, :]).then_inc(y_steps, 1)
                    v.wait_ge(yrs_ready, 2 * c + 2)
                    for i in range(TC):
                        nc.vector.tensor_scalar(y[:, i, :], y[:, i, :], ymv[:, i, 0:1], yrs[:, i:i + 1],
                                                ALU.subtract, ALU.mult).then_inc(normed, 1)
                prepare(0)
                front(0)
                with v.Fori(0, NC - 1) as c:
                    blocks(c)
                    prepare(c + 1)
                    add_routed(c)
                    front(c + 1)
                    norm_out(c)
                blocks(NC - 1)
                add_routed(NC - 1)
                norm_out(NC - 1)
                for j, i in enumerate(range(LP, TC)):
                    v.wait_ge(normed, NT - TC + i + 1)
                    nc.vector.tensor_tensor(y[:, i, :], y[:, i, :], held.gam[:], ALU.mult).then_inc(scaled_v, 1)
                    v.wait_ge(scaled_v, 2 * j + 1)
                    nc.vector.tensor_tensor(y[:, i, :], y[:, i, :], held.bet[:], ALU.add).then_inc(scaled_v, 1)
                    v.wait_ge(scaled_v, 2 * j + 2)
                    nc.vector.tensor_tensor(y[:, i, :], y[:, i, :], held.X[:, NT - TC + i, :],
                                            ALU.add).then_inc(final_v, 1)

            @block.scalar
            def _(act):
                def front(c):
                    for i in range(TC):
                        high(act, nc, c, i, t_ready, hi_ready, xt, p_up)
                    for l in range(FL):
                        act.wait_ge(lat_ready, FL * c + l + 1)
                        nc.scalar.activation(lat[0][:, l, :], p_up[:, 1 + l, :], ACT.Copy,
                                             scale=AS / (XS * WS)).then_inc(lat_hi, 1)
                    act.wait_ge(route_ready, (TC + 2) * c + TC + 2)
                    for i in range(TC):
                        act.wait_ge(r_ready, TC * c + i + 1)
                        nc.scalar.activation(routed[:, i, :], p_y[:, i, :], ACT.Copy,
                                             scale=route[:, i:i + 1]).then_inc(r_read, 1)

                def blocks(c):
                    for f in range(FU + 1):
                        if f < FU:
                            act.wait_ge(up_ready, FU * c + f + 1)
                            act.wait_ge(sq_ready, FU * c + (f if f >= 2 else 1))
                            nc.scalar.activation(relu[:, f % 2, :], p_up[:, f % 4, :], ACT.Relu,
                                                 scale=FS ** 0.5 / (XS * WS)).then_inc(relu_ready, 1)
                        if f:
                            g = f - 1
                            act.wait_ge(sq_ready, FU * c + g + 2)
                            act.wait_ge(down_done, FU * c + (NH if g < NH else g + 1))
                            nc.scalar.activation(hid[0][:, g % NH, :], sq[:, g % 2, :], ACT.Copy).then_inc(hh_ready, 1)
                front(0)
                with act.Fori(0, NC - 1) as c:
                    blocks(c)
                    front(c + 1)
                blocks(NC - 1)

            @block.tensor
            def _(pe):
                pe.wait_ge(w2_in, 32)
                for l in range(FL):
                    for k in range(FL):
                        last = nc.tensor.matmul(p_y[:, l, :], expert_t[:, k, 128 * l:128 * l + 128], fc2[:, k, :],
                                                start=k == 0, stop=k == FL - 1)
                    last.then_inc(w2_ready, 1)
                pe.wait_ge(w2_split, 2 * FL)
                pe.sem_inc(t_ready, 2)
                pe.sem_inc(down_done, NH)

                def turn(c):
                    pe.wait_ge(sq_ready, FU * c + 1)
                    for i in range(TC):
                        pe.wait_ge(xn_ready, TC * c + i + 1)
                        transpose_tile(nc, held, p_up[:, i, :], xn[:, i % 2, :]).then_inc(t_ready, 1)

                def front(c):
                    pe.wait_ge(xt_ready, TC * c + TC)
                    for i in range(TC):
                        for k in range(KB):
                            last = mm3(nc, p_up[:, 0, NE * i:NE * i + NE],
                                       [x[:, k, 128 * i:128 * i + 128] for x in xt],
                                       [w[:, k, INT + LAT:FC] for w in up_w], k == 0, k == KB - 1)
                    last.then_inc(logit_ready, 1)
                    for l in range(FL):
                        for k in range(KB):
                            last = mm3(nc, p_up[:, 1 + l, :], [w[:, k, INT + 128 * l:INT + 128 * l + 128] for w in up_w],
                                       [x[:, k, :] for x in xt], k == 0, k == KB - 1)
                        last.then_inc(lat_ready, 1)
                    up(c, 0)
                    pe.wait_ge(lat_lo, FL * c + FL)
                    pe.wait_ge(y_read, TC * c + 1)
                    for i in range(TC):
                        for l in range(FL):
                            last = mm3(nc, p_y[:, i, :], [x[:, l, 128 * i:128 * i + 128] for x in lat],
                                       [w[:, l, :] for w in w2], l == 0, l == FL - 1)
                        last.then_inc(r_ready, 1)

                def up(c, f):
                    if f == 0:
                        pe.wait_ge(route_ready, (TC + 2) * c + TC)
                    elif f <= 2:
                        pe.wait_ge(lat_lo, FL * c + f)
                    elif f >= 4:
                        pe.wait_ge(sq_ready, FU * c + f - 2)
                    for k in range(KB):
                        last = mm3(nc, p_up[:, f % 4, :], [w[:, k, 128 * f:128 * f + 128] for w in up_w],
                                   [x[:, k, :] for x in xt], k == 0, k == KB - 1)
                    last.then_inc(up_ready, 1)

                def down(c, f):
                    pe.wait_ge(h_ready, FU * c + f + 1)
                    if f == 0:
                        pe.wait_ge(r_read, TC * c + TC)
                    for i in range(TC):
                        last = mm3(nc, p_y[:, i, :], [h[:, f % NH, 128 * i:128 * i + 128] for h in hid],
                                   [w[:, f, :] for w in dn_w], f == 0, f == FU - 1)
                        if f == FU - 1:
                            last.then_inc(y_ready, 1)
                    if f < FU - 1:
                        last.then_inc(down_done, 1)

                def blocks(c, more):
                    up(c, 1)
                    for f in range(2, FU):
                        up(c, f)
                        down(c, f - 2)
                    down(c, FU - 2)
                    if more:
                        turn(c + 1)
                    down(c, FU - 1)
                    pe.wait_ge(y_ready, TC * c + TC)
                    pe.sem_inc(down_done, 1)
                turn(0)
                front(0)
                with pe.Fori(0, NC - 1) as c:
                    blocks(c, True)
                    front(c + 1)
                blocks(NC - 1, False)


def build(nc, a, out):
    held = Held()
    with ExitStack() as es:
        def sb(name, shape, dt=F32):
            return es.enter_context(nc.sbuf_tensor(name, shape, dt))

        held.sems = es
        held.apart = es.enter_context(nc.semaphore("apart"))
        held.rs_ready = es.enter_context(nc.semaphore("rs_ready"))
        held.rs_steps = 0
        held.X = sb("X", [128, NT, D])
        held.mv = sb("mv", [128, NT, 2])
        held.st = sb("st", [128, TC, 6])
        held.mvc = sb("mvc", [128, TC, 2])
        held.ve = sb("ve", [128, NT])
        held.rstd = sb("rstd", [128, NT, 1])
        held.mhalf = sb("mhalf", [128, NT])
        held.ident = sb("ident", [128, 128])
        held.ones = sb("ones", [128, 128])
        held.onehot = sb("onehot", [128, 128], BF16)
        held.mask_a = sb("mask_a", [96, 8])
        held.mask_b = sb("mask_b", [128, 2])
        held.mask_bs = sb("mask_bs", [128, 2])
        held.mk01 = sb("mk01", [128, S], BF16)
        held.mk2 = sb("mk2", [S, S], BF16)
        held.nlp = sb("nlp", [128, 1])
        held.growth = sb("growth", [128, G6])
        held.gam = sb("gam", [128, D])
        held.bet = sb("bet", [128, D])
        held.ebias = sb("ebias", [128, EX4])
        held.rank = sb("rank", [128, EX4])
        held.lora_b = sb("lora_b", [EX4 * R8, D])
        held.wd_hi = sb("wd_hi", [128, DW], F16)
        held.wd_lo = sb("wd_lo", [128, DW], F16)
        with ExitStack() as early:
            def se(name, shape, dt=F32):
                return early.enter_context(nc.sbuf_tensor(name, shape, dt))
            held.wc_hi = se("wc_hi", [128, CW], F16)
            held.wc_lo = se("wc_lo", [128, CW], F16)
            held.kq_bias = se("kq_bias", [128, 1])
            held.wkq = se("wkq", [128, KB, 96 + QL])
            held.wqk = se("wqk", [128, 4, 96])
            held.wvo = [se("wvo_high", [128, D], F16), se("wvo_low", [128, D], F16)]
            held.bvo = [se("bvo_high", [1, D], F16), se("bvo_low", [1, D], F16)]
            held.units = se("units", [1, 128], F16)
            setup_stage(nc, held, a)
            stage_a(nc, held, a)
            stage_b(nc, held, a)
            stage_c(nc, held, a)
        held.wf_hi = sb("wf_hi", [128, FW], F16)
        held.wf_lo = sb("wf_lo", [128, FW], F16)
        stage_d(nc, held, a)
        stage_e(nc, held, a)
        stage_f(nc, held, a, out)


def on_partitions(np, w):
    k, n = w.shape[0] // 128, w.shape[1]
    return w.reshape(k, 128, n).transpose(1, 0, 2).reshape(128, k * n)


def kernel(**inputs):
    import numpy as np
    import concourse.bacc as bacc
    from concourse.bass_utils import run_bass_kernel_spmd

    i = {k: np.asarray(v) for k, v in inputs.items()}
    L = lambda w: on_partitions(np, w)
    fuse = i["L1_attn_fuse_weight"]
    ffn_down = i["L1_attn_ffn_down_w"].T
    pad = np.zeros((128 * len(FB) - FD, D), ffn_down.dtype)
    w_d_up = np.concatenate([i["L1_attn_up_w"].T, i["L1_attn_gate_w"].T, i["L1_attn_ffn_gate_w"].T,
                             i["L1_attn_ffn_up_w"].T], 1)
    w_d_dn = np.concatenate([i["L1_attn_local_approx_output"].T, fuse.transpose(2, 1, 0).reshape(G6 * SD, D),
                             ffn_down, pad], 0)
    lora_a = i["L0_ffn_lora_A"].reshape(EX4 * R8, D).T
    ctx = i["ctx_1024"]
    arrays = {
        "x": i["x"].reshape(TOK, D),
        "ctx": ctx.reshape(TOK, 128),
        "ctx_t": ctx.transpose(2, 0, 1).reshape(128, TOK),
        "mask": i["mask_SxS2_ff0"],
        "Wkvq": np.concatenate([i["L0_attn_Wkv_d"], i["L0_attn_Wq_d"]], 1),
        "bq_d": i["L0_attn_bq_d"], "bkv_rep": np.tile(i["L0_attn_bkv_d"], 24),
        "W_qk": i["L0_attn_W_qk"], "b_qk": i["L0_attn_b_qk"],
        "Wv_uT": i["L0_attn_Wv_u"].T, "bv_uT": i["L0_attn_bv_u"].reshape(4, 128).T, "Wo": i["L0_attn_Wo"], "bo": i["L0_attn_bo"],
        "w_c": np.concatenate([L(i["L0_ffn_W_up"].T), L(np.concatenate([i["L0_ffn_gate_w"].T, lora_a], 1))], 1),
        "expert_bias": i["L0_ffn_expert_bias"],
        "lora_B": i["L0_ffn_lora_B"].transpose(0, 2, 1).reshape(EX4 * R8, D),
        "w_d": np.concatenate([L(w_d_up), L(w_d_dn)], 1),
        "local_point": i["L1_attn_local_point"], "discount": i["L1_attn_discount_factor"],
        "Wk": i["L1_xattn_Wk"], "Wq": i["L1_xattn_Wq"], "WvT": i["L1_xattn_Wv"].T, "WskipT": i["L1_xattn_Wskip"].T,
        "w_f": np.concatenate([L(np.concatenate([i["L1_ffn_up_w"], i["L1_ffn_fc1_w"], i["L1_ffn_gate_w"]], 1)),
                               L(i["L1_ffn_down_w"])], 1),
        "expertT": i["L1_ffn_expert_w"].T, "fc2": i["L1_ffn_fc2_w"],
        "gamma": i["L1_ffn_ln_gamma"], "beta": i["L1_ffn_ln_beta"],
    }
    arrays = {k: np.ascontiguousarray(v) for k, v in arrays.items()}
    nc = bacc.Bacc("TRN2", target_bir_lowering=False, num_devices=1)
    a = {k: nc.dram_tensor("in_" + k, v.shape, F32, kind="ExternalInput").ap() for k, v in arrays.items()}
    out = nc.dram_tensor("out_x", (TOK, D), F32, kind="ExternalOutput").ap()
    build(nc, a, out)
    r = run_bass_kernel_spmd(nc, [{"in_" + k: v for k, v in arrays.items()}], core_ids=[0])
    return r.results[0]["out_x"].reshape(NSEQ, S, D)
```
